# Optimizing a Trainium2 kernel written in Bass

```python
import numpy as np
import jax
import jax.numpy as jnp

def _softmax(x, axis=-1):
    return jax.nn.softmax(x, axis=axis)

def _gelu(x):
    return jax.nn.gelu(x, approximate=True)

def _silu(x):
    return jax.nn.silu(x)

def _sigmoid(x):
    return jax.nn.sigmoid(x)

def _layernorm(x, axis=-1, eps=1e-05):
    m = jnp.mean(x, axis=axis, keepdims=True)
    v = jnp.var(x, axis=axis, keepdims=True)
    return (x - m) / jnp.sqrt(v + eps)

def _scatter_add(tgt, idx, src, axis=0):
    return tgt.at[idx].add(src)

def _segment_sum(src, seg, n):
    return jax.ops.segment_sum(src, seg, n)
kernel_name = 'mk_perceiver_d1_seqx_r8_239953'

def setup_inputs(seed: int=0):
    np.random.seed(seed)
    _w = jnp.asarray

    def _rec_inputs():
        import jax
        import jax.numpy as jnp
        _rk = jax.random.key(seed)
        x = -0.0003929 + 0.9999 * jax.random.normal(jax.random.fold_in(_rk, 1), (16, 64, 256), jnp.float32)
        _lenS = 64 - jax.random.randint(jax.random.fold_in(_rk, 7), (16,), 0, max(1, 64 // 4) + 1, jnp.int32)
        _lenS2 = 1601 - jax.random.randint(jax.random.fold_in(_rk, 8), (16,), 0, max(1, 1601 // 4) + 1, jnp.int32)
        _ctx_2048P = jax.random.normal(jax.random.fold_in(_rk, 11), (16, 16, 256), jnp.float32)
        _ctx_2048c = jax.random.dirichlet(jax.random.fold_in(_rk, 511), 0.3 * jnp.ones((16,), jnp.float32), (16, 1601))
        _ctx_2048t = jnp.einsum('bsk,bkd->bsd', _ctx_2048c, _ctx_2048P)
        _ctx_2048t = _ctx_2048t * jax.lax.rsqrt(jnp.mean(jnp.square(_ctx_2048t)) + 1e-12) * 0.953939
        ctx_2048 = -0.000514642 + 1.00011 * (_ctx_2048t + 0.3 * jax.random.normal(jax.random.fold_in(_rk, 611), (16, 1601, 256), jnp.float32))
        return (x, ctx_2048)
    x, ctx_2048 = _rec_inputs()

    def _L0_xattn_setup():
        import jax, jax.numpy as jnp
        import numpy as np
        NUM_HEADS = 16

        def _qdq(x):
            s = jnp.maximum(jnp.max(jnp.abs(x), axis=-1, keepdims=True) / 127.0, 1e-08)
            return jnp.clip(jnp.round(x / s), -127.0, 127.0) * s
        key = jax.random.key(seed)
        ks = jax.random.split(key, 8)
        B, N, M, D = (2, 512, 64, 256)
        w_std = 0.02
        return {'x': jax.random.normal(ks[0], (B, N, D), jnp.float32), 'cond': jax.random.normal(ks[1], (B, M, D), jnp.float32), 'wq': jax.random.normal(ks[2], (D, D), jnp.float32) * w_std, 'bq': jax.random.normal(ks[3], (D,), jnp.float32) * w_std, 'wkv': jax.random.normal(ks[4], (2 * D, D), jnp.float32) * w_std, 'bkv': jax.random.normal(ks[5], (2 * D,), jnp.float32) * w_std, 'wp': jax.random.normal(ks[6], (D, D), jnp.float32) * w_std, 'bp': jax.random.normal(ks[7], (D,), jnp.float32) * w_std}
    _L0_xattn_all = _L0_xattn_setup()
    _L0_xattn_in = {k: v for k, v in _L0_xattn_all.items() if k in ('wq', 'bq', 'wkv', 'bkv', 'wp', 'bp')}
    del _L0_xattn_all

    def _L0_attn_setup():
        import jax, jax.numpy as jnp
        import numpy as np
        D_MODEL = 256
        D_STATE = 128
        B, S = (8, 128)
        SURPRISE_TEMP = 1.0
        SURPRISE_THR = 0.7
        IMPORTANCE_THR = 0.5
        C_DECAY = 8.0
        RMS_EPS = 1e-06

        def _l2norm(x, eps=1e-12):
            n = jnp.sqrt(jnp.sum(x * x, axis=-1, keepdims=True))
            return x / jnp.maximum(n, eps)

        def _forward(x, Wk, Wv, Wq, fast_lambda, slow_lambda, Waf, baf, Was, bas, nm_w1, nm_b1, nm_w2, nm_b2, ir_w1, ir_b1, ir_w2, ir_b2, pw_w, pw_b, Wo, norm_w):
            b, s, _ = x.shape
            d = Wk.shape[1]
            k = _l2norm(x @ Wk)
            v = x @ Wv
            q = _l2norm(x @ Wq)
            r_fast = jax.nn.sigmoid(x @ Waf + baf)
            r_slow = jax.nn.sigmoid(x @ Was + bas)
            log_af = jnp.log(jax.nn.sigmoid(fast_lambda) + 1e-08)
            log_as = jnp.log(jax.nn.sigmoid(slow_lambda) + 1e-08)
            alpha_fast = jnp.exp(C_DECAY * r_fast * log_af)
            alpha_slow = jnp.exp(C_DECAY * r_slow * log_as)
            importance = jax.nn.sigmoid(jax.nn.gelu(x @ ir_w1 + ir_b1, approximate=False) @ ir_w2 + ir_b2)
            path_w = jax.nn.softmax(x @ pw_w + pw_b, axis=-1)
            neural_update = jax.nn.gelu(v @ nm_w1 + nm_b1, approximate=False) @ nm_w2 + nm_b2

            def step(carry, inp):
                fH, sH, nS = carry
                k_t, v_t, q_t, af_t, as_t, imp_t, pw_t, nu_t = inp
                pred_fast = jnp.einsum('bq,bqv->bv', q_t, fH)
                pred_slow = jnp.einsum('bq,bqv->bv', q_t, sH)
                pred = (pred_fast + pred_slow) * 0.5
                err = jnp.sum((v_t - pred) ** 2, axis=-1, keepdims=True)
                surprise = jax.nn.sigmoid(err / (SURPRISE_TEMP + 1e-06))
                sur_e = surprise[:, :, None]
                kv = k_t[:, :, None] * v_t[:, None, :]
                kpf = jnp.einsum('bk,bkv->bv', k_t, fH)
                delta_fast = kv - k_t[:, :, None] * kpf[:, None, :]
                af = af_t[:, :, None]
                fH = af * fH + (1.0 - af) * (sur_e * delta_fast)
                upd_slow = (imp_t > IMPORTANCE_THR).astype(x.dtype)[:, :, None]
                kps = jnp.einsum('bk,bkv->bv', k_t, sH)
                delta_slow = kv - k_t[:, :, None] * kps[:, None, :]
                a_s = as_t[:, :, None]
                sH = a_s * sH + (1.0 - a_s) * upd_slow * (sur_e * delta_slow)
                upd_n = (surprise > SURPRISE_THR).astype(x.dtype)
                nS = nS + upd_n * (nu_t - nS) * 0.1
                out_f = jnp.einsum('bq,bqv->bv', q_t, fH)
                out_s = jnp.einsum('bq,bqv->bv', q_t, sH)
                out_t = pw_t[:, 0:1] * out_f + pw_t[:, 1:2] * out_s + pw_t[:, 2:3] * nS
                return ((fH, sH, nS), out_t)
            init = (jnp.zeros((b, d, d), x.dtype), jnp.zeros((b, d, d), x.dtype), jnp.zeros((b, d), x.dtype))
            xs = tuple((jnp.swapaxes(a, 0, 1) for a in (k, v, q, alpha_fast, alpha_slow, importance, path_w, neural_update)))
            _, outs = jax.lax.scan(step, init, xs)
            out = jnp.swapaxes(outs, 0, 1)
            of = out.astype(jnp.float32)
            of = of * jax.lax.rsqrt(jnp.mean(of * of, axis=-1, keepdims=True) + RMS_EPS)
            out = (of * norm_w).astype(out.dtype)
            return out @ Wo
        key = jax.random.key(seed)
        ks = jax.random.split(key, 24)
        std = 0.02
        p = {}
        p['x'] = jax.random.normal(ks[0], (B, S, D_MODEL), dtype=jnp.float32)
        p['Wk'] = jax.random.normal(ks[1], (D_MODEL, D_STATE)) * std
        p['Wv'] = jax.random.normal(ks[2], (D_MODEL, D_STATE)) * std
        p['Wq'] = jax.random.normal(ks[3], (D_MODEL, D_STATE)) * std
        p['fast_lambda'] = jax.random.uniform(ks[4], (D_STATE,), minval=2.0, maxval=4.0)
        p['slow_lambda'] = jax.random.uniform(ks[5], (D_STATE,), minval=6.0, maxval=10.0)
        p['Waf'] = jax.random.normal(ks[6], (D_MODEL, D_STATE)) * std
        p['baf'] = jnp.zeros((D_STATE,))
        p['Was'] = jax.random.normal(ks[7], (D_MODEL, D_STATE)) * std
        p['bas'] = jnp.zeros((D_STATE,))
        p['nm_w1'] = jax.random.normal(ks[8], (D_STATE, 2 * D_STATE)) * std
        p['nm_b1'] = jnp.zeros((2 * D_STATE,))
        p['nm_w2'] = jax.random.normal(ks[9], (2 * D_STATE, D_STATE)) * std
        p['nm_b2'] = jnp.zeros((D_STATE,))
        p['ir_w1'] = jax.random.normal(ks[10], (D_MODEL, D_STATE)) * std
        p['ir_b1'] = jnp.zeros((D_STATE,))
        p['ir_w2'] = jax.random.normal(ks[11], (D_STATE, 1)) * std
        p['ir_b2'] = jnp.zeros((1,))
        p['pw_w'] = jax.random.normal(ks[12], (D_MODEL, 3)) * std
        p['pw_b'] = jnp.zeros((3,))
        p['Wo'] = jax.random.normal(ks[13], (D_STATE, D_MODEL)) * std
        p['norm_w'] = jnp.ones((D_STATE,))
        return p
    _L0_attn_all = _L0_attn_setup()
    _L0_attn_in = {k: v for k, v in _L0_attn_all.items() if k in ('Wk', 'Wv', 'Wq', 'fast_lambda', 'slow_lambda', 'Waf', 'baf', 'Was', 'bas', 'nm_w1', 'nm_b1', 'nm_w2', 'nm_b2', 'ir_w1', 'ir_b1', 'ir_w2', 'ir_b2', 'pw_w', 'pw_b', 'Wo', 'norm_w')}
    del _L0_attn_all

    def _L0_ffn_setup():
        import jax, jax.numpy as jnp
        import numpy as np
        B, S, H = (1, 128, 256)
        E, I, TOP_K = (64, 96, 8)
        key = jax.random.key(seed)
        k1, k2, k3, k4, k5 = jax.random.split(key, 5)
        std = 0.02
        return {'hidden_states': jax.random.normal(k1, (B, S, H), dtype=jnp.float32), 'router_w': jax.random.normal(k2, (E, H), dtype=jnp.float32) * std, 'gate_w': jax.random.normal(k3, (E, I, H), dtype=jnp.float32) * std, 'up_w': jax.random.normal(k4, (E, I, H), dtype=jnp.float32) * std, 'down_w': jax.random.normal(k5, (E, H, I), dtype=jnp.float32) * std}
    _L0_ffn_all = _L0_ffn_setup()
    _L0_ffn_in = {k: v for k, v in _L0_ffn_all.items() if k in ('router_w', 'gate_w', 'up_w', 'down_w')}
    del _L0_ffn_all
    return {'x': x, 'ctx_2048': ctx_2048, 'L0_xattn_wq': _L0_xattn_in['wq'], 'L0_xattn_bq': _L0_xattn_in['bq'], 'L0_xattn_wkv': _L0_xattn_in['wkv'], 'L0_xattn_bkv': _L0_xattn_in['bkv'], 'L0_xattn_wp': _L0_xattn_in['wp'], 'L0_xattn_bp': _L0_xattn_in['bp'], 'L0_attn_Wk': _L0_attn_in['Wk'], 'L0_attn_Wv': _L0_attn_in['Wv'], 'L0_attn_Wq': _L0_attn_in['Wq'], 'L0_attn_fast_lambda': _L0_attn_in['fast_lambda'], 'L0_attn_slow_lambda': _L0_attn_in['slow_lambda'], 'L0_attn_Waf': _L0_attn_in['Waf'], 'L0_attn_baf': _L0_attn_in['baf'], 'L0_attn_Was': _L0_attn_in['Was'], 'L0_attn_bas': _L0_attn_in['bas'], 'L0_attn_nm_w1': _L0_attn_in['nm_w1'], 'L0_attn_nm_b1': _L0_attn_in['nm_b1'], 'L0_attn_nm_w2': _L0_attn_in['nm_w2'], 'L0_attn_nm_b2': _L0_attn_in['nm_b2'], 'L0_attn_ir_w1': _L0_attn_in['ir_w1'], 'L0_attn_ir_b1': _L0_attn_in['ir_b1'], 'L0_attn_ir_w2': _L0_attn_in['ir_w2'], 'L0_attn_ir_b2': _L0_attn_in['ir_b2'], 'L0_attn_pw_w': _L0_attn_in['pw_w'], 'L0_attn_pw_b': _L0_attn_in['pw_b'], 'L0_attn_Wo': _L0_attn_in['Wo'], 'L0_attn_norm_w': _L0_attn_in['norm_w'], 'L0_ffn_router_w': _L0_ffn_in['router_w'], 'L0_ffn_gate_w': _L0_ffn_in['gate_w'], 'L0_ffn_up_w': _L0_ffn_in['up_w'], 'L0_ffn_down_w': _L0_ffn_in['down_w']}

def reference(x, ctx_2048, L0_xattn_wq, L0_xattn_bq, L0_xattn_wkv, L0_xattn_bkv, L0_xattn_wp, L0_xattn_bp, L0_attn_Wk, L0_attn_Wv, L0_attn_Wq, L0_attn_fast_lambda, L0_attn_slow_lambda, L0_attn_Waf, L0_attn_baf, L0_attn_Was, L0_attn_bas, L0_attn_nm_w1, L0_attn_nm_b1, L0_attn_nm_w2, L0_attn_nm_b2, L0_attn_ir_w1, L0_attn_ir_b1, L0_attn_ir_w2, L0_attn_ir_b2, L0_attn_pw_w, L0_attn_pw_b, L0_attn_Wo, L0_attn_norm_w, L0_ffn_router_w, L0_ffn_gate_w, L0_ffn_up_w, L0_ffn_down_w):
    import jax
    import jax.numpy as jnp

    def _L0_xattn_ref(x, cond, wq, bq, wkv, bkv, wp, bp):
        import jax, jax.numpy as jnp
        import numpy as np
        NUM_HEADS = 16

        def _qdq(x):
            s = jnp.maximum(jnp.max(jnp.abs(x), axis=-1, keepdims=True) / 127.0, 1e-08)
            return jnp.clip(jnp.round(x / s), -127.0, 127.0) * s
        B, N, C = x.shape
        M = cond.shape[1]
        H = NUM_HEADS
        Dh = C // H
        q = _qdq(x) @ _qdq(wq).T + bq
        kv = cond @ wkv.T + bkv
        k, v = jnp.split(kv, 2, axis=-1)
        q = q.reshape(B, N, H, Dh)
        k = k.reshape(B, M, H, Dh)
        v = v.reshape(B, M, H, Dh)
        scale = 1.0 / np.sqrt(Dh)
        attn = jax.nn.softmax(jnp.einsum('bnhd,bmhd->bhnm', q, k) * scale, axis=-1)
        o = jnp.einsum('bhnm,bmhd->bnhd', attn, v).reshape(B, N, C)
        out = _qdq(o) @ _qdq(wp).T + bp
        return out

    def _L0_attn_ref(x, Wk, Wv, Wq, fast_lambda, slow_lambda, Waf, baf, Was, bas, nm_w1, nm_b1, nm_w2, nm_b2, ir_w1, ir_b1, ir_w2, ir_b2, pw_w, pw_b, Wo, norm_w):
        import jax, jax.numpy as jnp
        import numpy as np
        D_MODEL = 256
        D_STATE = 128
        B, S = (8, 128)
        SURPRISE_TEMP = 1.0
        SURPRISE_THR = 0.7
        IMPORTANCE_THR = 0.5
        C_DECAY = 8.0
        RMS_EPS = 1e-06

        def _l2norm(x, eps=1e-12):
            n = jnp.sqrt(jnp.sum(x * x, axis=-1, keepdims=True))
            return x / jnp.maximum(n, eps)

        def _forward(x, Wk, Wv, Wq, fast_lambda, slow_lambda, Waf, baf, Was, bas, nm_w1, nm_b1, nm_w2, nm_b2, ir_w1, ir_b1, ir_w2, ir_b2, pw_w, pw_b, Wo, norm_w):
            b, s, _ = x.shape
            d = Wk.shape[1]
            k = _l2norm(x @ Wk)
            v = x @ Wv
            q = _l2norm(x @ Wq)
            r_fast = jax.nn.sigmoid(x @ Waf + baf)
            r_slow = jax.nn.sigmoid(x @ Was + bas)
            log_af = jnp.log(jax.nn.sigmoid(fast_lambda) + 1e-08)
            log_as = jnp.log(jax.nn.sigmoid(slow_lambda) + 1e-08)
            alpha_fast = jnp.exp(C_DECAY * r_fast * log_af)
            alpha_slow = jnp.exp(C_DECAY * r_slow * log_as)
            importance = jax.nn.sigmoid(jax.nn.gelu(x @ ir_w1 + ir_b1, approximate=False) @ ir_w2 + ir_b2)
            path_w = jax.nn.softmax(x @ pw_w + pw_b, axis=-1)
            neural_update = jax.nn.gelu(v @ nm_w1 + nm_b1, approximate=False) @ nm_w2 + nm_b2

            def step(carry, inp):
                fH, sH, nS = carry
                k_t, v_t, q_t, af_t, as_t, imp_t, pw_t, nu_t = inp
                pred_fast = jnp.einsum('bq,bqv->bv', q_t, fH)
                pred_slow = jnp.einsum('bq,bqv->bv', q_t, sH)
                pred = (pred_fast + pred_slow) * 0.5
                err = jnp.sum((v_t - pred) ** 2, axis=-1, keepdims=True)
                surprise = jax.nn.sigmoid(err / (SURPRISE_TEMP + 1e-06))
                sur_e = surprise[:, :, None]
                kv = k_t[:, :, None] * v_t[:, None, :]
                kpf = jnp.einsum('bk,bkv->bv', k_t, fH)
                delta_fast = kv - k_t[:, :, None] * kpf[:, None, :]
                af = af_t[:, :, None]
                fH = af * fH + (1.0 - af) * (sur_e * delta_fast)
                upd_slow = (imp_t > IMPORTANCE_THR).astype(x.dtype)[:, :, None]
                kps = jnp.einsum('bk,bkv->bv', k_t, sH)
                delta_slow = kv - k_t[:, :, None] * kps[:, None, :]
                a_s = as_t[:, :, None]
                sH = a_s * sH + (1.0 - a_s) * upd_slow * (sur_e * delta_slow)
                upd_n = (surprise > SURPRISE_THR).astype(x.dtype)
                nS = nS + upd_n * (nu_t - nS) * 0.1
                out_f = jnp.einsum('bq,bqv->bv', q_t, fH)
                out_s = jnp.einsum('bq,bqv->bv', q_t, sH)
                out_t = pw_t[:, 0:1] * out_f + pw_t[:, 1:2] * out_s + pw_t[:, 2:3] * nS
                return ((fH, sH, nS), out_t)
            init = (jnp.zeros((b, d, d), x.dtype), jnp.zeros((b, d, d), x.dtype), jnp.zeros((b, d), x.dtype))
            xs = tuple((jnp.swapaxes(a, 0, 1) for a in (k, v, q, alpha_fast, alpha_slow, importance, path_w, neural_update)))
            _, outs = jax.lax.scan(step, init, xs)
            out = jnp.swapaxes(outs, 0, 1)
            of = out.astype(jnp.float32)
            of = of * jax.lax.rsqrt(jnp.mean(of * of, axis=-1, keepdims=True) + RMS_EPS)
            out = (of * norm_w).astype(out.dtype)
            return out @ Wo
        return _forward(x, Wk, Wv, Wq, fast_lambda, slow_lambda, Waf, baf, Was, bas, nm_w1, nm_b1, nm_w2, nm_b2, ir_w1, ir_b1, ir_w2, ir_b2, pw_w, pw_b, Wo, norm_w)

    def _L0_ffn_ref(hidden_states, router_w, gate_w, up_w, down_w):
        import jax, jax.numpy as jnp
        import numpy as np
        B, S, H = (1, 128, 256)
        E, I, TOP_K = (64, 96, 8)
        b, s, h = hidden_states.shape
        x = hidden_states.reshape(-1, h)
        T = x.shape[0]
        logits = x @ router_w.T
        probs = jax.nn.softmax(logits.astype(jnp.float32), axis=-1)
        topk_w, topk_idx = jax.lax.top_k(probs, TOP_K)
        topk_w = topk_w / jnp.sum(topk_w, axis=-1, keepdims=True)
        topk_w = topk_w.astype(hidden_states.dtype)
        tok = jnp.arange(T)[:, None]
        combine = jnp.zeros((T, E), dtype=hidden_states.dtype).at[tok, topk_idx].add(topk_w)

        def body(acc, p):
            gw, uw, dw, cw = p
            hidden = jax.nn.silu(x @ gw.T) * (x @ uw.T)
            out = hidden @ dw.T
            return (acc + cw[:, None] * out, None)
        init = jnp.zeros_like(x)
        final, _ = jax.lax.scan(body, init, (gate_w, up_w, down_w, combine.T))
        return final.reshape(b, s, h)
    x = x + _L0_xattn_ref(_layernorm(x, axis=-1), ctx_2048, L0_xattn_wq, L0_xattn_bq, L0_xattn_wkv, L0_xattn_bkv, L0_xattn_wp, L0_xattn_bp)
    x = x + _L0_attn_ref(_layernorm(x, axis=-1), L0_attn_Wk, L0_attn_Wv, L0_attn_Wq, L0_attn_fast_lambda, L0_attn_slow_lambda, L0_attn_Waf, L0_attn_baf, L0_attn_Was, L0_attn_bas, L0_attn_nm_w1, L0_attn_nm_b1, L0_attn_nm_w2, L0_attn_nm_b2, L0_attn_ir_w1, L0_attn_ir_b1, L0_attn_ir_w2, L0_attn_ir_b2, L0_attn_pw_w, L0_attn_pw_b, L0_attn_Wo, L0_attn_norm_w)
    x = x + _L0_ffn_ref(_layernorm(x, axis=-1), L0_ffn_router_w, L0_ffn_gate_w, L0_ffn_up_w, L0_ffn_down_w)
    return x

_drawn_inputs = setup_inputs


def setup_inputs(seed=0):
    import zlib

    import numpy as np

    out = dict(_drawn_inputs(seed))
    spreads = {'L0_attn_baf': (0.0, 2.0),
     'L0_attn_bas': (0.0, 0.8),
     'L0_attn_nm_b1': (0.0, 0.1),
     'L0_attn_nm_b2': (0.0, 0.1),
     'L0_attn_ir_b1': (0.0, 0.8),
     'L0_attn_pw_b': (0.0, 0.8),
     'L0_attn_norm_w': (1.0, 0.2)}
    factors = {'L0_xattn_wq': 8.0,
     'L0_xattn_bq': 64.0,
     'L0_xattn_bkv': 8.0,
     'L0_xattn_bp': 2.863,
     'L0_attn_fast_lambda': 38.104,
     'L0_attn_slow_lambda': 8.0,
     'L0_attn_Waf': 64.0,
     'L0_attn_Was': 8.0,
     'L0_attn_nm_w1': 6.617,
     'L0_attn_ir_w1': 8.0,
     'L0_attn_ir_w2': 8.0,
     'L0_attn_pw_w': 18.642,
     'L0_ffn_router_w': 8.0,
     'L0_ffn_gate_w': 8.0,
     'L0_ffn_up_w': 8.0,
     'L0_ffn_down_w': 8.0,
     'L0_attn_Wk': 8.0,
     'L0_attn_Wq': 8.0}
    for name, (base, spread) in spreads.items():
        noise = np.random.default_rng([zlib.crc32(name.encode()), seed]).standard_normal(out[name].shape)
        drawn = base * np.exp(spread * noise) if base else spread * noise
        out[name] = jnp.asarray(drawn.astype(out[name].dtype))
    for name, factor in factors.items():
        out[name] = (out[name] * factor).astype(out[name].dtype)
    return out
```

```python
from contextlib import ExitStack

import concourse.bass as bass
from concourse import mybir

F32 = mybir.dt.float32
F16 = mybir.dt.float16
ACT = mybir.ActivationFunctionType
ALU = mybir.AluOpType
AX = mybir.AxisListType

P = 128
BATCH, STEPS, DM = 16, 64, 256
CTX = 1601
HEADS, DH = 16, 16
TOK = BATCH * STEPS
TILES = TOK // P
CI = DM // P
HG = P // DH
PAIRS = HEADS // 2
NCH = 4
COLS = [(0, 401), (401, 400), (801, 400), (1201, 400)]
ROWS = [(m, min(P, CTX - m)) for m in range(0, CTX, P)]
KROW = len(ROWS)
KGROUPS = CI * NCH
PROJ = KGROUPS + KROW
PROJ_STEP = 3
TGROUP = 4
TG = -(-KROW // TGROUP)
ROUND = 12582912.0
EPS_LN = 1e-5
assert PROJ == PROJ_STEP * (PAIRS - 1)


class Named:
    pass


class Tally:

    def __init__(self, sem):
        self.sem, self.n = sem, 0

    def inc(self, ins, by=1):
        ins.then_inc(self.sem, by)
        self.n += by
        return self.n


def row_stats(dve, t, src, done):
    for n in range(TILES):
        last = done.inc(dve.bn_stats(t.stat[:, n, :], src[:, n, :]))
    dve.wait_ge(done.sem, last)
    for n in range(TILES):
        last = done.inc(dve.bn_aggr(t.mv[:, n, :], t.stat[:, n, :]))
    dve.wait_ge(done.sem, last)
    return done.inc(dve.tensor_scalar(t.var[:, :], t.mv[:, :, 1], EPS_LN, None, ALU.add))


def normalise(dve, t, dst, src, done):
    last = done.inc(dve.reciprocal(t.rstd[:, :], t.std[:, :]))
    dve.wait_ge(done.sem, last)
    for n in range(TILES):
        last = done.inc(dve.tensor_scalar(dst[:, n, :], src[:, n, :], t.mv[:, n, 0:1], t.rstd[:, n:n + 1],
                                          ALU.subtract, ALU.mult))
    return last


def fake_quantise(dve, t, dst, src, n, done):
    last = done.inc(dve.tensor_reduce(t.amax[:, 0:n], src[:, :, :], AX.X, ALU.max, apply_absolute_value=True))
    dve.wait_ge(done.sem, last)
    last = done.inc(dve.tensor_scalar(t.qs[:, 0:n], t.amax[:, 0:n], 1.0 / 127.0, 1e-8, ALU.mult, ALU.max))
    dve.wait_ge(done.sem, last)
    last = done.inc(dve.reciprocal(t.qr[:, 0:n], t.qs[:, 0:n]))
    dve.wait_ge(done.sem, last)
    for k in range(n):
        last = done.inc(dve.tensor_scalar(src[:, k, :], src[:, k, :], t.qr[:, k:k + 1], ROUND, ALU.mult, ALU.add))
    dve.wait_ge(done.sem, last)
    last = done.inc(dve.tensor_scalar(src[:, :, :], src[:, :, :], ROUND, -127.0, ALU.subtract, ALU.max))
    dve.wait_ge(done.sem, last)
    for k in range(n):
        last = done.inc(dve.tensor_scalar(dst[:, k, :], src[:, k, :], 127.0, t.qs[:, k:k + 1], ALU.min, ALU.mult))
    return last


def queries(nc, io, c, t, bank):
    with ExitStack() as ctx:
        def sem(name):
            return ctx.enter_context(nc.semaphore(name))

        x_in, w_in, b_in = sem("q_x_in"), sem("q_w_in"), sem("q_b_in")
        pool_done, dve_done = sem("q_pool_done"), sem("q_dve_done")
        std_ready, turned, moved, wq_moved = (sem("q_std_ready"), sem("q_turned"), sem("q_moved"),
                                              sem("q_weights_moved"))
        w_turned, q_ready = sem("q_w_turned"), sem("q_ready")
        consts_ready = sem("q_consts_ready")
        var_ready, wquant, xquant = sem("q_var_ready"), sem("q_wquant"), sem("q_xquant")
        block = ctx.enter_context(nc.Block())

        @block.sync
        def _(sp):
            sp.dma_start(t.x[:, :, :], io["x"].rearrange("b t d -> (b t) d")
                         .rearrange("(n p) d -> p n d", p=P)).then_inc(x_in, 16)
            for w, dst in ((io["wq"], t.wq), (io["wp"], t.wp)):
                sp.dma_start(dst[:, :, :], w.rearrange("(j p) i -> p j i", p=P)).then_inc(w_in, 16)
            sp.dma_start(c.wkvT[:, :, :], io["wkvT"].rearrange("(j p) o -> p j o", p=P)).then_inc(b_in, 16)
            sp.dma_start(c.bk[:, :], io["bkvT"]).then_inc(b_in, 16)
            sp.dma_start(c.bq[:, :], io["bqT"]).then_inc(b_in, 16)
            sp.dma_start(c.bv[:, :], io["bv"].partition_broadcast(P)).then_inc(b_in, 16)
            sp.dma_start(c.bp[:, :], io["bp"].partition_broadcast(P)).then_inc(b_in, 16)
            sp.wait_ge(b_in, 80)

        @block.gpsimd
        def _(pool):
            done = Tally(pool_done)
            done.inc(pool.memset(c.ident[:, :], 0.0))
            done.inc(pool.memset(c.head_mask[:, :], 0.25))
            done.inc(pool.memset(c.pair_mask[:, :, :], 1.0))
            done.inc(pool.memset(c.gather[:, :], 0.0))
            done.inc(pool.memset(c.ones[:, :], 1.0))
            last = done.inc(pool.memset(c.batch_mask[:, :], 1.0))
            pool.wait_ge(pool_done, last)
            done.inc(pool.affine_select(out=c.ident[:, :], in_=c.ident[:, :], compare_op=ALU.not_equal,
                                        fill=1.0, base=0, pattern=[[-1, P]], channel_multiplier=1))
            last = done.inc(pool.affine_select(out=c.head_mask[:, :], in_=c.head_mask[:, :],
                                               compare_op=ALU.is_ge, fill=0.0, base=0,
                                               pattern=[[-DH, HG]], channel_multiplier=1))
            pool.wait_ge(pool_done, last)
            done.inc(pool.affine_select(out=c.head_mask[:, :], in_=c.head_mask[:, :], compare_op=ALU.is_ge,
                                        fill=0.0, base=DH - 1, pattern=[[DH, HG]], channel_multiplier=-1))
            for half, sign in enumerate((-1, 1)):
                own = c.pair_mask[:, half, :]
                done.inc(pool.affine_select(out=own, in_=own, compare_op=ALU.is_ge, fill=0.0,
                                            base=(STEPS - 1, -STEPS)[half], pattern=[[0, DH]],
                                            channel_multiplier=sign))
            mid = c.gather[:, STEPS:2 * STEPS]
            last = done.inc(pool.affine_select(out=mid, in_=mid, compare_op=ALU.not_equal, fill=1.0, base=0,
                                               pattern=[[-1, STEPS]], channel_multiplier=1))
            done.inc(pool.affine_select(out=c.batch_mask[:, :], in_=c.batch_mask[:, :], compare_op=ALU.is_ge,
                                        fill=0.0, base=0, pattern=[[-8, BATCH]], channel_multiplier=1))
            last = done.n
            pool.wait_ge(pool_done, last)
            done.inc(pool.affine_select(out=mid, in_=mid, compare_op=ALU.not_equal, fill=1.0, base=-STEPS,
                                        pattern=[[-1, STEPS]], channel_multiplier=1))
            last = done.inc(pool.affine_select(out=c.batch_mask[:, :], in_=c.batch_mask[:, :],
                                               compare_op=ALU.is_ge, fill=0.0, base=7,
                                               pattern=[[8, BATCH]], channel_multiplier=-1))
            pool.wait_ge(pool_done, last)
            pool.sem_inc(consts_ready, 1)

        @block.vector
        def _(dve):
            done = Tally(dve_done)
            dve.wait_ge(w_in, 32)
            fake_quantise(dve, t, t.wq, t.wq, CI, done)
            dve.wait_ge(dve_done, done.n)
            last = fake_quantise(dve, t, t.wp, t.wp, CI, done)
            dve.wait_ge(dve_done, last)
            dve.sem_inc(wquant, 1)
            dve.wait_ge(x_in, 16)
            last = row_stats(dve, t, t.x, done)
            dve.wait_ge(dve_done, last)
            dve.sem_inc(var_ready, 1)
            dve.wait_ge(std_ready, 1)
            last = normalise(dve, t, t.y, t.x, done)
            dve.wait_ge(dve_done, last)
            last = fake_quantise(dve, t, t.y, t.y, TILES, done)
            dve.wait_ge(dve_done, last)
            dve.sem_inc(xquant, 1)
            for n in range(TILES):
                dve.wait_ge(turned, n + 1)
                dve.tensor_copy(t.yT[:, :, n * P:(n + 1) * P],
                                bank[n][:, 0:DM].rearrange("p (j q) -> p j q", j=CI)).then_inc(moved, 1)

        @block.scalar
        def _(act):
            act.wait_ge(w_turned, 2)
            for k, dst in enumerate((c.wqT, c.wpT)):
                act.activation(dst[:, :, :], bank[k][:, :].rearrange("p (j o) -> p j o", j=CI),
                               ACT.Copy).then_inc(wq_moved, 1)
            act.wait_ge(var_ready, 1)
            act.activation(t.std[:, :], t.var[:, :], ACT.Sqrt).then_inc(std_ready, 1)
            act.wait_ge(b_in, 80)
            for k in range(2 * CI):
                j, half = k // 2, k % 2
                act.wait_ge(q_ready, k + 1)
                act.activation(c.qT[:, j, half * 512:half * 512 + 512], bank[k][:, :], ACT.Identity,
                               bias=c.bq[:, j:j + 1])

        @block.tensor
        def _(pe):
            pe.wait_ge(consts_ready, 1)
            pe.wait_ge(wquant, 1)
            for k, w in enumerate((t.wq, t.wp)):
                for i in range(CI):
                    for o in range(CI):
                        ins = pe.transpose(bank[k][:, i * DM + o * P:i * DM + o * P + P],
                                           w[:, o, i * P:(i + 1) * P], c.ident[:, :])
                ins.then_inc(w_turned, 1)
            pe.wait_ge(xquant, 1)
            pe.wait_ge(wq_moved, 2)
            for n in range(TILES):
                for i in range(CI):
                    ins = pe.transpose(bank[n][:, i * P:(i + 1) * P], t.y[:, n, i * P:(i + 1) * P],
                                       c.ident[:, :])
                ins.then_inc(turned, 1)
            for k in range(2 * CI):
                j, half = k // 2, k % 2
                if k == 0:
                    pe.wait_ge(moved, TILES)
                for i in range(CI):
                    ins = pe.matmul(bank[k][:, :], c.wqT[:, i, j * P:(j + 1) * P],
                                    t.yT[:, i, half * 512:half * 512 + 512], start=(i == 0), stop=(i == CI - 1))
                ins.then_inc(q_ready, 1)


def attention(nc, io, c, t, bank):
    score = bank[0:4]
    turn = bank[4:6]
    pvb, prj = bank[6], bank[7]
    with ExitStack() as ctx:
        def sb(name, shape):
            return ctx.enter_context(nc.sbuf_tensor(name, shape, F32))

        def sem(name):
            return ctx.enter_context(nc.semaphore(name))

        ctxT = [sb(f"ctxT{u}", [P, CI, CTX]) for u in range(2)]
        kT = [sb(f"kT{u}", [P, CI, CTX]) for u in range(2)]
        v = [sb(f"v{u}", [P, KROW, DM]) for u in range(2)]
        qblk = [sb(f"qblk{u}", [P, CI, HG, STEPS]) for u in range(2)]
        prob = [sb(f"prob{u}", [P, CTX]) for u in range(2)]
        probT = [sb(f"probT{u}", [P, TGROUP * P]) for u in range(2)]
        mx = sb("mx", [P, NCH])
        negmax = [sb(f"negmax{u}", [P, 1]) for u in range(2)]
        esum = [sb(f"esum{u}", [P, NCH]) for u in range(2)]
        den = sb("den", [P, 1])
        rden = sb("rden", [P, 1])

        ctx_in = [sem(f"ctx_in{u}") for u in range(2)]
        q_masked, proj_done, proj_out = sem("q_masked"), sem("proj_done"), sem("proj_out")
        scored, max_ready, exp_done = sem("scored"), sem("max_ready"), sem("exp_done")
        turned, turned_out, pv_done, o_out = sem("a_turned"), sem("turned_out"), sem("pv_done"), sem("o_out")
        mx_done, den_done = sem("mx_done"), sem("den_done")
        block = ctx.enter_context(nc.Block())

        def load(sp, b, u):
            sp.dma_start(ctxT[u][:, :, :], io["ctxT"][bass.ds(b, 1), :, :].rearrange("o (j p) m -> p (o j) m", p=P)
                         ).then_inc(ctx_in[u], 16)

        @block.sync
        def _(sp):
            load(sp, 0, 0)
            load(sp, 1, 1)
            with sp.Fori(0, BATCH // 2 - 1) as i:
                for u in range(2):
                    sp.wait_ge(proj_done, (2 * i + u + 1) * PROJ)
                    load(sp, 2 * i + u + 2, u)

        @block.gpsimd
        def _(pool):
            def mask(b, u, first):
                if not first:
                    pool.wait_ge(scored, (b - 1) * (PAIRS * NCH))
                for j in range(CI):
                    q = c.qT[:, j:j + 1, bass.ds(b * STEPS, STEPS)].broadcast_to([P, HG, STEPS])
                    own = c.head_mask[:, :].unsqueeze(2).broadcast_to([P, HG, STEPS])
                    pool.tensor_tensor(qblk[u][:, j, :, :], q, own, ALU.mult).then_inc(q_masked, 1)

            mask(0, 0, True)
            mask(1, 1, True)
            with pool.Fori(0, BATCH // 2 - 1) as i:
                for u in range(2):
                    mask(2 * i + u + 2, u, False)

        @block.scalar
        def _(act):
            def project_out(b, k, u):
                act.wait_ge(proj_done, b * PROJ + k + 1)
                if k < KGROUPS:
                    j, n = k // NCH, k % NCH
                    c0, w = COLS[n]
                    ins = act.activation(kT[u][:, j, c0:c0 + w], prj[:, 0:w], ACT.Identity,
                                         bias=c.bk[:, j:j + 1])
                else:
                    m = k - KGROUPS
                    ins = act.activation(v[u][0:ROWS[m][1], m, :], prj[0:ROWS[m][1], 0:DM], ACT.Copy)
                ins.then_inc(proj_out, 1)

            def exps(b, g, first):
                act.wait_ge(max_ready, b * PAIRS + g + 1)
                if not first:
                    act.wait_ge(turned, (b * PAIRS + g - 1) * TG)
                    act.wait_ge(o_out, b * PAIRS + g - 1)
                for n, (c0, w) in enumerate(COLS):
                    act.activation(prob[g % 2][:, c0:c0 + w], score[n][:, 0:w], ACT.Exp,
                                   bias=negmax[g % 2][:, 0:1],
                                   accum_out=esum[g % 2][:, n:n + 1]).then_inc(exp_done, 1)

            def batch(b, u, more, first=False):
                for g in range(PAIRS):
                    if more and g < PAIRS - 1:
                        project_out(b + 1, PROJ_STEP * g, 1 - u)
                    if g < PAIRS - 1:
                        exps(b, g + 1, first and g == 0)
                    elif more:
                        exps(b + 1, 0, False)
                    if more and g < PAIRS - 1:
                        project_out(b + 1, PROJ_STEP * g + 1, 1 - u)
                        project_out(b + 1, PROJ_STEP * g + 2, 1 - u)

            for k in range(PROJ):
                project_out(0, k, 0)
            exps(0, 0, True)
            batch(0, 0, True, True)
            with act.Fori(0, BATCH // 2 - 1) as i:
                batch(2 * i + 1, 1, True)
                batch(2 * i + 2, 0, True)
            batch(BATCH - 1, 1, False)

        @block.vector
        def _(dve):
            def maxima(b, g):
                for n, (c0, w) in enumerate(COLS):
                    dve.wait_ge(scored, (b * PAIRS + g) * NCH + n + 1)
                    dve.tensor_reduce(mx[:, n:n + 1], score[n][:, 0:w], AX.X, ALU.max).then_inc(mx_done, 1)
                dve.wait_ge(mx_done, (b * PAIRS + g + 1) * NCH)
                dve.tensor_reduce(negmax[g % 2][:, :], mx[:, :], AX.X, ALU.max, negate=True).then_inc(max_ready, 1)

            def turned_to_sbuf(b, g, r, first):
                k = (b * PAIRS + g) * TG + r
                dve.wait_ge(turned, k + 1)
                if not first:
                    dve.wait_ge(pv_done, k - 1)
                n = min(TGROUP, KROW - r * TGROUP)
                rows = ROWS[r * TGROUP + n - 1][1]
                dve.tensor_copy(probT[k2(g, r)][0:rows, 0:n * P], turn[k2(g, r)][0:rows, 0:n * P]
                                ).then_inc(turned_out, 1)

            def output(b, g):
                G = b * PAIRS + g
                dve.wait_ge(exp_done, (G + 1) * NCH)
                dve.tensor_reduce(den[:, :], esum[g % 2][:, :], AX.X, ALU.add).then_inc(den_done, 1)
                dve.wait_ge(den_done, 2 * G + 1)
                dve.reciprocal(rden[:, :], den[:, :]).then_inc(den_done, 1)
                dve.wait_ge(den_done, 2 * G + 2)
                dve.wait_ge(pv_done, (G + 1) * TG)
                h0 = 2 * DH * (g % (PAIRS // CI))
                dve.scalar_tensor_tensor(out=t.o[:, bass.ds(b, 1), g, :].rearrange("p o d -> p (o d)"),
                                         in0=pvb[:, h0:h0 + 2 * DH], scalar=rden[:, 0:1],
                                         in1=c.pair_mask[:, :, :].rearrange("p h d -> p (h d)"),
                                         op0=ALU.mult, op1=ALU.mult).then_inc(o_out, 1)

            def batch(b, u, more, first=False):
                for g in range(PAIRS):
                    if g < PAIRS - 1:
                        maxima(b, g + 1)
                    elif more:
                        maxima(b + 1, 0)
                    for r in range(TG):
                        turned_to_sbuf(b, g, r, first and g == 0 and r < 2)
                    output(b, g)

            maxima(0, 0)
            batch(0, 0, True, True)
            with dve.Fori(0, BATCH // 2 - 1) as i:
                batch(2 * i + 1, 1, True)
                batch(2 * i + 2, 0, True)
            batch(BATCH - 1, 1, False)

        @block.tensor
        def _(pe):
            def project(b, k, u, first):
                if not first:
                    pe.wait_ge(proj_out, b * PROJ + k)
                if k < KGROUPS:
                    j, n = k // NCH, k % NCH
                    c0, w = COLS[n]
                    for i in range(CI):
                        ins = pe.matmul(prj[:, 0:w], c.wkvT[:, i, j * P:(j + 1) * P], ctxT[u][:, i, c0:c0 + w],
                                        start=(i == 0), stop=(i == CI - 1))
                else:
                    m0, rows = ROWS[k - KGROUPS]
                    for i in range(CI):
                        ins = pe.matmul(prj[0:rows, 0:DM], ctxT[u][:, i, m0:m0 + rows], c.wkvT[:, i, DM:2 * DM],
                                        start=(i == 0), stop=(i == CI - 1))
                ins.then_inc(proj_done, 1)

            def scores(b, g, u, first):
                if g == 0:
                    pe.wait_ge(q_masked, (b + 1) * CI)
                    pe.wait_ge(proj_out, b * PROJ + PROJ)
                q = qblk[u][:, g // (PAIRS // CI), 2 * (g % (PAIRS // CI)):2 * (g % (PAIRS // CI)) + 2, :]
                for n, (c0, w) in enumerate(COLS):
                    if not first:
                        pe.wait_ge(exp_done, (b * PAIRS + g - 1) * NCH + n + 1)
                    pe.matmul(score[n][:, 0:w], q.rearrange("p h q -> p (h q)"),
                              kT[u][:, g // (PAIRS // CI), c0:c0 + w], start=True, stop=True
                              ).then_inc(scored, 1)

            def turn_probs(b, g, r, first):
                k = (b * PAIRS + g) * TG + r
                if r == 0:
                    pe.wait_ge(exp_done, (b * PAIRS + g + 1) * NCH)
                if not first:
                    pe.wait_ge(turned_out, k - 1)
                for s, (m0, rows) in enumerate(ROWS[r * TGROUP:(r + 1) * TGROUP]):
                    ins = pe.transpose(turn[k2(g, r)][0:rows, s * P:(s + 1) * P], prob[g % 2][:, m0:m0 + rows],
                                       c.ident[:, :])
                ins.then_inc(turned, 1)

            def times_v(b, g, u, r, first):
                k = (b * PAIRS + g) * TG + r
                pe.wait_ge(turned_out, k + 1)
                if r == 0 and not first:
                    pe.wait_ge(o_out, b * PAIRS + g)
                j = g // (PAIRS // CI)
                for s, (m0, rows) in enumerate(ROWS[r * TGROUP:(r + 1) * TGROUP]):
                    m = r * TGROUP + s
                    ins = pe.matmul(pvb[:, 0:P], probT[k2(g, r)][0:rows, s * P:(s + 1) * P],
                                    v[u][0:rows, m, j * P:(j + 1) * P], start=(m == 0), stop=(m == KROW - 1))
                ins.then_inc(pv_done, 1)

            def batch(b, u, more, loads, first=False):
                for g in range(PAIRS):
                    start = first and g == 0
                    if g < PAIRS - 1:
                        scores(b, g + 1, u, False)
                    elif more:
                        scores(b + 1, 0, 1 - u, False)
                    proj = more and g < PAIRS - 1
                    if proj and g == 0:
                        pe.wait_ge(ctx_in[1 - u], 16 * loads)
                    turn_probs(b, g, 0, start)
                    turn_probs(b, g, 1, start)
                    if proj:
                        project(b + 1, PROJ_STEP * g, 1 - u, False)
                    times_v(b, g, u, 0, start)
                    turn_probs(b, g, 2, False)
                    times_v(b, g, u, 1, start)
                    turn_probs(b, g, 3, False)
                    if proj:
                        project(b + 1, PROJ_STEP * g + 1, 1 - u, False)
                    times_v(b, g, u, 2, start)
                    times_v(b, g, u, 3, start)
                    if proj:
                        project(b + 1, PROJ_STEP * g + 2, 1 - u, False)

            pe.wait_ge(ctx_in[0], 16)
            for k in range(PROJ):
                project(0, k, 0, k == 0)
            scores(0, 0, 0, True)
            batch(0, 0, True, 1, True)
            with pe.Fori(0, BATCH // 2 - 1) as i:
                batch(2 * i + 1, 1, True, i + 2)
                batch(2 * i + 2, 0, True, i + 2)
            batch(BATCH - 1, 1, False, 0)


def k2(g, r):
    return (g * TG + r) % 2


def project_attention(nc, io, c, t, bank):
    with ExitStack() as ctx:
        def sem(name):
            return ctx.enter_context(nc.semaphore(name))

        gathered, with_bias, dve_done, oquant = sem("p_gathered"), sem("p_with_bias"), sem("p_dve_done"), sem("p_oquant")
        turned, moved, projected, var_ready, std_ready = (sem("p_turned"), sem("p_moved"), sem("p_projected"),
                                                          sem("p_var_ready"), sem("p_std_ready"))
        y_ready = sem("p_y_ready")
        block = ctx.enter_context(nc.Block())

        @block.tensor
        def _(pe):
            for n in range(TILES):
                for half in range(2):
                    sel = c.gather[:, (1 - half) * STEPS:(1 - half) * STEPS + P]
                    ins = pe.matmul(bank[n][:, 0:DM], sel, t.o[:, 2 * n + half, :, :].rearrange("p g d -> p (g d)"),
                                    start=(half == 0), stop=(half == 1))
                ins.then_inc(gathered, 1)
            pe.wait_ge(oquant, 1)
            for n in range(TILES):
                for i in range(CI):
                    ins = pe.transpose(bank[n][:, i * P:(i + 1) * P], t.y[:, n, i * P:(i + 1) * P], c.ident[:, :])
                ins.then_inc(turned, 1)
            for n in range(TILES):
                pe.wait_ge(moved, n + 1)
                for i in range(CI):
                    ins = pe.matmul(bank[n][:, 0:DM], t.yT[:, i, n * P:(n + 1) * P], c.wpT[:, i, :],
                                    start=(i == 0), stop=(i == CI - 1))
                ins.then_inc(projected, 1)
            pe.wait_ge(y_ready, 1)
            for n in range(TILES):
                for i in range(CI):
                    ins = pe.transpose(bank[n][:, i * P:(i + 1) * P], t.y[:, n, i * P:(i + 1) * P], c.ident[:, :])
                ins.then_inc(turned, 1)

        @block.scalar
        def _(act):
            act.wait_ge(var_ready, 1)
            act.activation(t.std[:, :], t.var[:, :], ACT.Sqrt).then_inc(std_ready, 1)

        @block.vector
        def _(dve):
            done = Tally(dve_done)
            for n in range(TILES):
                dve.wait_ge(gathered, n + 1)
                last = done.inc(dve.tensor_tensor(t.y[:, n, :], bank[n][:, 0:DM], c.bv[:, :], ALU.add))
            dve.wait_ge(dve_done, last)
            last = fake_quantise(dve, t, t.y, t.y, TILES, done)
            dve.wait_ge(dve_done, last)
            dve.sem_inc(oquant, 1)
            for n in range(TILES):
                dve.wait_ge(turned, n + 1)
                dve.tensor_copy(t.yT[:, :, n * P:(n + 1) * P],
                                bank[n][:, 0:DM].rearrange("p (j q) -> p j q", j=CI)).then_inc(moved, 1)
            for n in range(TILES):
                last = done.inc(dve.tensor_tensor(t.x[:, n, :], t.x[:, n, :], c.bp[:, :], ALU.add))
            dve.wait_ge(dve_done, last)
            for n in range(TILES):
                dve.wait_ge(projected, n + 1)
                last = done.inc(dve.tensor_tensor(t.x[:, n, :], bank[n][:, 0:DM], t.x[:, n, :], ALU.add))
            dve.wait_ge(dve_done, last)
            last = row_stats(dve, t, t.x, done)
            dve.wait_ge(dve_done, last)
            dve.sem_inc(var_ready, 1)
            dve.wait_ge(std_ready, 1)
            last = normalise(dve, t, t.y, t.x, done)
            dve.wait_ge(dve_done, last)
            dve.sem_inc(y_ready, 1)
            for n in range(TILES):
                dve.wait_ge(turned, TILES + n + 1)
                dve.tensor_copy(t.yT[:, :, n * P:(n + 1) * P],
                                bank[n][:, 0:DM].rearrange("p (j q) -> p j q", j=CI)).then_inc(moved, 1)


DS = 128
BLK = 8
NB = STEPS // BLK
HALF = BLK // 2
GROUPS = TOK // HALF
PAIR_S = [(s, r) for s in range(HALF) for r in range(s + 1, HALF)]
PAIR_O = [(s, r) for s in range(HALF) for r in range(s, HALF)]
DECAY = 8.0
KIND_K, KIND_Q, KIND_O = range(3)


def features(nc, io, c, t, m, bank):
    with ExitStack() as ctx:
        def sb(name, shape):
            return ctx.enter_context(nc.sbuf_tensor(name, shape, F32))

        def sem(name):
            return ctx.enter_context(nc.semaphore(name))

        w = {n: sb(f"w_{n}", [P, CI, DS]) for n in ("k", "v", "q", "af", "as", "ir")}
        w_pw, w_pwb, w_ir2, w_irb = sb("w_pw", [P, CI, 3]), sb("w_pwb", [P, CI, 3, P]), sb("w_ir2", [P, 1]), sb("w_irb", [P, P])
        w_nm1, w_nm2 = sb("w_nm1", [P, 2 * DS]), sb("w_nm2", [P, 2, DS])
        cols = sb("cols", [P, 12])
        lam8 = sb("lam8", [P, 2])
        la, irg, h1 = sb("la", [P, 2, TOK]), sb("irg", [P, TOK]), sb("h1", [P, 2, TOK])
        lg, sq, nrm = sb("lg", [P, 3, TOK]), sb("sq", [P, 2, TOK]), sb("nrm", [P, 2, TOK])
        upd, keep, top, al = sb("upd", [P, TOK]), sb("keep", [P, TOK]), sb("top", [P, TOK]), sb("al", [P, 2, TOK])

        w_in, dve_done, act_done, pe_done = sem("f_w_in"), sem("f_dve_done"), sem("f_act_done"), sem("f_pe_done")
        pool_done = sem("f_pool_done")
        block = ctx.enter_context(nc.Block())

        jobs = ([("v", h, "dve") for h in range(2)] + [(n, h, "act") for n in ("af", "as", "ir") for h in range(2)]
                + [(("nm1", j), h, "act") for j in range(2) for h in range(2)]
                + [(n, h, "dve") for n in ("k", "q") for h in range(2)]
                + [(("pw", n), h, "act") for n in range(3) for h in range(2)]
                + [("imp", h, "dve") for h in range(2)] + [("nu", h, "act") for h in range(2)]
                + [(("norm", n), h, "act") for n in range(2) for h in range(2)])
        DVE0 = 4
        taken, counts = [], {"dve": DVE0, "act": 0}
        for name, h, e in jobs:
            counts[e] += 1
            taken.append((e, counts[e]))
        at = {(name, h): taken[k] for k, (name, h, _) in enumerate(jobs)}
        JOBS_ACT = sum(e == "act" for _, _, e in jobs)
        SQUARED = DVE0 + sum(e == "dve" for _, _, e in jobs) + 2
        LAM_READY = SQUARED + 1
        LG_READY = LAM_READY + 3
        LA_READY = LG_READY + 3

        @block.sync
        def _(sp):
            for n in w:
                sp.dma_start(w[n][:, :, :], io["W" + n].rearrange("(i p) o -> p i o", p=P)).then_inc(w_in, 16)
            sp.dma_start(w_pw[:, :, :], io["pw_w"].rearrange("(i p) o -> p i o", p=P)).then_inc(w_in, 16)
            sp.dma_start(w_ir2[:, :], io["ir_w2"]).then_inc(w_in, 16)
            sp.dma_start(w_nm1[:, :], io["nm_w1"]).then_inc(w_in, 16)
            sp.dma_start(w_nm2[:, :, :], io["nm_w2"].rearrange("(i p) o -> p i o", p=P)).then_inc(w_in, 16)
            sp.dma_start(cols[:, 0:6], io["cols6"]).then_inc(w_in, 16)
            sp.dma_start(cols[:, 6:7], io["ir_b2"].partition_broadcast(P)).then_inc(w_in, 16)
            sp.dma_start(cols[:, 7:10], io["pw_b"].partition_broadcast(P)).then_inc(w_in, 16)
            sp.dma_start(cols[:, 10:12], io["lam"]).then_inc(w_in, 16)
            sp.wait_ge(w_in, 14 * 16)

        @block.gpsimd
        def _(pool):
            pool.memset(keep[:, :], 1.0).then_inc(pool_done, 1)
            pool.wait_ge(pool_done, 1)
            pool.memset(keep[:, :].rearrange("p (g t) -> p g t", t=BLK)[:, :, 0], 0.0).then_inc(pool_done, 1)
            pool.wait_ge(pool_done, 2)

        @block.tensor
        def _(pe):
            pe.wait_ge(w_in, 14 * 16)
            pe.wait_ge(dve_done, DVE0)

            def wait_for(e, n):
                pe.wait_ge({"dve": dve_done, "act": act_done}[e], n)

            for k, (name, h, _) in enumerate(jobs):
                if k >= 8:
                    wait_for(*taken[k - 8])
                b = bank[k % 8]
                half = slice(512 * h, 512 * h + 512)
                if name in w:
                    parts = [(w[name][:, i, :], t.yT[:, i, half]) for i in range(CI)]
                elif name[0] == "pw":
                    parts = [(w_pwb[:, i, name[1], :], t.yT[:, i, half]) for i in range(CI)]
                elif name[0] == "nm1":
                    wait_for(*at["v", h])
                    parts = [(w_nm1[:, name[1] * DS:(name[1] + 1) * DS], m.v[:, half])]
                elif name == "imp":
                    wait_for(*at["ir", h])
                    parts = [(w_irb[:, :], irg[:, half])]
                elif name == "nu":
                    wait_for(*at[("nm1", 1), h])
                    parts = [(w_nm2[:, j, :], h1[:, j, half]) for j in range(2)]
                else:
                    pe.wait_ge(dve_done, SQUARED)
                    parts = [(c.ones[:, :], sq[:, name[1], half])]
                for i, (lhs, rhs) in enumerate(parts):
                    ins = pe.matmul(b[:, :], lhs, rhs, start=(i == 0), stop=(i == len(parts) - 1))
                ins.then_inc(pe_done, 1)

        @block.scalar
        def _(act):
            done = Tally(act_done)
            act.wait_ge(w_in, 14 * 16)
            for k, (name, h, e) in enumerate(jobs):
                if e != "act":
                    continue
                act.wait_ge(pe_done, k + 1)
                half = slice(512 * h, 512 * h + 512)
                b = bank[k % 8][:, :]
                if name == "af":
                    ins = act.activation(la[:, 0, half], b, ACT.Sigmoid, bias=cols[:, 0:1])
                elif name == "as":
                    ins = act.activation(la[:, 1, half], b, ACT.Sigmoid, bias=cols[:, 1:2])
                elif name == "ir":
                    ins = act.activation(irg[:, half], b, ACT.Gelu, bias=cols[:, 2:3])
                elif name[0] == "nm1":
                    ins = act.activation(h1[:, name[1], half], b, ACT.Gelu, bias=cols[:, 3 + name[1]:4 + name[1]])
                elif name[0] == "pw":
                    ins = act.activation(lg[:, name[1], half], b, ACT.Identity, bias=cols[:, 7 + name[1]:8 + name[1]])
                elif name == "nu":
                    ins = act.activation(m.nu[:, half], b, ACT.Identity, bias=cols[:, 5:6])
                else:
                    ins = act.activation(nrm[:, name[1], half], b, ACT.Sqrt)
                assert done.inc(ins) == at[name, h][1]
            last = done.inc(act.activation(lam8[:, :], cols[:, 10:12], ACT.Sigmoid))
            act.wait_ge(dve_done, LAM_READY)
            done.inc(act.activation(lam8[:, :], lam8[:, :], ACT.Ln))
            act.wait_ge(dve_done, LG_READY)
            done.inc(act.activation(lg[:, :, :], lg[:, :, :], ACT.Exp))
            act.wait_ge(dve_done, LA_READY)
            done.inc(act.activation(al[:, :, :], la[:, :, :], ACT.Exp))

        @block.vector
        def _(dve):
            done = Tally(dve_done)
            dve.wait_ge(w_in, 14 * 16)
            for i in range(CI):
                for n in range(3):
                    ins = dve.tensor_scalar(w_pwb[:, i, n, :], c.ones[:, :], w_pw[:, i, n:n + 1], None, ALU.mult)
                done.inc(ins)
            done.inc(dve.tensor_scalar(w_irb[:, :], c.ones[:, :], w_ir2[:, 0:1], None, ALU.mult))
            done.inc(dve.memset(m.lx[:, :, :], 0.0))
            assert done.n == DVE0
            for k, (name, h, e) in enumerate(jobs):
                if e != "dve":
                    continue
                dve.wait_ge(pe_done, k + 1)
                half = slice(512 * h, 512 * h + 512)
                b = bank[k % 8][:, :]
                if name == "imp":
                    ins = dve.tensor_scalar(upd[:, half], b, cols[:, 6:7], 0.0, ALU.add, ALU.is_gt)
                else:
                    ins = dve.tensor_copy({"v": m.v, "k": m.k, "q": m.qh}[name][:, half], b)
                assert done.inc(ins) == at[name, h][1]
            dve.wait_ge(dve_done, done.n)
            done.inc(dve.tensor_tensor(sq[:, 0, :], m.k[:, :], m.k[:, :], ALU.mult))
            done.inc(dve.tensor_tensor(sq[:, 1, :], m.qh[:, :], m.qh[:, :], ALU.mult))
            assert done.n == SQUARED
            dve.wait_ge(act_done, JOBS_ACT + 1)
            done.inc(dve.tensor_scalar(lam8[:, :], lam8[:, :], 1e-8, None, ALU.add))
            assert done.n == LAM_READY
            dve.wait_ge(dve_done, done.inc(dve.tensor_tensor(top[:, :], lg[:, 0, :], lg[:, 1, :], ALU.max)))
            dve.wait_ge(dve_done, done.inc(dve.tensor_tensor(top[:, :], top[:, :], lg[:, 2, :], ALU.max)))
            done.inc(dve.tensor_tensor(lg[:, :, :], lg[:, :, :], top[:, :].unsqueeze(1).broadcast_to([P, 3, TOK]),
                                       ALU.subtract))
            assert done.n == LG_READY
            dve.wait_ge(act_done, JOBS_ACT + 2)
            dve.wait_ge(dve_done, done.inc(dve.tensor_scalar(lam8[:, :], lam8[:, :], DECAY, None, ALU.mult)))
            for x in range(2):
                done.inc(dve.tensor_scalar(la[:, x, :], la[:, x, :], lam8[:, x:x + 1], None, ALU.mult))
            assert done.n == LA_READY
            done.inc(dve.tensor_scalar(nrm[:, :, :], nrm[:, :, :], 1e-12, None, ALU.max))
            dve.wait_ge(dve_done, done.n)
            dve.wait_ge(dve_done, done.inc(dve.reciprocal(nrm[:, :, :], nrm[:, :, :])))
            done.inc(dve.tensor_tensor(m.k[:, :], m.k[:, :], nrm[:, 0, :], ALU.mult))
            dve.wait_ge(dve_done, done.inc(dve.tensor_tensor(m.qh[:, :], m.qh[:, :], nrm[:, 1, :], ALU.mult)))
            dve.wait_ge(pool_done, 2)
            for x in range(2):
                done.inc(dve.tensor_tensor_scan(m.lb[:, x, :], keep[:, :], la[:, x, :], 0.0, ALU.mult, ALU.add))
            dve.wait_ge(dve_done, done.n)
            lb8 = m.lb[:, :, :].rearrange("p x (g t) -> p (x g) t", t=BLK)
            lx8 = m.lx[:, :, :].rearrange("p x (g t) -> p (x g) t", t=BLK)
            done.inc(dve.tensor_copy(lx8[:, :, 1:BLK], lb8[:, :, 0:BLK - 1]))
            dve.wait_ge(act_done, JOBS_ACT + 3)
            dve.wait_ge(dve_done, done.inc(dve.tensor_tensor(top[:, :], lg[:, 0, :], lg[:, 1, :], ALU.add)))
            dve.wait_ge(dve_done, done.inc(dve.tensor_tensor(top[:, :], top[:, :], lg[:, 2, :], ALU.add)))
            dve.wait_ge(dve_done, done.inc(dve.reciprocal(top[:, :], top[:, :])))
            done.inc(dve.tensor_tensor(m.pw2[:, :], lg[:, 2, :], top[:, :], ALU.mult))
            for x in range(2):
                dve.wait_ge(dve_done, done.inc(dve.tensor_tensor(lg[:, x, :], lg[:, x, :], top[:, :], ALU.mult)))
                done.inc(dve.tensor_tensor(m.oq[:, x, :], lg[:, x, :], m.qh[:, :], ALU.mult))
            dve.wait_ge(dve_done, done.n)
            done.inc(dve.tensor_scalar(m.qh[:, :], m.qh[:, :], 0.5, None, ALU.mult))
            dve.wait_ge(act_done, JOBS_ACT + 4)
            dve.wait_ge(dve_done, done.inc(dve.tensor_scalar(al[:, :, :], al[:, :, :], -1.0, 1.0, ALU.mult, ALU.add)))
            done.inc(dve.tensor_tensor(m.u[:, :, :], al[:, :, :], m.k[:, :].unsqueeze(1).broadcast_to([P, 2, TOK]),
                                       ALU.mult))
            dve.wait_ge(dve_done, done.n)
            dve.wait_ge(dve_done, done.inc(dve.tensor_tensor(m.u[:, 1, :], m.u[:, 1, :], upd[:, :], ALU.mult)))


def factors(nc, c, m, f, bank):
    with ExitStack() as ctx:
        def sem(name):
            return ctx.enter_context(nc.semaphore(name))

        diff, exped, mult, summed, stored, pool_done = (sem("g_diff"), sem("g_exped"), sem("g_mult"), sem("g_summed"),
                                                        sem("g_stored"), sem("g_pool_done"))
        block = ctx.enter_context(nc.Block())

        def by(tensor, n):
            return tensor.rearrange("p x (g t) -> p x g t", t=n)

        lb8, lx8, u8 = by(m.lb[:, :, :], BLK), by(m.lx[:, :, :], BLK), by(m.u[:, :, :], BLK)
        lb4, lx4, u4 = by(m.lb[:, :, :], HALF), by(m.lx[:, :, :], HALF), by(m.u[:, :, :], HALF)
        k4 = m.k[:, :].rearrange("p (g t) -> p g t", t=HALF)
        q4 = m.qh[:, :].rearrange("p (g t) -> p g t", t=HALF)
        k8 = m.k[:, :].rearrange("p (g t) -> p g t", t=BLK)
        q8 = m.qh[:, :].rearrange("p (g t) -> p g t", t=BLK)
        oq4, oq8 = by(m.oq[:, :, :], HALF), by(m.oq[:, :, :], BLK)
        z = [f.z[:, x, :, :, :].rearrange("p n b t -> p b n t") for x in range(2)]
        zn = [f.zn[:, x, :, :, :].rearrange("p n b t -> p b n t") for x in range(2)]
        lbn = [m.lb[:, x, :].rearrange("p (b n t) -> p b n t", b=BATCH, n=NB) for x in range(2)]
        un = [m.u[:, x, :].rearrange("p (b n t) -> p b n t", b=BATCH, n=NB) for x in range(2)]
        G8 = TOK // BLK
        CHUNK = 512
        cp_cols = f.cp[:, :, :, :, :].rearrange("p x k i g -> p (x k i g)")
        co_cols = f.co[:, :, :, :].rearrange("p x i g -> p (x i g)")
        chunks = ([cp_cols[:, a:a + CHUNK] for a in range(0, 4 * len(PAIR_S) * GROUPS, CHUNK)]
                  + [co_cols[:, a:a + CHUNK] for a in range(0, 2 * len(PAIR_O) * GROUPS, CHUNK)])
        n_cp = 4 * len(PAIR_S) * GROUPS // CHUNK
        near = [f.near[:, x, :, :, :] for x in range(2)]

        def end(x, i):
            return lb8[:, x, :, i].unsqueeze(2).broadcast_to([P, G8, HALF])

        @block.vector
        def _(dve):
            done = Tally(diff)
            for i, (s, r) in enumerate(PAIR_S):
                ins = dve.tensor_tensor(f.cp[:, :, 0, i, :], lx4[:, :, :, r], lb4[:, :, :, s], ALU.subtract)
            done.inc(ins)
            for i, (s, r) in enumerate(PAIR_O):
                if s < r:
                    ins = dve.tensor_tensor(f.co[:, :, i, :], lb4[:, :, :, r], lb4[:, :, :, s], ALU.subtract)
                else:
                    ins = dve.memset(f.co[:, :, i, :], 0.0)
            done.inc(ins)
            for x in range(2):
                ins = dve.tensor_tensor(z[x], lbn[x][:, :, :, BLK - 1:BLK].broadcast_to([P, BATCH, NB, BLK]), lbn[x],
                                        ALU.subtract)
            done.inc(ins)
            for x in range(2):
                dve.tensor_tensor(near[x][:, KIND_K], lx8[:, x, :, HALF:BLK], end(x, HALF - 1), ALU.subtract)
                dve.tensor_tensor(near[x][:, KIND_O], lb8[:, x, :, HALF:BLK], end(x, HALF - 1), ALU.subtract)
                dve.memset(zn[x][:, :, :, HALF:BLK], 0.0)
                ins = dve.tensor_tensor(zn[x][:, :, :, 0:HALF],
                                        lbn[x][:, :, :, HALF - 1:HALF].broadcast_to([P, BATCH, NB, HALF]),
                                        lbn[x][:, :, :, 0:HALF], ALU.subtract)
            done.inc(ins)

            md = Tally(mult)
            dve.wait_ge(exped, 1)
            for i, (s, r) in enumerate(PAIR_S):
                last = md.inc(dve.tensor_tensor(f.cp[:, :, 0, i, :], f.cp[:, :, 0, i, :], u4[:, :, :, s], ALU.mult))
            dve.wait_ge(mult, last)
            for i, (s, r) in enumerate(PAIR_S):
                last = md.inc(dve.tensor_tensor(f.cp[:, :, 1, i, :], f.cp[:, :, 0, i, :],
                                                q4[:, :, r].unsqueeze(1).broadcast_to([P, 2, GROUPS]), ALU.mult))
            dve.wait_ge(mult, last)
            for i, (s, r) in enumerate(PAIR_S):
                last = md.inc(dve.tensor_tensor(f.cp[:, :, 0, i, :], f.cp[:, :, 0, i, :],
                                                k4[:, :, r].unsqueeze(1).broadcast_to([P, 2, GROUPS]), ALU.mult))
            assert last == 3 * len(PAIR_S)
            dve.wait_ge(exped, 4)
            kb = m.k[:, :].unsqueeze(1).broadcast_to([P, 2, TOK])
            qb = m.qh[:, :].unsqueeze(1).broadcast_to([P, 2, TOK])
            for x in range(2):
                last = md.inc(dve.tensor_tensor(z[x], z[x], un[x], ALU.mult))
            last = md.inc(dve.tensor_tensor(f.far[:, :, KIND_Q, :], f.far[:, :, KIND_K, :], qb, ALU.mult))
            last = md.inc(dve.tensor_tensor(f.far[:, :, KIND_O, :], f.far[:, :, KIND_O, :], m.oq[:, :, :], ALU.mult))
            dve.wait_ge(mult, last)
            last = md.inc(dve.tensor_tensor(f.far[:, :, KIND_K, :], f.far[:, :, KIND_K, :], kb, ALU.mult))
            dve.wait_ge(exped, 5)
            for x in range(2):
                last = md.inc(dve.tensor_tensor(near[x][:, KIND_Q], near[x][:, KIND_K], q8[:, :, HALF:BLK], ALU.mult))
                last = md.inc(dve.tensor_tensor(near[x][:, KIND_O], near[x][:, KIND_O], oq8[:, x, :, HALF:BLK], ALU.mult))
                last = md.inc(dve.tensor_tensor(zn[x][:, :, :, 0:HALF], zn[x][:, :, :, 0:HALF], un[x][:, :, :, 0:HALF],
                                                ALU.mult))
                dve.wait_ge(mult, last)
                last = md.inc(dve.tensor_tensor(near[x][:, KIND_K], near[x][:, KIND_K], k8[:, :, HALF:BLK], ALU.mult))
            dve.wait_ge(mult, last)

        @block.scalar
        def _(act):
            act.wait_ge(diff, 1)
            act.activation(f.cp[:, :, 0, :, :], f.cp[:, :, 0, :, :], ACT.Exp).then_inc(exped, 1)
            act.wait_ge(diff, 2)
            act.activation(f.co[:, :, :, :], f.co[:, :, :, :], ACT.Exp).then_inc(exped, 1)
            act.activation(f.far[:, :, KIND_K, :], m.lx[:, :, :], ACT.Exp)
            act.activation(f.far[:, :, KIND_O, :], m.lb[:, :, :], ACT.Exp).then_inc(exped, 1)
            act.wait_ge(diff, 3)
            act.activation(f.z[:, :, :, :, :], f.z[:, :, :, :, :], ACT.Exp).then_inc(exped, 1)
            act.activation(f.dec[:, :, :], lb8[:, :, :, BLK - 1], ACT.Exp)
            act.wait_ge(diff, 4)
            for x in range(2):
                act.activation(near[x][:, KIND_K], near[x][:, KIND_K], ACT.Exp)
                act.activation(near[x][:, KIND_O], near[x][:, KIND_O], ACT.Exp)
                ins = act.activation(zn[x][:, :, :, 0:HALF], zn[x][:, :, :, 0:HALF], ACT.Exp)
            ins.then_inc(exped, 1)
            for k, cols in enumerate(chunks):
                act.wait_ge(summed, k + 1)
                act.activation(cols, bank[k % 8][:, :], ACT.Copy).then_inc(stored, 1)

        @block.gpsimd
        def _(pool):
            done = Tally(pool_done)
            pool.wait_ge(exped, 2)
            for i, (s, r) in enumerate(PAIR_O):
                last = done.inc(pool.tensor_tensor(f.co[:, :, i, :], f.co[:, :, i, :], u4[:, :, :, s], ALU.mult))
            pool.wait_ge(pool_done, last)
            for i, (s, r) in enumerate(PAIR_O):
                last = done.inc(pool.tensor_tensor(f.co[:, :, i, :], f.co[:, :, i, :], oq4[:, :, :, r], ALU.mult))

        @block.tensor
        def _(pe):
            pe.wait_ge(mult, 3 * len(PAIR_S))
            for k, cols in enumerate(chunks):
                if k == n_cp:
                    pe.wait_ge(pool_done, 2 * len(PAIR_O))
                if k >= 8:
                    pe.wait_ge(stored, k - 7)
                pe.matmul(bank[k % 8][:, :], c.ones[:, :], cols, start=True, stop=True).then_inc(summed, 1)


def scan(nc, c, m, f, s, bank):
    acc = [bank[0:2], bank[2:4]]
    ring, errb, wtb = bank[4:6], bank[6], bank[7]
    with ExitStack() as ctx:
        def sb(name, shape):
            return ctx.enter_context(nc.sbuf_tensor(name, shape, F32))

        def sem(name):
            return ctx.enter_context(nc.semaphore(name))

        res = sb("res", [P, 2, 2, BATCH, BLK])
        w = sb("w", [P, 2, 2, BATCH, BLK])
        pred, sq = sb("pred", [P, BATCH]), sb("sqe", [P, BATCH])
        tmp1, tmp2 = sb("tmp1", [P, 4, BATCH]), sb("tmp2", [P, 4, 2, BATCH])
        tmpo = sb("tmpo", [P, 2, HALF, BATCH])

        dve_done, sq_ready, err_ready, sig_ready, w_ready = (sem("s_dve_done"), sem("s_sq_ready"), sem("s_err_ready"),
                                                             sem("s_sig_ready"), sem("s_w_ready"))
        x_done, x_out, acc_ready, acc_read = sem("s_x_done"), sem("s_x_out"), sem("s_acc_ready"), sem("s_acc_read")
        wt_ready, wt_out, z_ready, out_done, pool_done = (sem("s_wt_ready"), sem("s_wt_out"), sem("s_z_ready"),
                                                          sem("s_out_done"), sem("s_pool_done"))
        block = ctx.enter_context(nc.Block())

        v5 = m.v[:, :].rearrange("p (b n t) -> p b n t", b=BATCH, n=NB)
        sig5 = m.sig[:, :].rearrange("p (b n t) -> p b n t", b=BATCH, n=NB)
        out5 = m.out[:, :, :].rearrange("p x (b n t) -> p x b n t", b=BATCH, n=NB)
        z5 = f.z[:, :, :, :, :].rearrange("p x n b t -> p x n (b t)")
        zn5 = f.zn[:, :, :, :, :].rearrange("p x n b t -> p x n (b t)")
        far5 = f.far[:, :, :, :].rearrange("p x k (b n t) -> p x k b n t", b=BATCH, n=NB)
        near5 = f.near[:, :, :, :, :].rearrange("p x k (b n) t -> p x k b n t", b=BATCH)
        dec5 = f.dec[:, :, :].rearrange("p x (b n) -> p x b n", b=BATCH)
        cp = f.cp[:, :, :, :, :].rearrange("p x k i (b g) -> p (x k) i b g", b=BATCH)
        co = f.co[:, :, :, :].rearrange("p x i (b g) -> p x i b g", b=BATCH)
        accv = [[a[:, 0:3 * P].rearrange("p (k b t) -> p k b t", k=3, b=BATCH) for a in pair] for pair in acc]
        res4 = res[:, :, :, :, :].rearrange("p x k b t -> p (x k) b t")
        w4 = w[:, :, :, :, :].rearrange("p x k b t -> p (x k) b t")

        def items(n):
            if n == NB:
                return [[] for _ in range(BLK)]
            work = ([("cross", k, x) for k in range(n) for x in range(2)] + [("near", n, x) for x in range(2)]
                    + [("read", k, x) for k in range(n - 1) for x in range(2)])
            per = -(-len(work) // BLK)
            return [work[i * per:(i + 1) * per] for i in range(BLK)]

        def coef(n, kind, k, x):
            if kind == "cross":
                return s.cross[:, k, x, :, :, :]
            return s.near[:, n % 2, x, :, :, :]

        ring_at = {}
        for x in range(2):
            ring_at[0, "near", 0, x] = x
        for n in range(1, NB):
            for step in items(n):
                for it in step:
                    if it[0] != "read":
                        ring_at[(n,) + it] = len(ring_at)

        @block.tensor
        def _(pe):
            def product(n, kind, k, x):
                q = ring_at[n, kind, k, x]
                if q >= 2:
                    pe.wait_ge(x_out, q - 1)
                b = ring[q % 2]
                if kind == "cross":
                    pe.matmul(b[:, 0:3 * P].rearrange("p (k b t) -> p k b t", k=3, b=BATCH), z5[:, x, k, :],
                              far5[:, x, :, :, n, :], start=True, stop=True).then_inc(x_done, 1)
                else:
                    pe.matmul(b[:, 0:3 * P // 2].rearrange("p (k b t) -> p k b t", k=3, b=BATCH), zn5[:, x, n, :],
                              near5[:, x, :, :, n, :], start=True, stop=True).then_inc(x_done, 1)

            def read_far(n, k, x):
                pe.wait_ge(x_out, ring_at[n, "cross", k, x] + 1)
                if k == 0 and n >= 2:
                    pe.wait_ge(acc_read, 2 * (n - 1))
                return pe.matmul(accv[n % 2][x], s.wt[:, k, x, :], s.cross[:, k, x, :, :, :],
                                 start=(k == 0), stop=(k == n - 1), skip_group_check=True)

            def turn_w(n, h):
                pe.wait_ge(w_ready, BLK * n + HALF * (h + 1))
                if 2 * n + h >= 1:
                    pe.wait_ge(wt_out, 2 * n + h)
                for x in range(2):
                    ins = pe.transpose(wtb[:, x * P:(x + 1) * P], w[:, x, 0, :, :].rearrange("p b t -> p (b t)"),
                                       c.ident[:, :])
                ins.then_inc(wt_ready, 1)
                pe.wait_ge(wt_out, 2 * n + h + 1)

            for x in range(2):
                product(0, "near", 0, x)
            for n in range(NB):
                work = items(n + 1)
                if 1 <= n < NB - 1:
                    zwait = n
                else:
                    zwait = 0
                for t in range(BLK):
                    T = BLK * n + t
                    pe.wait_ge(sq_ready, T + 1)
                    pe.matmul(errb[:, 0:BATCH], c.ones[:, :], sq[:, :], start=True, stop=True).then_inc(err_ready, 1)
                    if t == 0 and zwait:
                        pe.wait_ge(z_ready, zwait)
                    for kind, k, x in work[t]:
                        if kind == "read":
                            read_far(n + 1, k, x)
                        else:
                            product(n + 1, kind, k, x)
                    if t == HALF - 1:
                        turn_w(n, 0)
                        pe.wait_ge(acc_read, 2 * n + 1)
                        for x in range(2):
                            pe.wait_ge(x_out, ring_at[n, "near", n, x] + 1)
                            ins = pe.matmul(accv[n % 2][x][:, :, :, HALF:BLK], s.wt[:, n, x, :],
                                            s.near[:, n % 2, x, :, :, :], start=(n == 0), stop=True,
                                            skip_group_check=True)
                        ins.then_inc(acc_ready, 1)
                    if t == BLK - 1 and n < NB - 1:
                        turn_w(n, 1)
                        for x in range(2):
                            ins = read_far(n + 1, n, x)
                        ins.then_inc(acc_ready, 1)

        @block.scalar
        def _(act):
            for n in range(NB):
                for t in range(BLK):
                    act.wait_ge(err_ready, BLK * n + t + 1)
                    act.activation(sig5[:, :, n, t], errb[:, 0:BATCH], ACT.Sigmoid, scale=1.0 / (1.0 + 1e-6)
                                   ).then_inc(sig_ready, 1)
                    if t in (HALF - 1, BLK - 1) and (n < NB - 1 or t < BLK - 1):
                        act.wait_ge(wt_ready, 2 * n + t // HALF + 1)
                        act.activation(s.wt[:, n, :, :].rearrange("p x v -> p (x v)"), wtb[:, 0:2 * P], ACT.Copy
                                       ).then_inc(wt_out, 1)

        @block.gpsimd
        def _(pool):
            done = Tally(pool_done)
            last = done.inc(pool.memset(m.out[:, :, :], 0.0))
            pool.wait_ge(pool_done, last)
            pool.sem_inc(out_done, 1)
            for n in range(NB):
                if 1 <= n < NB - 1:
                    pool.wait_ge(x_done, max(q for key, q in ring_at.items() if key[0] == n) + 1)
                    for x in range(2):
                        zb = f.z[:, x, 0:n, :, :]
                        ins = pool.tensor_tensor(zb, zb, dec5[:, x, :, n].unsqueeze(1).unsqueeze(3)
                                                 .broadcast_to([P, n, BATCH, BLK]), ALU.mult)
                        last = done.inc(ins)
                    pool.wait_ge(pool_done, last)
                    pool.sem_inc(z_ready, 1)
                for t in range(BLK):
                    h, s0 = divmod(t, HALF)
                    i0 = PAIR_O.index((s0, s0))
                    cnt = HALF - s0
                    pool.wait_ge(w_ready, BLK * n + t + 1)
                    last = done.inc(pool.tensor_tensor(
                        tmpo[:, :, 0:cnt, :], co[:, :, i0:i0 + cnt, :, 2 * n + h],
                        w[:, :, 0, :, t].unsqueeze(2).broadcast_to([P, 2, cnt, BATCH]), ALU.mult))
                    pool.wait_ge(pool_done, last)
                    o = out5[:, :, :, n, t:HALF * (h + 1)].rearrange("p x b t -> p x t b")
                    last = done.inc(pool.tensor_tensor(o, o, tmpo[:, :, 0:cnt, :], ALU.add))
                    pool.wait_ge(pool_done, last)
                    pool.sem_inc(out_done, 1)

        @block.vector
        def _(dve):
            done = Tally(dve_done)

            def then(ins):
                dve.wait_ge(dve_done, done.inc(ins))

            def store_coefs(n, kind, k, x):
                q = ring_at[n, kind, k, x]
                dve.wait_ge(x_done, q + 1)
                width = BLK if kind == "cross" else HALF
                src = ring[q % 2][:, 0:3 * BATCH * width].rearrange("p (k b t) -> p k b t", k=3, b=BATCH)
                own = c.batch_mask[:, :].unsqueeze(1).unsqueeze(3).broadcast_to([P, 3, BATCH, width])
                dve.tensor_tensor(coef(n, kind, k, x), src, own, ALU.mult).then_inc(x_out, 1)

            then(dve.memset(w[:, :, :, :, :], 0.0))
            for x in range(2):
                store_coefs(0, "near", 0, x)
            for n in range(NB):
                work = items(n + 1)
                for t in range(BLK):
                    T = BLK * n + t
                    h, r = divmod(t, HALF)
                    lo, hi = HALF * h, HALF * (h + 1)
                    if r == 0:
                        vh = v5[:, :, n, lo:hi]
                        if T == 0:
                            done.inc(dve.tensor_copy(res[:, 0, :, :, lo:hi], vh.unsqueeze(1).broadcast_to([P, 2, BATCH, HALF])))
                            done.inc(dve.tensor_copy(res[:, 1, 0, :, lo:hi], vh))
                            done.inc(dve.memset(res[:, 1, 1, :, lo:hi], 0.0))
                        else:
                            dve.wait_ge(acc_ready, 2 * n + h)
                            a = accv[n % 2]
                            done.inc(dve.tensor_tensor(res[:, 0, :, :, lo:hi], vh.unsqueeze(1).broadcast_to([P, 2, BATCH, HALF]),
                                                       a[0][:, 0:2, :, lo:hi], ALU.subtract))
                            done.inc(dve.tensor_tensor(res[:, 1, 0, :, lo:hi], vh, a[1][:, 0, :, lo:hi], ALU.subtract))
                            done.inc(dve.tensor_scalar(res[:, 1, 1, :, lo:hi], a[1][:, 1, :, lo:hi], -1.0, None, ALU.mult))
                        dve.wait_ge(dve_done, done.n)
                    else:
                        i = PAIR_S.index((r - 1, r))
                        then(dve.tensor_tensor(tmp1[:, :, :], cp[:, :, i, :, 2 * n + h], w4[:, :, :, t - 1], ALU.mult))
                        then(dve.tensor_tensor(res4[:, :, :, t], res4[:, :, :, t], tmp1[:, :, :], ALU.subtract))
                    then(dve.tensor_tensor(pred[:, :], res[:, 0, 1, :, t], res[:, 1, 1, :, t], ALU.add))
                    if T:
                        dve.wait_ge(err_ready, T)
                    dve.tensor_tensor(sq[:, :], pred[:, :], pred[:, :], ALU.mult).then_inc(sq_ready, 1)
                    if r == 0:
                        if T:
                            dve.wait_ge(out_done, 1)
                            for x in range(2):
                                done.inc(dve.tensor_copy(out5[:, x, :, n, lo:hi], accv[n % 2][x][:, KIND_O, :, lo:hi]))
                            dve.wait_ge(dve_done, done.n)
                        dve.sem_inc(acc_read, 1)
                    elif r < HALF - 1:
                        cnt = HALF - 1 - r
                        i = PAIR_S.index((r - 1, r + 1))
                        later = res4[:, :, :, t + 1:hi].rearrange("p c b t -> p c t b")
                        then(dve.tensor_tensor(tmp2[:, :, 0:cnt, :], cp[:, :, i:i + cnt, :, 2 * n + h],
                                               w4[:, :, :, t - 1].unsqueeze(2).broadcast_to([P, 4, cnt, BATCH]), ALU.mult))
                        done.inc(dve.tensor_tensor(later, later, tmp2[:, :, 0:cnt, :], ALU.subtract))
                    for it in work[t]:
                        if it[0] != "read":
                            store_coefs(n + 1, *it)
                    dve.wait_ge(sig_ready, T + 1)
                    dve.wait_ge(dve_done, done.n)
                    if T >= BLK:
                        dve.wait_ge(out_done, T - BLK + 2)
                    ins = dve.tensor_tensor(w[:, :, :, :, t], res[:, :, 0, :, t].unsqueeze(2).broadcast_to([P, 2, 2, BATCH]),
                                            sig5[:, :, n, t].unsqueeze(1).unsqueeze(1).broadcast_to([P, 2, 2, BATCH]), ALU.mult)
                    ins.then_inc(w_ready, 1)
                    dve.wait_ge(w_ready, T + 1)


def memory_output(nc, io, c, t, m, bank):
    with ExitStack() as ctx:
        def sem(name):
            return ctx.enter_context(nc.semaphore(name))

        wo = ctx.enter_context(nc.sbuf_tensor("wo", [P, DM], F32))
        nw = ctx.enter_context(nc.sbuf_tensor("nw", [P, 1], F32))
        tmp = ctx.enter_context(nc.sbuf_tensor("mo_tmp", [P, TOK], F32))
        keep = ctx.enter_context(nc.sbuf_tensor("mo_keep", [P, TOK], F32))
        w_in, dve_done, sq_ready, summed, rooted = (sem("o_w_in"), sem("o_dve_done"), sem("o_sq_ready"), sem("o_summed"),
                                                    sem("o_rooted"))
        normed, projected, var_ready, std_ready = sem("o_normed"), sem("o_projected"), sem("o_var_ready"), sem("o_std_ready")
        y_ready, turned, moved = sem("o_y_ready"), sem("o_turned"), sem("o_moved")
        block = ctx.enter_context(nc.Block())

        @block.sync
        def _(sp):
            sp.dma_start(wo[:, :], io["Wo"]).then_inc(w_in, 16)
            sp.dma_start(nw[:, :], io["norm_w"]).then_inc(w_in, 16)
            sp.wait_ge(w_in, 32)

        @block.vector
        def _(dve):
            done = Tally(dve_done)

            def then(ins):
                dve.wait_ge(dve_done, done.inc(ins))

            then(dve.tensor_scalar(tmp[:, :], m.sig[:, :], 0.7, 0.1, ALU.is_gt, ALU.mult))
            then(dve.tensor_scalar(keep[:, :], tmp[:, :], -1.0, 1.0, ALU.mult, ALU.add))
            then(dve.memset(keep[:, :].rearrange("p (b t) -> p b t", t=STEPS)[:, :, 0], 0.0))
            then(dve.tensor_tensor(m.nu[:, :], m.nu[:, :], tmp[:, :], ALU.mult))
            then(dve.tensor_tensor_scan(tmp[:, :], keep[:, :], m.nu[:, :], 0.0, ALU.mult, ALU.add))
            then(dve.tensor_tensor(tmp[:, :], tmp[:, :], m.pw2[:, :], ALU.mult))
            then(dve.tensor_tensor(tmp[:, :], tmp[:, :], m.out[:, 0, :], ALU.add))
            then(dve.tensor_tensor(tmp[:, :], tmp[:, :], m.out[:, 1, :], ALU.add))
            dve.tensor_tensor(m.sig[:, :], tmp[:, :], tmp[:, :], ALU.mult).then_inc(sq_ready, 1)
            dve.wait_ge(w_in, 32)
            for h in range(2):
                dve.wait_ge(summed, h + 1)
                done.inc(dve.tensor_scalar(keep[:, 512 * h:512 * h + 512], bank[h][:, :], 1.0 / DS, 1e-6, ALU.mult, ALU.add))
            dve.wait_ge(dve_done, done.n)
            dve.sem_inc(sq_ready, 1)
            dve.wait_ge(rooted, 1)
            then(dve.reciprocal(keep[:, :], keep[:, :]))
            dve.scalar_tensor_tensor(out=tmp[:, :], in0=tmp[:, :], scalar=nw[:, 0:1], in1=keep[:, :],
                                     op0=ALU.mult, op1=ALU.mult).then_inc(normed, 1)
            for n in range(TILES):
                dve.wait_ge(projected, n + 1)
                last = done.inc(dve.tensor_tensor(t.x[:, n, :], bank[n][:, 0:DM], t.x[:, n, :], ALU.add))
            dve.wait_ge(dve_done, last)
            last = row_stats(dve, t, t.x, done)
            dve.wait_ge(dve_done, last)
            dve.sem_inc(var_ready, 1)
            dve.wait_ge(std_ready, 1)
            last = normalise(dve, t, t.y, t.x, done)
            dve.wait_ge(dve_done, last)
            dve.sem_inc(y_ready, 1)
            for n in range(TILES):
                dve.wait_ge(turned, n + 1)
                dve.tensor_copy(t.yT[:, :, n * P:(n + 1) * P],
                                bank[n][:, 0:DM].rearrange("p (j q) -> p j q", j=CI)).then_inc(moved, 1)

        @block.scalar
        def _(act):
            act.wait_ge(sq_ready, 2)
            act.activation(keep[:, :], keep[:, :], ACT.Sqrt).then_inc(rooted, 1)
            act.wait_ge(var_ready, 1)
            act.activation(t.std[:, :], t.var[:, :], ACT.Sqrt).then_inc(std_ready, 1)

        @block.tensor
        def _(pe):
            pe.wait_ge(sq_ready, 1)
            for h in range(2):
                pe.matmul(bank[h][:, :], c.ones[:, :], m.sig[:, 512 * h:512 * h + 512], start=True, stop=True
                          ).then_inc(summed, 1)
            pe.wait_ge(w_in, 32)
            pe.wait_ge(normed, 1)
            for n in range(TILES):
                pe.matmul(bank[n][:, 0:DM], tmp[:, n * P:(n + 1) * P], wo[:, :], start=True, stop=True).then_inc(projected, 1)
            pe.wait_ge(y_ready, 1)
            for n in range(TILES):
                for i in range(CI):
                    ins = pe.transpose(bank[n][:, i * P:(i + 1) * P], t.y[:, n, i * P:(i + 1) * P], c.ident[:, :])
                ins.then_inc(turned, 1)


EXPERTS, EW, TOPK = 64, 96, 8
UNITS = 2


def route(nc, io, c, t, cw_rows, bank):
    with ExitStack() as ctx:
        def sb(name, shape):
            return ctx.enter_context(nc.sbuf_tensor(name, shape, F32))

        def sem(name):
            return ctx.enter_context(nc.semaphore(name))

        rw, prob, rest = sb("rw", [P, CI, EXPERTS]), sb("r_prob", [P, TILES, EXPERTS]), sb("r_rest", [P, TILES, EXPERTS])
        top, cwT = sb("r_top", [P, TILES, TOPK]), sb("cwT", [EXPERTS, TOK])
        neg, den, sum8 = sb("r_neg", [P, TILES]), sb("r_den", [P, TILES]), sb("r_sum8", [P, TILES])
        w_in, routed, neg_ready, exped, dve_done = sem("r_w_in"), sem("r_routed"), sem("r_neg_ready"), sem("r_exped"), sem("r_dve_done")
        chosen, turned, moved, stored = sem("r_chosen"), sem("r_turned"), sem("r_moved"), sem("r_stored")
        block = ctx.enter_context(nc.Block())

        @block.sync
        def _(sp):
            sp.dma_start(rw[:, :, :], io["routerT"].rearrange("(i p) e -> p i e", p=P)).then_inc(w_in, 16)
            sp.wait_ge(moved, 2)
            sp.dma_start(cw_rows, cwT[:, :]).then_inc(stored, 16)
            sp.wait_ge(stored, 16)

        @block.tensor
        def _(pe):
            pe.wait_ge(w_in, 16)
            for n in range(TILES):
                for i in range(CI):
                    ins = pe.matmul(bank[n][:, 0:EXPERTS], t.yT[:, i, n * P:(n + 1) * P], rw[:, i, :],
                                    start=(i == 0), stop=(i == CI - 1))
                ins.then_inc(routed, 1)
            pe.wait_ge(chosen, 1)
            for n in range(TILES):
                ins = pe.transpose(bank[n // 4][0:EXPERTS, (n % 4) * P:(n % 4 + 1) * P], prob[:, n, :], c.ident[:, :])
                if n % 4 == 3:
                    ins.then_inc(turned, 1)

        @block.scalar
        def _(act):
            for n in range(TILES):
                act.wait_ge(neg_ready, n + 1)
                act.activation(prob[:, n, :], bank[n][:, 0:EXPERTS], ACT.Exp, bias=neg[:, n:n + 1],
                               accum_out=den[:, n:n + 1]).then_inc(exped, 1)

        @block.vector
        def _(dve):
            done = Tally(dve_done)

            def then(ins):
                dve.wait_ge(dve_done, done.inc(ins))

            for n in range(TILES):
                dve.wait_ge(routed, n + 1)
                dve.tensor_reduce(neg[:, n:n + 1], bank[n][:, 0:EXPERTS], AX.X, ALU.max, negate=True).then_inc(neg_ready, 1)
            dve.wait_ge(exped, TILES)
            then(dve.reciprocal(den[:, :], den[:, :]))
            for n in range(TILES):
                done.inc(dve.tensor_scalar(prob[:, n, :], prob[:, n, :], den[:, n:n + 1], None, ALU.mult))
            dve.wait_ge(dve_done, done.n)
            for n in range(TILES):
                done.inc(dve.max(top[:, n, :], prob[:, n, :]))
            dve.wait_ge(dve_done, done.n)
            for n in range(TILES):
                done.inc(dve.match_replace(rest[:, n, :], top[:, n, :], prob[:, n, :], 0.0))
            dve.wait_ge(dve_done, done.n)
            done.inc(dve.tensor_tensor(prob[:, :, :], prob[:, :, :], rest[:, :, :], ALU.subtract))
            then(dve.tensor_reduce(sum8[:, :], top[:, :, :], AX.X, ALU.add))
            then(dve.reciprocal(sum8[:, :], sum8[:, :]))
            for n in range(TILES):
                done.inc(dve.tensor_scalar(prob[:, n, :], prob[:, n, :], sum8[:, n:n + 1], None, ALU.mult))
            dve.wait_ge(dve_done, done.n)
            dve.sem_inc(chosen, 1)
            for k in range(2):
                dve.wait_ge(turned, k + 1)
                dve.tensor_copy(cwT[:, 512 * k:512 * k + 512], bank[k][0:EXPERTS, :]).then_inc(moved, 1)


def experts(nc, io, c, t, cw_rows, bank):
    acc = bank[0:4]
    gate, up = bank[4:6], bank[6:8]
    WS, XS, HS = 64.0, 64.0, 16.0
    with ExitStack() as ctx:
        def sb(name, shape, dt=F32):
            return ctx.enter_context(nc.sbuf_tensor(name, shape, dt))

        def sem(name):
            return ctx.enter_context(nc.semaphore(name))

        wgu = [sb(f"wgu{u}", [P, CI, 2, EW]) for u in range(2)]
        wd = [sb(f"wd{u}", [EW, DM]) for u in range(2)]
        wgu_hl = [[sb(f"wgu{part}{u}", [P, CI, 2, EW], F16) for part in "hl"] for u in range(2)]
        wd_hl = [[sb(f"wd{part}{u}", [EW, DM], F16) for part in "hl"] for u in range(2)]
        x_hl = [sb(f"xT{part}", [P, CI, TOK], F16) for part in "hl"]
        cw = [sb(f"cw{u}", [EW, TOK]) for u in range(2)]
        silu = [sb(f"silu{h}", [EW, 512]) for h in range(2)]
        upw = [sb(f"upw{h}", [EW, 512]) for h in range(2)]
        hid = [sb(f"hid{h}", [EW, 512]) for h in range(2)]
        hid_hl = [[sb(f"hid{part}{h}", [EW, 512], F16) for part in "hl"] for h in range(2)]
        zeros = sb("zeros", [P, P], F16)
        w_in, cw_in = [sem(f"e_w_in{u}") for u in range(2)], [sem(f"e_cw_in{u}") for u in range(2)]
        zeroed, gated, upped, silued, weighted, hid_ready = (sem("e_zeroed"), sem("e_gated"), sem("e_upped"), sem("e_silued"),
                                                             sem("e_weighted"), sem("e_hid_ready"))
        x_high, x_low, w_high, w_low, hid_high, hid_low = (sem("e_x_high"), sem("e_x_low"), sem("e_w_high"), sem("e_w_low"),
                                                           sem("e_hid_high"), sem("e_hid_low"))
        down_done, out_ready, out_sent = sem("e_down_done"), sem("e_out_ready"), sem("e_out_sent")
        block = ctx.enter_context(nc.Block())

        def load(sp, e, u):
            one = bass.ds(e, 1)
            sp.dma_start(wgu[u][:, :, :, :], io["guT"][one].rearrange("o p i g w -> p (o i) g w")).then_inc(w_in[u], 16)
            sp.dma_start(wd[u][:, :], io["downT"][one].rearrange("o w d -> (o w) d")).then_inc(w_in[u], 16)
            sp.dma_start(cw[u][:, :], cw_rows[one, :].broadcast_to([EW, TOK])).then_inc(cw_in[u], 16)

        @block.sync
        def _(sp):
            load(sp, 0, 0)
            load(sp, 1, 1)
            with sp.Fori(0, EXPERTS // 2 - 1) as i:
                for u in range(2):
                    sp.wait_ge(w_low, 4 * i + 2 * u + 2)
                    sp.wait_ge(weighted, 4 * i + 2 * u + 2)
                    load(sp, 2 * i + u + 2, u)
            for n in range(TILES // 2):
                sp.wait_ge(out_ready, 2 * n + 2)
                sp.dma_start(io["out"].rearrange("b t d -> (b t) d").rearrange("(n p) d -> p n d", p=P)[:, 2 * n:2 * n + 2, :],
                             t.x[:, 2 * n:2 * n + 2, :]).then_inc(out_sent, 16)
            sp.wait_ge(out_sent, 16 * TILES // 2)

        @block.gpsimd
        def _(pool):
            pool.memset(zeros[:, :], 0.0).then_inc(zeroed, 1)

        @block.tensor
        def _(pe):
            def gate_up(q, r, first=False):
                u, h = (r // 2) % 2, r % 2
                if h == 0:
                    pe.wait_ge(w_low, q + 2)
                if not first:
                    pe.wait_ge(hid_ready, q - 1)
                cols = slice(512 * h, 512 * h + 512)
                for g, (dst, done) in enumerate(((gate[h], gated), (up[h], upped))):
                    terms = [(a, b, i) for a, b in ((0, 0), (0, 1), (1, 0)) for i in range(CI)]
                    for k, (a, b, i) in enumerate(terms):
                        ins = pe.matmul(dst[0:EW, :], wgu_hl[u][a][:, i, g, :], x_hl[b][:, i, cols],
                                        start=(k == 0), stop=(k == len(terms) - 1))
                    ins.then_inc(done, 1)

            def down(q, r):
                u, h = (r // 2) % 2, r % 2
                pe.wait_ge(hid_low, q + 1)
                for k in range(4):
                    n = 4 * h + k
                    for a, b in ((0, 0), (0, 1), (1, 0)):
                        ins = pe.matmul(acc[n // 2][:, (n % 2) * DM:(n % 2 + 1) * DM], hid_hl[h][a][:, k * P:(k + 1) * P],
                                        wd_hl[u][b][:, :], start=False, stop=True, skip_group_check=True)
                ins.then_inc(down_done, 1)

            pe.wait_ge(zeroed, 1)
            pe.wait_ge(x_low, 1)
            for a in acc:
                pe.matmul(a[:, :], zeros[:, :], x_hl[0][:, 0, 0:512], start=True, stop=True)
            gate_up(0, 0, True)
            gate_up(1, 1, True)
            down(0, 0)
            with pe.Fori(0, EXPERTS // 2 - 1) as i:
                for r in range(4):
                    gate_up(4 * i + r + 2, r + 2)
                    down(4 * i + r + 1, r + 1)
            last = 2 * EXPERTS - 4
            for r in range(2):
                gate_up(last + r + 2, r + 2)
                down(last + r + 1, r + 1)
            down(last + 3, 3)

        @block.scalar
        def _(act):
            def split_weights(e, u, loads, first):
                act.wait_ge(w_in[u], 32 * loads)
                if not first:
                    act.wait_ge(down_done, 2 * e - 2)
                act.activation(wgu_hl[u][0][:, :, :, :], wgu[u][:, :, :, :], ACT.Copy, scale=WS).then_inc(w_high, 1)
                act.activation(wd_hl[u][0][:, :], wd[u][:, :], ACT.Copy, scale=WS).then_inc(w_high, 1)

            def unit(q, r, first=False):
                h = r % 2
                act.wait_ge(gated, q + 1)
                if not first:
                    act.wait_ge(hid_ready, q - 1)
                act.activation(silu[h][:, :], gate[h][0:EW, :], ACT.Silu, scale=1.0 / (WS * XS)).then_inc(silued, 1)
                act.wait_ge(hid_ready, q + 1)
                if not first:
                    act.wait_ge(down_done, q - 1)
                act.activation(hid_hl[h][0][:, :], hid[h][:, :], ACT.Copy).then_inc(hid_high, 1)

            act.activation(x_hl[0][:, :, :], t.yT[:, :, :], ACT.Copy, scale=XS).then_inc(x_high, 1)
            split_weights(0, 0, 1, True)
            split_weights(1, 1, 1, True)
            for r in range(2):
                unit(r, r, True)
            with act.Fori(0, EXPERTS // 2 - 1) as i:
                for u in range(2):
                    unit(4 * i + 2 * u + 2, 2)
                    split_weights(2 * i + 2 + u, u, i + 2, False)
                    unit(4 * i + 2 * u + 3, 3)
            for r in range(2, 4):
                unit(2 * EXPERTS - 4 + r, r)

        @block.vector
        def _(dve):
            def split_weights(e, u):
                for k, (w, hl) in enumerate(((wgu, wgu_hl), (wd, wd_hl))):
                    dve.wait_ge(w_high, 2 * e + k + 1)
                    if k == 0:
                        src, high, low = w[u][:, :, :, :], hl[u][0][:, :, :, :], hl[u][1][:, :, :, :]
                        src, high, low = (a.rearrange("p i g w -> p (i g w)") for a in (src, high, low))
                    else:
                        src, high, low = w[u][:, :], hl[u][0][:, :], hl[u][1][:, :]
                    dve.scalar_tensor_tensor(out=low, in0=src, scalar=WS, in1=high, op0=ALU.mult,
                                             op1=ALU.subtract).then_inc(w_low, 1)

            def unit(q, r, loads, first=False):
                u, h = (r // 2) % 2, r % 2
                if h == 0:
                    dve.wait_ge(cw_in[u], 16 * loads)
                dve.wait_ge(upped, q + 1)
                if not first:
                    dve.wait_ge(hid_ready, q - 1)
                dve.scalar_tensor_tensor(out=upw[h][:, :], in0=up[h][0:EW, :], scalar=HS / (WS * XS),
                                         in1=cw[u][:, 512 * h:512 * h + 512], op0=ALU.mult, op1=ALU.mult
                                         ).then_inc(weighted, 1)
                dve.wait_ge(weighted, q + 1)
                dve.wait_ge(silued, q + 1)
                if not first:
                    dve.wait_ge(hid_low, q - 1)
                dve.tensor_tensor(hid[h][:, :], upw[h][:, :], silu[h][:, :], ALU.mult).then_inc(hid_ready, 1)

            def low(q, r):
                h = r % 2
                dve.wait_ge(hid_high, q + 1)
                dve.tensor_tensor(hid_hl[h][1][:, :], hid[h][:, :], hid_hl[h][0][:, :], ALU.subtract).then_inc(hid_low, 1)

            dve.wait_ge(x_high, 1)
            dve.scalar_tensor_tensor(out=x_hl[1][:, :, :].rearrange("p i n -> p (i n)"),
                                     in0=t.yT[:, :, :].rearrange("p i n -> p (i n)"), scalar=XS,
                                     in1=x_hl[0][:, :, :].rearrange("p i n -> p (i n)"), op0=ALU.mult, op1=ALU.subtract
                                     ).then_inc(x_low, 1)
            split_weights(0, 0)
            split_weights(1, 1)
            for r in range(2):
                unit(r, r, 1, True)
                low(r, r)
            with dve.Fori(0, EXPERTS // 2 - 1) as i:
                for u in range(2):
                    q = 4 * i + 2 * u + 2
                    unit(q, 2 + 2 * u, i + 1 + u)
                    low(q, 0)
                    split_weights(2 * i + 2 + u, u)
                    unit(q + 1, 3 + 2 * u, i + 1 + u)
                    low(q + 1, 1)
            for r in range(2, 4):
                unit(2 * EXPERTS - 4 + r, r, EXPERTS // 2)
                low(2 * EXPERTS - 4 + r, r)
            dve.wait_ge(down_done, 2 * EXPERTS)
            for n in range(TILES):
                dve.scalar_tensor_tensor(out=t.x[:, n, :], in0=acc[n // 2][:, (n % 2) * DM:(n % 2 + 1) * DM],
                                         scalar=1.0 / (WS * HS), in1=t.x[:, n, :], op0=ALU.mult, op1=ALU.add
                                         ).then_inc(out_ready, 1)


def store_rows(nc, src, dst):
    with nc.semaphore("st_out") as st_out, nc.Block() as block:
        @block.sync
        def _(sp):
            sp.dma_start(dst.rearrange("b t d -> (b t) d").rearrange("(n p) d -> p n d", p=P), src[:, :, :]
                         ).then_inc(st_out, 16)
            sp.wait_ge(st_out, 16)


def perceiver_layer(nc, io, upto=9):
    with ExitStack() as ctx:
        def sb(name, shape):
            return ctx.enter_context(nc.sbuf_tensor(name, shape, F32))

        bank = [ctx.enter_context(nc.psum_tensor(f"bank{n}", [P, 512], F32)) for n in range(8)]
        t = Named()
        t.x = sb("x", [P, TILES, DM])
        t.y = sb("y", [P, TILES, DM])
        t.yT = sb("yT", [P, CI, TOK])
        t.stat = sb("stat", [P, TILES, 6])
        t.mv = sb("mv", [P, TILES, 2])
        t.var = sb("var", [P, TILES])
        t.std = sb("std", [P, TILES])
        t.rstd = sb("rstd", [P, TILES])
        t.amax = sb("amax", [P, TILES])
        t.qs = sb("qs", [P, TILES])
        t.qr = sb("qr", [P, TILES])
        c = Named()
        c.ident = sb("ident", [P, P])
        c.ones = sb("ones", [P, P])
        c.batch_mask = sb("batch_mask", [P, BATCH])
        with ExitStack() as xa:
            def xb(name, shape):
                return xa.enter_context(nc.sbuf_tensor(name, shape, F32))
            c.head_mask = xb("head_mask", [P, HG])
            c.pair_mask = xb("pair_mask", [P, 2, DH])
            c.gather = xb("gather", [P, 3 * STEPS])
            c.wkvT = xb("wkvT", [P, CI, 2 * DM])
            c.wqT = xb("wqT", [P, CI, DM])
            c.wpT = xb("wpT", [P, CI, DM])
            c.qT = xb("qT", [P, CI, TOK])
            c.bq, c.bk = xb("bq", [P, CI]), xb("bk", [P, CI])
            c.bv, c.bp = xb("bv", [P, DM]), xb("bp", [P, DM])
            t.o = xb("o", [P, BATCH, PAIRS, 2 * DH])
            with ExitStack() as wa:
                t.wq = wa.enter_context(nc.sbuf_tensor("wq", [P, CI, DM], F32))
                t.wp = wa.enter_context(nc.sbuf_tensor("wp", [P, CI, DM], F32))
                queries(nc, io, c, t, bank)
            attention(nc, io, c, t, bank)
            project_attention(nc, io, c, t, bank)
        if upto == 3:
            store_rows(nc, t.x, io["out"])
            return
        with ExitStack() as me:
            def mb(name, shape):
                return me.enter_context(nc.sbuf_tensor(name, shape, F32))
            m = Named()
            m.v = mb("v", [P, TOK])
            m.nu = mb("nu", [P, TOK])
            m.sig = mb("sig", [P, TOK])
            m.pw2 = mb("pw2", [P, TOK])
            m.out = mb("out", [P, 2, TOK])
            with ExitStack() as sc:
                room = sc.enter_context(nc.sbuf_tensor("room", [P, 10 * TOK], F32))
                place = 0

                def carve(pattern, size, **dims):
                    nonlocal place
                    place += size
                    return room[:, place - size:place].rearrange(pattern, **dims)

                m.k, m.qh = carve("p (a t) -> p (a t)", TOK, a=1), carve("p (a t) -> p (a t)", TOK, a=1)
                m.oq, m.lb, m.lx, m.u = [carve("p (x t) -> p x t", 2 * TOK, x=2) for _ in range(4)]
                features(nc, io, c, t, m, bank)

                def fb(name, shape):
                    return sc.enter_context(nc.sbuf_tensor(name, shape, F32))
                f = Named()
                f.cp = fb("cp", [P, 2, 2, len(PAIR_S), GROUPS])
                f.co = fb("co", [P, 2, len(PAIR_O), GROUPS])
                f.far = fb("far", [P, 2, 3, TOK])
                f.near = fb("near", [P, 2, 3, TOK // BLK, HALF])
                f.z = fb("z", [P, 2, NB, BATCH, BLK])
                f.zn = fb("zn", [P, 2, NB, BATCH, BLK])
                f.dec = fb("dec", [P, 2, TOK // BLK])
                factors(nc, c, m, f, bank)
                place = 0
                s = Named()
                s.cross = carve("p (k x i b t) -> p k x i b t", (NB - 1) * 2 * 3 * P, k=NB - 1, x=2, i=3, b=BATCH)
                s.wt = carve("p (k x v) -> p k x v", NB * 2 * P, k=NB, x=2)
                s.near = carve("p (u x i b t) -> p u x i b t", 2 * 2 * 3 * P // 2, u=2, x=2, i=3, b=BATCH)
                scan(nc, c, m, f, s, bank)
            memory_output(nc, io, c, t, m, bank)
        if upto == 7:
            store_rows(nc, t.x, io["out"])
            return
        cw_rows = nc.dram_tensor("cw_rows", [EXPERTS, TOK], F32, kind="Internal").ap()
        route(nc, io, c, t, cw_rows, bank)
        experts(nc, io, c, t, cw_rows, bank)


def layout(inputs):
    import numpy as np
    a = {k: np.asarray(v) for k, v in inputs.items()}
    X, A, F = "L0_xattn_", "L0_attn_", "L0_ffn_"
    return {
        "x": a["x"],
        "ctxT": a["ctx_2048"].transpose(0, 2, 1),
        "wq": a[X + "wq"], "wp": a[X + "wp"],
        "wkvT": a[X + "wkv"].T,
        "bqT": a[X + "bq"].reshape(CI, P).T,
        "bkvT": a[X + "bkv"][:DM].reshape(CI, P).T,
        "bv": a[X + "bkv"][DM:], "bp": a[X + "bp"],
        "Wk": a[A + "Wk"], "Wv": a[A + "Wv"], "Wq": a[A + "Wq"], "Waf": a[A + "Waf"], "Was": a[A + "Was"],
        "Wir": a[A + "ir_w1"], "ir_w2": a[A + "ir_w2"], "ir_b2": a[A + "ir_b2"],
        "pw_w": a[A + "pw_w"], "pw_b": a[A + "pw_b"], "nm_w1": a[A + "nm_w1"], "nm_w2": a[A + "nm_w2"],
        "cols6": np.stack([a[A + "baf"], a[A + "bas"], a[A + "ir_b1"], *a[A + "nm_b1"].reshape(2, P), a[A + "nm_b2"]], 1),
        "lam": np.stack([a[A + "fast_lambda"], a[A + "slow_lambda"]], 1),
        "Wo": a[A + "Wo"], "norm_w": a[A + "norm_w"].reshape(P, 1),
        "routerT": a[F + "router_w"].T,
        "guT": np.stack([a[F + n].transpose(0, 2, 1).reshape(EXPERTS, CI, P, EW) for n in ("gate_w", "up_w")], 3)
        .transpose(0, 2, 1, 3, 4),
        "downT": a[F + "down_w"].transpose(0, 2, 1),
    }


def kernel(**inputs):
    import numpy as np
    import concourse.bacc as bacc
    from concourse.bass_utils import run_bass_kernel_spmd

    nc = bacc.Bacc("TRN2", target_bir_lowering=False, num_devices=1)
    arrays, io = {}, {}
    for name, a in layout(inputs).items():
        a = np.ascontiguousarray(a)
        arrays[f"in_{name}_dram"] = a
        io[name] = nc.dram_tensor(f"in_{name}_dram", a.shape, mybir.dt.from_np(a.dtype), kind="ExternalInput").ap()
    io["out"] = nc.dram_tensor("out_0_dram", (BATCH, STEPS, DM), F32, kind="ExternalOutput").ap()
    perceiver_layer(nc, io)
    r = run_bass_kernel_spmd(nc, [arrays], core_ids=[0])
    return r.results[0]["out_0_dram"]
```

```python
from contextlib import ExitStack

import concourse.bass as bass
from concourse import mybir

F32 = mybir.dt.float32
F16 = mybir.dt.float16
ACT = mybir.ActivationFunctionType
ALU = mybir.AluOpType
AX = mybir.AxisListType

P = 128
BATCH, STEPS, DM = 16, 64, 256
CTX = 1601
HEADS, DH = 16, 16
TOK = BATCH * STEPS
TILES = TOK // P
CI = DM // P
HG = P // DH
PAIRS = HEADS // 2
NCH = 4
COLS = [(n * 3 * P, 3 * P if n < NCH - 1 else CTX - n * 3 * P) for n in range(NCH)]
ROWS = [(m, min(P, CTX - m)) for m in range(0, CTX, P)]
KROW = len(ROWS)
KGROUPS = CI * NCH
VTILES = [(m, 2 if m + 1 < KROW and ROWS[m + 1][1] == P else 1) for m in range(0, KROW, 2)]
PROJ = KGROUPS + len(VTILES)
TURNS = [[(m, rows) for m, rows in ROWS if c0 <= m < c0 + w] for c0, w in COLS]
TBLOCKS = max(len(turns) for turns in TURNS)
ROUND = 12582912.0
EPS_LN = 1e-5
SPLIT, Q_SPLIT = 64.0, 4.0
P_LOG = 6.931471805599453
assert PROJ == 2 * PAIRS - 1


class Named:
    pass


class Tally:

    def __init__(self, sem):
        self.sem, self.n = sem, 0

    def inc(self, ins, by=1):
        ins.then_inc(self.sem, by)
        self.n += by
        return self.n


def row_stats(dve, t, src, done):
    for n in range(TILES):
        last = done.inc(dve.bn_stats(t.stat[:, n, :], src[:, n, :]))
    dve.wait_ge(done.sem, last)
    for n in range(TILES):
        last = done.inc(dve.bn_aggr(t.mv[:, n, :], t.stat[:, n, :]))
    dve.wait_ge(done.sem, last)
    return done.inc(dve.tensor_scalar(t.var[:, :], t.mv[:, :, 1], EPS_LN, None, ALU.add))


def normalise(dve, t, dst, src, done):
    last = done.inc(dve.reciprocal(t.rstd[:, :], t.std[:, :]))
    dve.wait_ge(done.sem, last)
    for n in range(TILES):
        last = done.inc(dve.tensor_scalar(dst[:, n, :], src[:, n, :], t.mv[:, n, 0:1], t.rstd[:, n:n + 1],
                                          ALU.subtract, ALU.mult))
    return last


def fake_quantise(dve, t, dst, src, n, done):
    last = done.inc(dve.tensor_reduce(t.amax[:, 0:n], src[:, :, :], AX.X, ALU.max, apply_absolute_value=True))
    dve.wait_ge(done.sem, last)
    last = done.inc(dve.tensor_scalar(t.qs[:, 0:n], t.amax[:, 0:n], 1.0 / 127.0, 1e-8, ALU.mult, ALU.max))
    dve.wait_ge(done.sem, last)
    last = done.inc(dve.reciprocal(t.qr[:, 0:n], t.qs[:, 0:n]))
    dve.wait_ge(done.sem, last)
    for k in range(n):
        last = done.inc(dve.tensor_scalar(src[:, k, :], src[:, k, :], t.qr[:, k:k + 1], ROUND, ALU.mult, ALU.add))
    dve.wait_ge(done.sem, last)
    last = done.inc(dve.tensor_scalar(src[:, :, :], src[:, :, :], ROUND, -127.0, ALU.subtract, ALU.max))
    dve.wait_ge(done.sem, last)
    for k in range(n):
        last = done.inc(dve.tensor_scalar(dst[:, k, :], src[:, k, :], 127.0, t.qs[:, k:k + 1], ALU.min, ALU.mult))
    return last


def queries(nc, io, c, t, bank):
    with ExitStack() as ctx:
        def sem(name):
            return ctx.enter_context(nc.semaphore(name))

        x_in, w_in, b_in = sem("q_x_in"), sem("q_w_in"), sem("q_b_in")
        pool_done, dve_done = sem("q_pool_done"), sem("q_dve_done")
        std_ready, turned, moved, wq_moved = (sem("q_std_ready"), sem("q_turned"), sem("q_moved"),
                                              sem("q_weights_moved"))
        w_turned, q_ready = sem("q_w_turned"), sem("q_ready")
        consts_ready = sem("q_consts_ready")
        var_ready, wquant, xquant = sem("q_var_ready"), sem("q_wquant"), sem("q_xquant")
        q_moved = sem("q_moved_out")
        block = ctx.enter_context(nc.Block())

        @block.sync
        def _(sp):
            sp.dma_start(t.x[:, :, :], io["x"].rearrange("b t d -> (b t) d")
                         .rearrange("(n p) d -> p n d", p=P)).then_inc(x_in, 16)
            for w, dst in ((io["wq"], t.wq), (io["wp"], t.wp)):
                sp.dma_start(dst[:, :, :], w.rearrange("(j p) i -> p j i", p=P)).then_inc(w_in, 16)
            sp.dma_start(t.wkvT[:, :, :], io["wkvT"].rearrange("(j p) o -> p j o", p=P)).then_inc(b_in, 16)
            sp.dma_start(c.bk[:, :], io["bkvT"]).then_inc(b_in, 16)
            sp.dma_start(c.bq[:, :], io["bqT"]).then_inc(b_in, 16)
            sp.dma_start(c.bv[:, :], io["bv"].partition_broadcast(P)).then_inc(b_in, 16)
            sp.dma_start(c.bp[:, :], io["bp"].partition_broadcast(P)).then_inc(b_in, 16)
            sp.wait_ge(b_in, 80)

        @block.gpsimd
        def _(pool):
            done = Tally(pool_done)
            done.inc(pool.memset(c.ident[:, :], 0.0))
            done.inc(pool.memset(c.head_mask[:, :], 1.0))
            done.inc(pool.memset(c.pair_mask[:, :, :, :], 1.0 / SPLIT))
            done.inc(pool.memset(c.gather[:, :], 0.0))
            done.inc(pool.memset(c.ones[:, :], 1.0))
            last = done.inc(pool.memset(c.batch_mask[:, :], 1.0))
            pool.wait_ge(pool_done, last)
            done.inc(pool.affine_select(out=c.ident[:, :], in_=c.ident[:, :], compare_op=ALU.not_equal,
                                        fill=1.0, base=0, pattern=[[-1, P]], channel_multiplier=1))
            last = done.inc(pool.affine_select(out=c.head_mask[:, :], in_=c.head_mask[:, :],
                                               compare_op=ALU.is_ge, fill=0.0, base=0,
                                               pattern=[[-DH, HG]], channel_multiplier=1))
            pool.wait_ge(pool_done, last)
            done.inc(pool.affine_select(out=c.head_mask[:, :], in_=c.head_mask[:, :], compare_op=ALU.is_ge,
                                        fill=0.0, base=DH - 1, pattern=[[DH, HG]], channel_multiplier=-1))
            for half, sign in enumerate((-1, 1)):
                own = c.pair_mask[:, :, half, :]
                done.inc(pool.affine_select(out=own, in_=own, compare_op=ALU.is_ge, fill=0.0,
                                            base=(STEPS - 1, -STEPS)[half], pattern=[[0, 2], [0, DH]],
                                            channel_multiplier=sign))
            mid = c.gather[:, STEPS:2 * STEPS]
            last = done.inc(pool.affine_select(out=mid, in_=mid, compare_op=ALU.not_equal, fill=1.0, base=0,
                                               pattern=[[-1, STEPS]], channel_multiplier=1))
            done.inc(pool.affine_select(out=c.batch_mask[:, :], in_=c.batch_mask[:, :], compare_op=ALU.is_ge,
                                        fill=0.0, base=0, pattern=[[-8, BATCH]], channel_multiplier=1))
            last = done.n
            pool.wait_ge(pool_done, last)
            done.inc(pool.affine_select(out=mid, in_=mid, compare_op=ALU.not_equal, fill=1.0, base=-STEPS,
                                        pattern=[[-1, STEPS]], channel_multiplier=1))
            last = done.inc(pool.affine_select(out=c.batch_mask[:, :], in_=c.batch_mask[:, :],
                                               compare_op=ALU.is_ge, fill=0.0, base=7,
                                               pattern=[[8, BATCH]], channel_multiplier=-1))
            pool.wait_ge(pool_done, last)
            pool.sem_inc(consts_ready, 1)

        @block.vector
        def _(dve):
            done = Tally(dve_done)
            dve.wait_ge(w_in, 32)
            fake_quantise(dve, t, t.wq, t.wq, CI, done)
            dve.wait_ge(dve_done, done.n)
            last = fake_quantise(dve, t, t.wp, t.wp, CI, done)
            dve.wait_ge(dve_done, last)
            dve.sem_inc(wquant, 1)
            dve.wait_ge(x_in, 16)
            last = row_stats(dve, t, t.x, done)
            dve.wait_ge(dve_done, last)
            dve.sem_inc(var_ready, 1)
            dve.wait_ge(std_ready, 1)
            last = normalise(dve, t, t.y, t.x, done)
            dve.wait_ge(dve_done, last)
            last = fake_quantise(dve, t, t.y, t.y, TILES, done)
            dve.wait_ge(dve_done, last)
            dve.sem_inc(xquant, 1)
            for n in range(TILES):
                dve.wait_ge(turned, n + 1)
                dve.tensor_copy(t.yT[:, :, n * P:(n + 1) * P],
                                bank[n][:, 0:DM].rearrange("p (j q) -> p j q", j=CI)).then_inc(moved, 1)
            dve.wait_ge(b_in, 80)
            for k in range(CI):
                high = done.inc(dve.tensor_scalar(c.w_hl[0][:, k, :], t.wkvT[:, k, :], SPLIT, None, ALU.mult))
            dve.wait_ge(dve_done, high)
            for k in range(CI):
                done.inc(dve.scalar_tensor_tensor(out=c.w_hl[1][:, k, :], in0=t.wkvT[:, k, :], scalar=SPLIT,
                                                  in1=c.w_hl[0][:, k, :], op0=ALU.mult, op1=ALU.subtract))
            for k in range(2 * CI):
                j, cols = k // 2, slice(k % 2 * 512, k % 2 * 512 + 512)
                dve.wait_ge(q_moved, k + 1)
                high = done.inc(dve.tensor_scalar(c.q_hl[0][:, j, cols], t.qT[:, j, cols], Q_SPLIT, None, ALU.mult))
                dve.wait_ge(dve_done, high)
                done.inc(dve.scalar_tensor_tensor(out=c.q_hl[1][:, j, cols], in0=t.qT[:, j, cols], scalar=Q_SPLIT,
                                                  in1=c.q_hl[0][:, j, cols], op0=ALU.mult, op1=ALU.subtract))

        @block.scalar
        def _(act):
            act.wait_ge(w_turned, 2)
            for k, dst in enumerate((c.wqT, c.wpT)):
                act.activation(dst[:, :, :], bank[k][:, :].rearrange("p (j o) -> p j o", j=CI),
                               ACT.Copy).then_inc(wq_moved, 1)
            act.wait_ge(var_ready, 1)
            act.activation(t.std[:, :], t.var[:, :], ACT.Sqrt).then_inc(std_ready, 1)
            act.wait_ge(b_in, 80)
            for k in range(2 * CI):
                j, half = k // 2, k % 2
                act.wait_ge(q_ready, k + 1)
                act.activation(t.qT[:, j, half * 512:half * 512 + 512], bank[k][:, :], ACT.Identity,
                               bias=c.bq[:, j:j + 1]).then_inc(q_moved, 1)

        @block.tensor
        def _(pe):
            pe.wait_ge(consts_ready, 1)
            pe.wait_ge(wquant, 1)
            for k, w in enumerate((t.wq, t.wp)):
                for i in range(CI):
                    for o in range(CI):
                        ins = pe.transpose(bank[k][:, i * DM + o * P:i * DM + o * P + P],
                                           w[:, o, i * P:(i + 1) * P], c.ident[:, :])
                ins.then_inc(w_turned, 1)
            pe.wait_ge(xquant, 1)
            pe.wait_ge(wq_moved, 2)
            for n in range(TILES):
                for i in range(CI):
                    ins = pe.transpose(bank[n][:, i * P:(i + 1) * P], t.y[:, n, i * P:(i + 1) * P],
                                       c.ident[:, :])
                ins.then_inc(turned, 1)
            for k in range(2 * CI):
                j, half = k // 2, k % 2
                if k == 0:
                    pe.wait_ge(moved, TILES)
                for i in range(CI):
                    ins = pe.matmul(bank[k][:, :], c.wqT[:, i, j * P:(j + 1) * P],
                                    t.yT[:, i, half * 512:half * 512 + 512], start=(i == 0), stop=(i == CI - 1))
                ins.then_inc(q_ready, 1)


def attention(nc, io, c, t, bank):
    score = bank[0:4]
    turn = bank[4:6]
    pvb, prj = bank[6], bank[7]
    TERMS = ((0, 0), (0, 1), (1, 0))
    with ExitStack() as ctx:
        def sb(name, shape, dt=F32):
            return ctx.enter_context(nc.sbuf_tensor(name, shape, dt))

        def sem(name):
            return ctx.enter_context(nc.semaphore(name))

        raw = sb("ctx_raw", [P, CI, CTX])
        ctx_hl = [[sb(f"ctx{part}{u}", [P, CI, CTX], F16) for part in "hl"] for u in range(2)]
        fresh = [sb(f"fresh{k}", [P, 2 * DM]) for k in range(2)]
        kT = [[sb(f"kT{part}{u}", [P, CI, CTX], F16) for part in "hl"] for u in range(2)]
        v = [sb(f"v{u}", [P, KROW, PAIRS, 2, 2 * DH], F16) for u in range(2)]
        qblk = [[sb(f"qblk{part}{u}", [P, CI, HG, STEPS], F16) for part in "hl"] for u in range(2)]
        prob = [sb(f"prob{u}", [P, CTX]) for u in range(2)]
        probT = [[sb(f"probT{part}{u}", [P, TBLOCKS * P], F16) for part in "hl"] for u in range(2)]
        bk = sb("bk_scaled", [P, CI])
        mx, top = sb("mx", [P, NCH]), sb("row_max", [P, 1])
        shift = [sb(f"shift{u}", [P, 1]) for u in range(2)]
        esum = [sb(f"esum{u}", [P, NCH]) for u in range(2)]
        den = sb("den", [P, 1])
        rden = sb("rden", [P, 1])
        parts_out = [sb(f"parts_out{u}", [P, 2, 2 * DH]) for u in range(2)]

        ctx_in = [sem(f"ctx_in{j}") for j in range(CI)]
        ctx_scaled, ctx_high, ctx_low = sem("ctx_scaled"), sem("ctx_high"), sem("ctx_low")
        bk_scaled, kv_high, kv_low = sem("bk_scaled_up"), sem("kv_high"), sem("kv_low")
        q_masked, proj_done, proj_out = sem("q_masked"), sem("proj_done"), sem("proj_out")
        scored, max_ready, exp_done = sem("scored"), sem("max_ready"), sem("exp_done")
        turned, p_high, p_low = sem("a_turned"), sem("p_high"), sem("p_low")
        pv_done, o_out, o_summed = sem("pv_done"), sem("o_out"), sem("o_summed")
        cleared, mx_done, den_done = sem("cleared"), sem("mx_done"), sem("den_done")
        block = ctx.enter_context(nc.Block())

        def kv_parts(k, u):
            now = fresh[(u * PROJ + k) % 2]
            if k < KGROUPS:
                j, (c0, w) = k // NCH, COLS[k % NCH]
                return (*(kT[u][part][:, j, c0:c0 + w] for part in range(2)), now[:, 0:w])
            m, n = VTILES[k - KGROUPS]
            rows = ROWS[m][1]
            return (*(v[u][0:rows, m:m + n, :, part, :].rearrange("p m g d -> p (m g) d") for part in range(2)),
                    now[0:rows, 0:n * DM].rearrange("p (g d) -> p g d", g=n * PAIRS))

        def in_batches(eng, batch):
            batch(0, 0, True, True, True, 3)
            with eng.Fori(0, BATCH // 2 - 2) as i:
                batch(2 * i + 1, 1, True, True, False, 2 * i + 4)
                batch(2 * i + 2, 0, True, True, False, 2 * i + 5)
            batch(BATCH - 3, 1, True, True, False, BATCH)
            batch(BATCH - 2, 0, True, False, False, 0)
            batch(BATCH - 1, 1, False, False, False, 0)

        @block.sync
        def _(sp):
            def load(b, j):
                sp.dma_start(raw[:, j, :], io["ctxT"][bass.ds(b, 1), j * P:(j + 1) * P, :]
                             .rearrange("o p m -> p (o m)")).then_inc(ctx_in[j], 16)

            for j in range(CI):
                load(0, j)
            with sp.Fori(0, BATCH - 1) as i:
                for j in range(CI):
                    sp.wait_ge(ctx_low, i * KGROUPS + (j + 1) * NCH)
                    load(i + 1, j)

        @block.gpsimd
        def _(pool):
            def mask(b, u, k, first):
                if not first:
                    pool.wait_ge(scored, (b - 1) * (PAIRS * NCH))
                part, j = k // CI, k % CI
                q = c.q_hl[part][:, j:j + 1, bass.ds(b * STEPS, STEPS)].broadcast_to([P, HG, STEPS])
                own = c.head_mask[:, :].unsqueeze(2).broadcast_to([P, HG, STEPS])
                pool.tensor_tensor(qblk[u][part][:, j, :, :], q, own, ALU.mult).then_inc(q_masked, 1)

            def ctx_lows(b, u, n):
                j, (c0, w) = n // NCH, COLS[n % NCH]
                pool.wait_ge(ctx_high, b * KGROUPS + n + 1)
                pool.tensor_tensor(ctx_hl[u][1][:, j, c0:c0 + w], raw[:, j, c0:c0 + w], ctx_hl[u][0][:, j, c0:c0 + w],
                                   ALU.subtract).then_inc(ctx_low, 1)

            def kv_lows(b, k, u):
                pool.wait_ge(kv_high, b * PROJ + k + 1)
                high, low, src = kv_parts(k, u)
                pool.tensor_tensor(low, src, high, ALU.subtract).then_inc(kv_low, 1)

            def sum_parts(b, g):
                pool.wait_ge(o_out, b * PAIRS + g + 1)
                pool.tensor_tensor(t.o[:, bass.ds(b, 1), g, :].rearrange("p o d -> p (o d)"), parts_out[g % 2][:, 0, :],
                                   parts_out[g % 2][:, 1, :], ALU.add).then_inc(o_summed, 1)

            def batch(b, u, more, split, first, loads):
                for g in range(PAIRS):
                    if more and g > 0:
                        kv_lows(b + 1, 2 * g - 1, 1 - u)
                    if more and g < 2 * CI:
                        mask(b + 1, 1 - u, g, first)
                    if more:
                        kv_lows(b + 1, 2 * g, 1 - u)
                    if split:
                        ctx_lows(b + 2, u, g)
                    sum_parts(b, g)

            for n in range(KGROUPS):
                ctx_lows(0, 0, n)
            for k in range(2 * CI):
                mask(0, 0, k, True)
            for k in range(PROJ):
                kv_lows(0, k, 0)
            for n in range(KGROUPS):
                ctx_lows(1, 1, n)
            in_batches(pool, batch)

        @block.scalar
        def _(act):
            def project_out(b, k, u, first=False):
                act.wait_ge(proj_done, b * PROJ + k + 1)
                if not first:
                    act.wait_ge(kv_low, b * PROJ + k - 1)
                now = fresh[(u * PROJ + k) % 2]
                if k < KGROUPS:
                    j, w = k // NCH, COLS[k % NCH][1]
                    ins = act.activation(now[:, 0:w], prj[:, 0:w], ACT.Identity, bias=bk[:, j:j + 1], scale=1.0 / SPLIT)
                else:
                    m, n = VTILES[k - KGROUPS]
                    rows = ROWS[m][1]
                    ins = act.activation(now[0:rows, 0:n * DM], prj[0:rows, 0:n * DM], ACT.Copy, scale=1.0 / SPLIT)
                ins.then_inc(proj_out, 1)

            def exp(b, g, n, first):
                if n == 0:
                    act.wait_ge(max_ready, b * PAIRS + g + 1)
                    if not first:
                        act.wait_ge(turned, (b * PAIRS + g - 1) * NCH)
                        act.wait_ge(o_out, b * PAIRS + g - 1)
                c0, w = COLS[n]
                act.activation(prob[g % 2][:, c0:c0 + w], score[n][:, 0:w], ACT.Exp,
                               bias=shift[g % 2][:, 0:1], scale=1.0 / (4 * SPLIT * Q_SPLIT),
                               accum_out=esum[g % 2][:, n:n + 1]).then_inc(exp_done, 1)

            def highs(b, g, r, first):
                k = (b * PAIRS + g) * NCH + r
                act.wait_ge(turned, k + 1)
                if not first:
                    act.wait_ge(pv_done, k - 1)
                rows, n = group(r)
                act.activation(probT[k2(g, r)][0][0:rows, 0:n * P], turn[k2(g, r)][0:rows, 0:n * P], ACT.Copy
                               ).then_inc(p_high, 1)

            def batch(b, u, more, split, first, loads):
                for g in range(PAIRS):
                    for n in range(NCH):
                        exp(b, g, n, first and g < 2)
                        if n == 0 and more and g > 0:
                            project_out(b + 1, 2 * g - 1, 1 - u)
                        if n == 2 and more:
                            project_out(b + 1, 2 * g, 1 - u)
                        if n > 0:
                            highs(b, g, n - 1, first and g == 0 and n <= 2)
                    highs(b, g, NCH - 1, False)

            act.activation(bk[:, :], c.bk[:, :], ACT.Copy, scale=SPLIT).then_inc(bk_scaled, 1)
            act.wait_ge(bk_scaled, 1)
            for k in range(PROJ):
                project_out(0, k, 0, k < 2)
            in_batches(act, batch)

        @block.vector
        def _(dve):
            def scale_ctx(b, n, loads):
                j, (c0, w) = n // NCH, COLS[n % NCH]
                if n % NCH == 0:
                    dve.wait_ge(ctx_in[j], 16 * loads)
                dve.tensor_scalar(raw[:, j, c0:c0 + w], raw[:, j, c0:c0 + w], SPLIT, None, ALU.mult
                                  ).then_inc(ctx_scaled, 1)

            def ctx_highs(b, u, n):
                j, (c0, w) = n // NCH, COLS[n % NCH]
                dve.wait_ge(ctx_scaled, b * KGROUPS + n + 1)
                dve.tensor_copy(ctx_hl[u][0][:, j, c0:c0 + w], raw[:, j, c0:c0 + w]).then_inc(ctx_high, 1)

            def kv_highs(b, k, u):
                dve.wait_ge(proj_out, b * PROJ + k + 1)
                high, _, src = kv_parts(k, u)
                dve.tensor_copy(high, src).then_inc(kv_high, 1)

            def maximum(b, g, n):
                dve.wait_ge(scored, (b * PAIRS + g) * NCH + n + 1)
                dve.tensor_reduce(mx[:, n:n + 1], score[n][:, 0:COLS[n][1]], AX.X, ALU.max).then_inc(mx_done, 1)

            def overall(b, g):
                k = (b * PAIRS + g) * (NCH + 1)
                dve.wait_ge(mx_done, k + NCH)
                dve.tensor_reduce(top[:, :], mx[:, :], AX.X, ALU.max).then_inc(mx_done, 1)
                dve.wait_ge(mx_done, k + NCH + 1)
                dve.tensor_scalar(shift[g % 2][:, :], top[:, :], -1.0 / (4 * SPLIT * Q_SPLIT), P_LOG, ALU.mult, ALU.add
                                  ).then_inc(max_ready, 1)

            def lows(b, g, r):
                dve.wait_ge(p_high, (b * PAIRS + g) * NCH + r + 1)
                rows, n = group(r)
                high, low = (probT[k2(g, r)][part][0:rows, 0:n * P] for part in range(2))
                dve.tensor_tensor(low, turn[k2(g, r)][0:rows, 0:n * P], high, ALU.subtract).then_inc(p_low, 1)

            def output(b, g, first):
                G = b * PAIRS + g
                dve.wait_ge(exp_done, (G + 1) * NCH)
                dve.tensor_reduce(den[:, :], esum[g % 2][:, :], AX.X, ALU.add).then_inc(den_done, 1)
                dve.wait_ge(den_done, 2 * G + 1)
                dve.reciprocal(rden[:, :], den[:, :]).then_inc(den_done, 1)
                dve.wait_ge(den_done, 2 * G + 2)
                dve.wait_ge(pv_done, (G + 1) * NCH)
                if not first:
                    dve.wait_ge(o_summed, G - 1)
                dve.scalar_tensor_tensor(out=parts_out[g % 2][:, :, :].rearrange("p a d -> p (a d)"),
                                         in0=pvb[:, 0:4 * DH], scalar=rden[:, 0:1],
                                         in1=c.pair_mask[:, :, :, :].rearrange("p a h d -> p (a h d)"),
                                         op0=ALU.mult, op1=ALU.mult).then_inc(o_out, 1)

            def batch(b, u, more, split, first, loads):
                for g in range(PAIRS):
                    ahead = more or g < PAIRS - 1
                    nxt = (b, g + 1) if g < PAIRS - 1 else (b + 1, 0)
                    for n in range(NCH):
                        if ahead:
                            maximum(*nxt, n)
                        if n == NCH - 1 and ahead:
                            overall(*nxt)
                        lows(b, g, n)
                        if n == 0 and more and g > 0:
                            kv_highs(b + 1, 2 * g - 1, 1 - u)
                        if n == 2 and more:
                            kv_highs(b + 1, 2 * g, 1 - u)
                        if n == 1 and split:
                            scale_ctx(b + 2, g, loads)
                    if split:
                        ctx_highs(b + 2, u, g)
                    output(b, g, first and g < 2)

            dve.memset(turn[k2(0, NCH - 1)][:, (TBLOCKS - 1) * P:TBLOCKS * P], 0.0).then_inc(cleared, 1)
            for n in range(KGROUPS):
                scale_ctx(0, n, 1)
                ctx_highs(0, 0, n)
            for k in range(PROJ):
                kv_highs(0, k, 0)
            for n in range(KGROUPS):
                scale_ctx(1, n, 2)
                ctx_highs(1, 1, n)
            for n in range(NCH):
                maximum(0, 0, n)
            overall(0, 0)
            in_batches(dve, batch)

        @block.tensor
        def _(pe):
            def project(b, k, u, first):
                if not first:
                    pe.wait_ge(proj_out, b * PROJ + k)
                terms = [(a, x, i) for a, x in TERMS for i in range(CI)]
                for q, (a, x, i) in enumerate(terms if k < KGROUPS else ()):
                    j, (c0, w) = k // NCH, COLS[k % NCH]
                    ins = pe.matmul(prj[:, 0:w], c.w_hl[a][:, i, j * P:(j + 1) * P], ctx_hl[u][x][:, i, c0:c0 + w],
                                    start=(q == 0), stop=(q == len(terms) - 1))
                m, n = VTILES[k - KGROUPS] if k >= KGROUPS else (0, 0)
                for s in range(n):
                    m0, rows = ROWS[m + s]
                    for q, (a, x, i) in enumerate(terms):
                        ins = pe.matmul(prj[0:rows, s * DM:(s + 1) * DM], ctx_hl[u][a][:, i, m0:m0 + rows],
                                        c.w_hl[x][:, i, DM:2 * DM], start=(q == 0), stop=(q == len(terms) - 1))
                ins.then_inc(proj_done, 1)

            def scores(b, g, n, u, first):
                if g == 0 and n == 0:
                    pe.wait_ge(q_masked, (b + 1) * 2 * CI)
                    pe.wait_ge(kv_low, b * PROJ + KGROUPS)
                j, h = g // (PAIRS // CI), 2 * (g % (PAIRS // CI))
                c0, w = COLS[n]
                if not first:
                    pe.wait_ge(exp_done, (b * PAIRS + g - 1) * NCH + n + 1)
                for q, (a, x) in enumerate(TERMS):
                    ins = pe.matmul(score[n][:, 0:w], qblk[u][a][:, j, h:h + 2, :].rearrange("p h q -> p (h q)"),
                                    kT[u][x][:, j, c0:c0 + w], start=(q == 0), stop=(q == len(TERMS) - 1))
                ins.then_inc(scored, 1)

            def turn_probs(b, g, r, first):
                k = (b * PAIRS + g) * NCH + r
                pe.wait_ge(exp_done, k + 1)
                if not first:
                    pe.wait_ge(p_low, k - 1)
                for s, (m0, rows) in enumerate(TURNS[r]):
                    ins = pe.transpose(turn[k2(g, r)][0:rows, s * P:(s + 1) * P], prob[g % 2][:, m0:m0 + rows],
                                       c.ident[:, :])
                ins.then_inc(turned, 1)

            def times_v(b, g, u, r, first):
                k = (b * PAIRS + g) * NCH + r
                pe.wait_ge(p_low, k + 1)
                if g == 0 and r == 0:
                    pe.wait_ge(kv_low, (b + 1) * PROJ)
                if r == 0 and not first:
                    pe.wait_ge(o_out, b * PAIRS + g)
                for s, (m0, rows) in enumerate(TURNS[r]):
                    m = m0 // P
                    for part in range(2):
                        ins = pe.matmul(pvb[:, 0:4 * DH], probT[k2(g, r)][part][0:rows, s * P:(s + 1) * P],
                                        v[u][0:rows, m, g, :, :].rearrange("p a d -> p (a d)"),
                                        start=(m == 0 and part == 0), stop=(m == KROW - 1 and part == 1))
                ins.then_inc(pv_done, 1)

            def batch(b, u, more, split, first, loads):
                for g in range(PAIRS):
                    start = first and g == 0
                    if more and g == 0:
                        pe.wait_ge(ctx_low, (b + 2) * KGROUPS)
                    for n in range(NCH):
                        turn_probs(b, g, n, start and n < 2)
                        if g < PAIRS - 1:
                            scores(b, g + 1, n, u, False)
                        elif more:
                            scores(b + 1, 0, n, 1 - u, False)
                        if n == 0 and more:
                            project(b + 1, 2 * g, 1 - u, False)
                        if n == NCH - 1 and more and g < PAIRS - 1:
                            project(b + 1, 2 * g + 1, 1 - u, False)
                        if n > 0:
                            times_v(b, g, u, n - 1, start)
                    times_v(b, g, u, NCH - 1, start)

            pe.wait_ge(cleared, 1)
            pe.wait_ge(ctx_low, KGROUPS)
            for k in range(PROJ):
                project(0, k, 0, k == 0)
            for n in range(NCH):
                scores(0, 0, n, 0, True)
            in_batches(pe, batch)


def group(r):
    return P, len(TURNS[r])


def k2(g, r):
    return (g * NCH + r) % 2


def project_attention(nc, io, c, t, bank):
    with ExitStack() as ctx:
        def sem(name):
            return ctx.enter_context(nc.semaphore(name))

        gathered, with_bias, dve_done, oquant = sem("p_gathered"), sem("p_with_bias"), sem("p_dve_done"), sem("p_oquant")
        turned, moved, projected, var_ready, std_ready = (sem("p_turned"), sem("p_moved"), sem("p_projected"),
                                                          sem("p_var_ready"), sem("p_std_ready"))
        y_ready = sem("p_y_ready")
        block = ctx.enter_context(nc.Block())

        @block.tensor
        def _(pe):
            for n in range(TILES):
                for half in range(2):
                    sel = c.gather[:, (1 - half) * STEPS:(1 - half) * STEPS + P]
                    ins = pe.matmul(bank[n][:, 0:DM], sel, t.o[:, 2 * n + half, :, :].rearrange("p g d -> p (g d)"),
                                    start=(half == 0), stop=(half == 1))
                ins.then_inc(gathered, 1)
            pe.wait_ge(oquant, 1)
            for n in range(TILES):
                for i in range(CI):
                    ins = pe.transpose(bank[n][:, i * P:(i + 1) * P], t.y[:, n, i * P:(i + 1) * P], c.ident[:, :])
                ins.then_inc(turned, 1)
            for n in range(TILES):
                pe.wait_ge(moved, n + 1)
                for i in range(CI):
                    ins = pe.matmul(bank[n][:, 0:DM], t.yT[:, i, n * P:(n + 1) * P], c.wpT[:, i, :],
                                    start=(i == 0), stop=(i == CI - 1))
                ins.then_inc(projected, 1)
            pe.wait_ge(y_ready, 1)
            for n in range(TILES):
                for i in range(CI):
                    ins = pe.transpose(bank[n][:, i * P:(i + 1) * P], t.y[:, n, i * P:(i + 1) * P], c.ident[:, :])
                ins.then_inc(turned, 1)

        @block.scalar
        def _(act):
            act.wait_ge(var_ready, 1)
            act.activation(t.std[:, :], t.var[:, :], ACT.Sqrt).then_inc(std_ready, 1)

        @block.vector
        def _(dve):
            done = Tally(dve_done)
            for n in range(TILES):
                dve.wait_ge(gathered, n + 1)
                last = done.inc(dve.tensor_tensor(t.y[:, n, :], bank[n][:, 0:DM], c.bv[:, :], ALU.add))
            dve.wait_ge(dve_done, last)
            last = fake_quantise(dve, t, t.y, t.y, TILES, done)
            dve.wait_ge(dve_done, last)
            dve.sem_inc(oquant, 1)
            for n in range(TILES):
                dve.wait_ge(turned, n + 1)
                dve.tensor_copy(t.yT[:, :, n * P:(n + 1) * P],
                                bank[n][:, 0:DM].rearrange("p (j q) -> p j q", j=CI)).then_inc(moved, 1)
            for n in range(TILES):
                last = done.inc(dve.tensor_tensor(t.x[:, n, :], t.x[:, n, :], c.bp[:, :], ALU.add))
            dve.wait_ge(dve_done, last)
            for n in range(TILES):
                dve.wait_ge(projected, n + 1)
                last = done.inc(dve.tensor_tensor(t.x[:, n, :], bank[n][:, 0:DM], t.x[:, n, :], ALU.add))
            dve.wait_ge(dve_done, last)
            last = row_stats(dve, t, t.x, done)
            dve.wait_ge(dve_done, last)
            dve.sem_inc(var_ready, 1)
            dve.wait_ge(std_ready, 1)
            last = normalise(dve, t, t.y, t.x, done)
            dve.wait_ge(dve_done, last)
            dve.sem_inc(y_ready, 1)
            for n in range(TILES):
                dve.wait_ge(turned, TILES + n + 1)
                dve.tensor_copy(t.yT[:, :, n * P:(n + 1) * P],
                                bank[n][:, 0:DM].rearrange("p (j q) -> p j q", j=CI)).then_inc(moved, 1)


DS = 128
BLK = 8
NB = STEPS // BLK
HALF = BLK // 2
GROUPS = TOK // HALF
PAIR_S = [(s, r) for s in range(HALF) for r in range(s + 1, HALF)]
PAIR_O = [(s, r) for s in range(HALF) for r in range(s, HALF)]
DECAY = 8.0
KIND_K, KIND_Q, KIND_O = range(3)


def features(nc, io, c, t, m, bank):
    with ExitStack() as ctx:
        def sb(name, shape):
            return ctx.enter_context(nc.sbuf_tensor(name, shape, F32))

        def sem(name):
            return ctx.enter_context(nc.semaphore(name))

        w = {n: sb(f"w_{n}", [P, CI, DS]) for n in ("k", "v", "q", "af", "as", "ir")}
        w_pw, w_pwb, w_ir2, w_irb = sb("w_pw", [P, CI, 3]), sb("w_pwb", [P, CI, 3, P]), sb("w_ir2", [P, 1]), sb("w_irb", [P, P])
        w_nm1, w_nm2 = sb("w_nm1", [P, 2 * DS]), sb("w_nm2", [P, 2, DS])
        cols = sb("cols", [P, 12])
        lam8 = sb("lam8", [P, 2])
        la, irg, h1 = sb("la", [P, 2, TOK]), sb("irg", [P, TOK]), sb("h1", [P, 2, TOK])
        lg, sq, nrm = sb("lg", [P, 3, TOK]), sb("sq", [P, 2, TOK]), sb("nrm", [P, 2, TOK])
        upd, keep, top, al = sb("upd", [P, TOK]), sb("keep", [P, TOK]), sb("top", [P, TOK]), sb("al", [P, 2, TOK])

        w_in, dve_done, act_done, pe_done = sem("f_w_in"), sem("f_dve_done"), sem("f_act_done"), sem("f_pe_done")
        pool_done = sem("f_pool_done")
        block = ctx.enter_context(nc.Block())

        jobs = ([("v", h, "dve") for h in range(2)] + [(n, h, "act") for n in ("af", "as", "ir") for h in range(2)]
                + [(("nm1", j), h, "act") for j in range(2) for h in range(2)]
                + [(n, h, "dve") for n in ("k", "q") for h in range(2)]
                + [(("pw", n), h, "act") for n in range(3) for h in range(2)]
                + [("imp", h, "dve") for h in range(2)] + [("nu", h, "act") for h in range(2)]
                + [(("norm", n), h, "act") for n in range(2) for h in range(2)])
        DVE0 = 4
        taken, counts = [], {"dve": DVE0, "act": 0}
        for name, h, e in jobs:
            counts[e] += 1
            taken.append((e, counts[e]))
        at = {(name, h): taken[k] for k, (name, h, _) in enumerate(jobs)}
        JOBS_ACT = sum(e == "act" for _, _, e in jobs)
        SQUARED = DVE0 + sum(e == "dve" for _, _, e in jobs) + 2
        LAM_READY = SQUARED + 1
        LG_READY = LAM_READY + 3
        LA_READY = LG_READY + 3

        @block.sync
        def _(sp):
            for n in w:
                sp.dma_start(w[n][:, :, :], io["W" + n].rearrange("(i p) o -> p i o", p=P)).then_inc(w_in, 16)
            sp.dma_start(w_pw[:, :, :], io["pw_w"].rearrange("(i p) o -> p i o", p=P)).then_inc(w_in, 16)
            sp.dma_start(w_ir2[:, :], io["ir_w2"]).then_inc(w_in, 16)
            sp.dma_start(w_nm1[:, :], io["nm_w1"]).then_inc(w_in, 16)
            sp.dma_start(w_nm2[:, :, :], io["nm_w2"].rearrange("(i p) o -> p i o", p=P)).then_inc(w_in, 16)
            sp.dma_start(cols[:, 0:6], io["cols6"]).then_inc(w_in, 16)
            sp.dma_start(cols[:, 6:7], io["ir_b2"].partition_broadcast(P)).then_inc(w_in, 16)
            sp.dma_start(cols[:, 7:10], io["pw_b"].partition_broadcast(P)).then_inc(w_in, 16)
            sp.dma_start(cols[:, 10:12], io["lam"]).then_inc(w_in, 16)
            sp.wait_ge(w_in, 14 * 16)

        @block.gpsimd
        def _(pool):
            pool.memset(keep[:, :], 1.0).then_inc(pool_done, 1)
            pool.wait_ge(pool_done, 1)
            pool.memset(keep[:, :].rearrange("p (g t) -> p g t", t=BLK)[:, :, 0], 0.0).then_inc(pool_done, 1)
            pool.wait_ge(pool_done, 2)

        @block.tensor
        def _(pe):
            pe.wait_ge(w_in, 14 * 16)
            pe.wait_ge(dve_done, DVE0)

            def wait_for(e, n):
                pe.wait_ge({"dve": dve_done, "act": act_done}[e], n)

            for k, (name, h, _) in enumerate(jobs):
                if k >= 8:
                    wait_for(*taken[k - 8])
                b = bank[k % 8]
                half = slice(512 * h, 512 * h + 512)
                if name in w:
                    parts = [(w[name][:, i, :], t.yT[:, i, half]) for i in range(CI)]
                elif name[0] == "pw":
                    parts = [(w_pwb[:, i, name[1], :], t.yT[:, i, half]) for i in range(CI)]
                elif name[0] == "nm1":
                    wait_for(*at["v", h])
                    parts = [(w_nm1[:, name[1] * DS:(name[1] + 1) * DS], m.v[:, half])]
                elif name == "imp":
                    wait_for(*at["ir", h])
                    parts = [(w_irb[:, :], irg[:, half])]
                elif name == "nu":
                    wait_for(*at[("nm1", 1), h])
                    parts = [(w_nm2[:, j, :], h1[:, j, half]) for j in range(2)]
                else:
                    pe.wait_ge(dve_done, SQUARED)
                    parts = [(c.ones[:, :], sq[:, name[1], half])]
                for i, (lhs, rhs) in enumerate(parts):
                    ins = pe.matmul(b[:, :], lhs, rhs, start=(i == 0), stop=(i == len(parts) - 1))
                ins.then_inc(pe_done, 1)

        @block.scalar
        def _(act):
            done = Tally(act_done)
            act.wait_ge(w_in, 14 * 16)
            for k, (name, h, e) in enumerate(jobs):
                if e != "act":
                    continue
                act.wait_ge(pe_done, k + 1)
                half = slice(512 * h, 512 * h + 512)
                b = bank[k % 8][:, :]
                if name == "af":
                    ins = act.activation(la[:, 0, half], b, ACT.Sigmoid, bias=cols[:, 0:1])
                elif name == "as":
                    ins = act.activation(la[:, 1, half], b, ACT.Sigmoid, bias=cols[:, 1:2])
                elif name == "ir":
                    ins = act.activation(irg[:, half], b, ACT.Gelu, bias=cols[:, 2:3])
                elif name[0] == "nm1":
                    ins = act.activation(h1[:, name[1], half], b, ACT.Gelu, bias=cols[:, 3 + name[1]:4 + name[1]])
                elif name[0] == "pw":
                    ins = act.activation(lg[:, name[1], half], b, ACT.Identity, bias=cols[:, 7 + name[1]:8 + name[1]])
                elif name == "nu":
                    ins = act.activation(m.nu[:, half], b, ACT.Identity, bias=cols[:, 5:6])
                else:
                    ins = act.activation(nrm[:, name[1], half], b, ACT.Sqrt)
                assert done.inc(ins) == at[name, h][1]
            last = done.inc(act.activation(lam8[:, :], cols[:, 10:12], ACT.Sigmoid))
            act.wait_ge(dve_done, LAM_READY)
            done.inc(act.activation(lam8[:, :], lam8[:, :], ACT.Ln))
            act.wait_ge(dve_done, LG_READY)
            done.inc(act.activation(lg[:, :, :], lg[:, :, :], ACT.Exp))
            act.wait_ge(dve_done, LA_READY)
            done.inc(act.activation(al[:, :, :], la[:, :, :], ACT.Exp))

        @block.vector
        def _(dve):
            done = Tally(dve_done)
            dve.wait_ge(w_in, 14 * 16)
            for i in range(CI):
                for n in range(3):
                    ins = dve.tensor_scalar(w_pwb[:, i, n, :], c.ones[:, :], w_pw[:, i, n:n + 1], None, ALU.mult)
                done.inc(ins)
            done.inc(dve.tensor_scalar(w_irb[:, :], c.ones[:, :], w_ir2[:, 0:1], None, ALU.mult))
            done.inc(dve.memset(m.lx[:, :, :], 0.0))
            assert done.n == DVE0
            for k, (name, h, e) in enumerate(jobs):
                if e != "dve":
                    continue
                dve.wait_ge(pe_done, k + 1)
                half = slice(512 * h, 512 * h + 512)
                b = bank[k % 8][:, :]
                if name == "imp":
                    ins = dve.tensor_scalar(upd[:, half], b, cols[:, 6:7], 0.0, ALU.add, ALU.is_gt)
                else:
                    ins = dve.tensor_copy({"v": m.v, "k": m.k, "q": m.qh}[name][:, half], b)
                assert done.inc(ins) == at[name, h][1]
            dve.wait_ge(dve_done, done.n)
            done.inc(dve.tensor_tensor(sq[:, 0, :], m.k[:, :], m.k[:, :], ALU.mult))
            done.inc(dve.tensor_tensor(sq[:, 1, :], m.qh[:, :], m.qh[:, :], ALU.mult))
            assert done.n == SQUARED
            dve.wait_ge(act_done, JOBS_ACT + 1)
            done.inc(dve.tensor_scalar(lam8[:, :], lam8[:, :], 1e-8, None, ALU.add))
            assert done.n == LAM_READY
            dve.wait_ge(dve_done, done.inc(dve.tensor_tensor(top[:, :], lg[:, 0, :], lg[:, 1, :], ALU.max)))
            dve.wait_ge(dve_done, done.inc(dve.tensor_tensor(top[:, :], top[:, :], lg[:, 2, :], ALU.max)))
            done.inc(dve.tensor_tensor(lg[:, :, :], lg[:, :, :], top[:, :].unsqueeze(1).broadcast_to([P, 3, TOK]),
                                       ALU.subtract))
            assert done.n == LG_READY
            dve.wait_ge(act_done, JOBS_ACT + 2)
            dve.wait_ge(dve_done, done.inc(dve.tensor_scalar(lam8[:, :], lam8[:, :], DECAY, None, ALU.mult)))
            for x in range(2):
                done.inc(dve.tensor_scalar(la[:, x, :], la[:, x, :], lam8[:, x:x + 1], None, ALU.mult))
            assert done.n == LA_READY
            done.inc(dve.tensor_scalar(nrm[:, :, :], nrm[:, :, :], 1e-12, None, ALU.max))
            dve.wait_ge(dve_done, done.n)
            dve.wait_ge(dve_done, done.inc(dve.reciprocal(nrm[:, :, :], nrm[:, :, :])))
            done.inc(dve.tensor_tensor(m.k[:, :], m.k[:, :], nrm[:, 0, :], ALU.mult))
            dve.wait_ge(dve_done, done.inc(dve.tensor_tensor(m.qh[:, :], m.qh[:, :], nrm[:, 1, :], ALU.mult)))
            dve.wait_ge(pool_done, 2)
            for x in range(2):
                done.inc(dve.tensor_tensor_scan(m.lb[:, x, :], keep[:, :], la[:, x, :], 0.0, ALU.mult, ALU.add))
            dve.wait_ge(dve_done, done.n)
            lb8 = m.lb[:, :, :].rearrange("p x (g t) -> p (x g) t", t=BLK)
            lx8 = m.lx[:, :, :].rearrange("p x (g t) -> p (x g) t", t=BLK)
            done.inc(dve.tensor_copy(lx8[:, :, 1:BLK], lb8[:, :, 0:BLK - 1]))
            dve.wait_ge(act_done, JOBS_ACT + 3)
            dve.wait_ge(dve_done, done.inc(dve.tensor_tensor(top[:, :], lg[:, 0, :], lg[:, 1, :], ALU.add)))
            dve.wait_ge(dve_done, done.inc(dve.tensor_tensor(top[:, :], top[:, :], lg[:, 2, :], ALU.add)))
            dve.wait_ge(dve_done, done.inc(dve.reciprocal(top[:, :], top[:, :])))
            done.inc(dve.tensor_tensor(m.pw2[:, :], lg[:, 2, :], top[:, :], ALU.mult))
            for x in range(2):
                dve.wait_ge(dve_done, done.inc(dve.tensor_tensor(lg[:, x, :], lg[:, x, :], top[:, :], ALU.mult)))
                done.inc(dve.tensor_tensor(m.oq[:, x, :], lg[:, x, :], m.qh[:, :], ALU.mult))
            dve.wait_ge(dve_done, done.n)
            done.inc(dve.tensor_scalar(m.qh[:, :], m.qh[:, :], 0.5, None, ALU.mult))
            dve.wait_ge(act_done, JOBS_ACT + 4)
            dve.wait_ge(dve_done, done.inc(dve.tensor_scalar(al[:, :, :], al[:, :, :], -1.0, 1.0, ALU.mult, ALU.add)))
            done.inc(dve.tensor_tensor(m.u[:, :, :], al[:, :, :], m.k[:, :].unsqueeze(1).broadcast_to([P, 2, TOK]),
                                       ALU.mult))
            dve.wait_ge(dve_done, done.n)
            dve.wait_ge(dve_done, done.inc(dve.tensor_tensor(m.u[:, 1, :], m.u[:, 1, :], upd[:, :], ALU.mult)))


def factors(nc, c, m, f, bank):
    with ExitStack() as ctx:
        def sem(name):
            return ctx.enter_context(nc.semaphore(name))

        diff, exped, mult, summed, stored, pool_done = (sem("g_diff"), sem("g_exped"), sem("g_mult"), sem("g_summed"),
                                                        sem("g_stored"), sem("g_pool_done"))
        block = ctx.enter_context(nc.Block())

        def by(tensor, n):
            return tensor.rearrange("p x (g t) -> p x g t", t=n)

        lb8, lx8, u8 = by(m.lb[:, :, :], BLK), by(m.lx[:, :, :], BLK), by(m.u[:, :, :], BLK)
        lb4, lx4, u4 = by(m.lb[:, :, :], HALF), by(m.lx[:, :, :], HALF), by(m.u[:, :, :], HALF)
        k4 = m.k[:, :].rearrange("p (g t) -> p g t", t=HALF)
        q4 = m.qh[:, :].rearrange("p (g t) -> p g t", t=HALF)
        k8 = m.k[:, :].rearrange("p (g t) -> p g t", t=BLK)
        q8 = m.qh[:, :].rearrange("p (g t) -> p g t", t=BLK)
        oq4, oq8 = by(m.oq[:, :, :], HALF), by(m.oq[:, :, :], BLK)
        z = [f.z[:, x, :, :, :].rearrange("p n b t -> p b n t") for x in range(2)]
        zn = [f.zn[:, x, :, :, :].rearrange("p n b t -> p b n t") for x in range(2)]
        lbn = [m.lb[:, x, :].rearrange("p (b n t) -> p b n t", b=BATCH, n=NB) for x in range(2)]
        un = [m.u[:, x, :].rearrange("p (b n t) -> p b n t", b=BATCH, n=NB) for x in range(2)]
        G8 = TOK // BLK
        CHUNK = 512
        cp_cols = f.cp[:, :, :, :, :].rearrange("p x k i g -> p (x k i g)")
        co_cols = f.co[:, :, :, :].rearrange("p x i g -> p (x i g)")
        chunks = ([cp_cols[:, a:a + CHUNK] for a in range(0, 4 * len(PAIR_S) * GROUPS, CHUNK)]
                  + [co_cols[:, a:a + CHUNK] for a in range(0, 2 * len(PAIR_O) * GROUPS, CHUNK)])
        n_cp = 4 * len(PAIR_S) * GROUPS // CHUNK
        near = [f.near[:, x, :, :, :] for x in range(2)]

        def end(x, i):
            return lb8[:, x, :, i].unsqueeze(2).broadcast_to([P, G8, HALF])

        @block.vector
        def _(dve):
            done = Tally(diff)
            for i, (s, r) in enumerate(PAIR_S):
                ins = dve.tensor_tensor(f.cp[:, :, 0, i, :], lx4[:, :, :, r], lb4[:, :, :, s], ALU.subtract)
            done.inc(ins)
            for i, (s, r) in enumerate(PAIR_O):
                if s < r:
                    ins = dve.tensor_tensor(f.co[:, :, i, :], lb4[:, :, :, r], lb4[:, :, :, s], ALU.subtract)
                else:
                    ins = dve.memset(f.co[:, :, i, :], 0.0)
            done.inc(ins)
            for x in range(2):
                ins = dve.tensor_tensor(z[x], lbn[x][:, :, :, BLK - 1:BLK].broadcast_to([P, BATCH, NB, BLK]), lbn[x],
                                        ALU.subtract)
            done.inc(ins)
            for x in range(2):
                dve.tensor_tensor(near[x][:, KIND_K], lx8[:, x, :, HALF:BLK], end(x, HALF - 1), ALU.subtract)
                dve.tensor_tensor(near[x][:, KIND_O], lb8[:, x, :, HALF:BLK], end(x, HALF - 1), ALU.subtract)
                dve.memset(zn[x][:, :, :, HALF:BLK], 0.0)
                ins = dve.tensor_tensor(zn[x][:, :, :, 0:HALF],
                                        lbn[x][:, :, :, HALF - 1:HALF].broadcast_to([P, BATCH, NB, HALF]),
                                        lbn[x][:, :, :, 0:HALF], ALU.subtract)
            done.inc(ins)

            md = Tally(mult)
            dve.wait_ge(exped, 1)
            for i, (s, r) in enumerate(PAIR_S):
                last = md.inc(dve.tensor_tensor(f.cp[:, :, 0, i, :], f.cp[:, :, 0, i, :], u4[:, :, :, s], ALU.mult))
            dve.wait_ge(mult, last)
            for i, (s, r) in enumerate(PAIR_S):
                last = md.inc(dve.tensor_tensor(f.cp[:, :, 1, i, :], f.cp[:, :, 0, i, :],
                                                q4[:, :, r].unsqueeze(1).broadcast_to([P, 2, GROUPS]), ALU.mult))
            dve.wait_ge(mult, last)
            for i, (s, r) in enumerate(PAIR_S):
                last = md.inc(dve.tensor_tensor(f.cp[:, :, 0, i, :], f.cp[:, :, 0, i, :],
                                                k4[:, :, r].unsqueeze(1).broadcast_to([P, 2, GROUPS]), ALU.mult))
            assert last == 3 * len(PAIR_S)
            dve.wait_ge(exped, 4)
            kb = m.k[:, :].unsqueeze(1).broadcast_to([P, 2, TOK])
            qb = m.qh[:, :].unsqueeze(1).broadcast_to([P, 2, TOK])
            for x in range(2):
                last = md.inc(dve.tensor_tensor(z[x], z[x], un[x], ALU.mult))
            last = md.inc(dve.tensor_tensor(f.far[:, :, KIND_Q, :], f.far[:, :, KIND_K, :], qb, ALU.mult))
            last = md.inc(dve.tensor_tensor(f.far[:, :, KIND_O, :], f.far[:, :, KIND_O, :], m.oq[:, :, :], ALU.mult))
            dve.wait_ge(mult, last)
            last = md.inc(dve.tensor_tensor(f.far[:, :, KIND_K, :], f.far[:, :, KIND_K, :], kb, ALU.mult))
            dve.wait_ge(exped, 5)
            for x in range(2):
                last = md.inc(dve.tensor_tensor(near[x][:, KIND_Q], near[x][:, KIND_K], q8[:, :, HALF:BLK], ALU.mult))
                last = md.inc(dve.tensor_tensor(near[x][:, KIND_O], near[x][:, KIND_O], oq8[:, x, :, HALF:BLK], ALU.mult))
                last = md.inc(dve.tensor_tensor(zn[x][:, :, :, 0:HALF], zn[x][:, :, :, 0:HALF], un[x][:, :, :, 0:HALF],
                                                ALU.mult))
                dve.wait_ge(mult, last)
                last = md.inc(dve.tensor_tensor(near[x][:, KIND_K], near[x][:, KIND_K], k8[:, :, HALF:BLK], ALU.mult))
            dve.wait_ge(mult, last)

        @block.scalar
        def _(act):
            act.wait_ge(diff, 1)
            act.activation(f.cp[:, :, 0, :, :], f.cp[:, :, 0, :, :], ACT.Exp).then_inc(exped, 1)
            act.wait_ge(diff, 2)
            act.activation(f.co[:, :, :, :], f.co[:, :, :, :], ACT.Exp).then_inc(exped, 1)
            act.activation(f.far[:, :, KIND_K, :], m.lx[:, :, :], ACT.Exp)
            act.activation(f.far[:, :, KIND_O, :], m.lb[:, :, :], ACT.Exp).then_inc(exped, 1)
            act.wait_ge(diff, 3)
            act.activation(f.z[:, :, :, :, :], f.z[:, :, :, :, :], ACT.Exp).then_inc(exped, 1)
            act.activation(f.dec[:, :, :], lb8[:, :, :, BLK - 1], ACT.Exp)
            act.wait_ge(diff, 4)
            for x in range(2):
                act.activation(near[x][:, KIND_K], near[x][:, KIND_K], ACT.Exp)
                act.activation(near[x][:, KIND_O], near[x][:, KIND_O], ACT.Exp)
                ins = act.activation(zn[x][:, :, :, 0:HALF], zn[x][:, :, :, 0:HALF], ACT.Exp)
            ins.then_inc(exped, 1)
            for k, cols in enumerate(chunks):
                act.wait_ge(summed, k + 1)
                act.activation(cols, bank[k % 8][:, :], ACT.Copy).then_inc(stored, 1)

        @block.gpsimd
        def _(pool):
            done = Tally(pool_done)
            pool.wait_ge(exped, 2)
            for i, (s, r) in enumerate(PAIR_O):
                last = done.inc(pool.tensor_tensor(f.co[:, :, i, :], f.co[:, :, i, :], u4[:, :, :, s], ALU.mult))
            pool.wait_ge(pool_done, last)
            for i, (s, r) in enumerate(PAIR_O):
                last = done.inc(pool.tensor_tensor(f.co[:, :, i, :], f.co[:, :, i, :], oq4[:, :, :, r], ALU.mult))

        @block.tensor
        def _(pe):
            pe.wait_ge(mult, 3 * len(PAIR_S))
            for k, cols in enumerate(chunks):
                if k == n_cp:
                    pe.wait_ge(pool_done, 2 * len(PAIR_O))
                if k >= 8:
                    pe.wait_ge(stored, k - 7)
                pe.matmul(bank[k % 8][:, :], c.ones[:, :], cols, start=True, stop=True).then_inc(summed, 1)


def scan(nc, c, m, f, s, bank):
    acc = [bank[0:2], bank[2:4]]
    ring, errb, wtb = bank[4:6], bank[6], bank[7]
    with ExitStack() as ctx:
        def sb(name, shape):
            return ctx.enter_context(nc.sbuf_tensor(name, shape, F32))

        def sem(name):
            return ctx.enter_context(nc.semaphore(name))

        res = sb("res", [P, 2, 2, BATCH, BLK])
        w = sb("w", [P, 2, 2, BATCH, BLK])
        pred, sq = sb("pred", [P, BATCH]), sb("sqe", [P, BATCH])
        tmp1, tmp2 = sb("tmp1", [P, 4, BATCH]), sb("tmp2", [P, 4, 2, BATCH])
        tmpo = sb("tmpo", [P, 2, HALF, BATCH])

        dve_done, sq_ready, err_ready, sig_ready, w_ready = (sem("s_dve_done"), sem("s_sq_ready"), sem("s_err_ready"),
                                                             sem("s_sig_ready"), sem("s_w_ready"))
        x_done, x_out, acc_ready, acc_read = sem("s_x_done"), sem("s_x_out"), sem("s_acc_ready"), sem("s_acc_read")
        wt_ready, wt_out, z_ready, out_done, pool_done = (sem("s_wt_ready"), sem("s_wt_out"), sem("s_z_ready"),
                                                          sem("s_out_done"), sem("s_pool_done"))
        block = ctx.enter_context(nc.Block())

        v5 = m.v[:, :].rearrange("p (b n t) -> p b n t", b=BATCH, n=NB)
        sig5 = m.sig[:, :].rearrange("p (b n t) -> p b n t", b=BATCH, n=NB)
        out5 = m.out[:, :, :].rearrange("p x (b n t) -> p x b n t", b=BATCH, n=NB)
        z5 = f.z[:, :, :, :, :].rearrange("p x n b t -> p x n (b t)")
        zn5 = f.zn[:, :, :, :, :].rearrange("p x n b t -> p x n (b t)")
        far5 = f.far[:, :, :, :].rearrange("p x k (b n t) -> p x k b n t", b=BATCH, n=NB)
        near5 = f.near[:, :, :, :, :].rearrange("p x k (b n) t -> p x k b n t", b=BATCH)
        dec5 = f.dec[:, :, :].rearrange("p x (b n) -> p x b n", b=BATCH)
        cp = f.cp[:, :, :, :, :].rearrange("p x k i (b g) -> p (x k) i b g", b=BATCH)
        co = f.co[:, :, :, :].rearrange("p x i (b g) -> p x i b g", b=BATCH)
        accv = [[a[:, 0:3 * P].rearrange("p (k b t) -> p k b t", k=3, b=BATCH) for a in pair] for pair in acc]
        res4 = res[:, :, :, :, :].rearrange("p x k b t -> p (x k) b t")
        w4 = w[:, :, :, :, :].rearrange("p x k b t -> p (x k) b t")

        def items(n):
            if n == NB:
                return [[] for _ in range(BLK)]
            work = ([("cross", k, x) for k in range(n) for x in range(2)] + [("near", n, x) for x in range(2)]
                    + [("read", k, x) for k in range(n - 1) for x in range(2)])
            per = -(-len(work) // BLK)
            return [work[i * per:(i + 1) * per] for i in range(BLK)]

        def coef(n, kind, k, x):
            if kind == "cross":
                return s.cross[:, k, x, :, :, :]
            return s.near[:, n % 2, x, :, :, :]

        ring_at = {}
        for x in range(2):
            ring_at[0, "near", 0, x] = x
        for n in range(1, NB):
            for step in items(n):
                for it in step:
                    if it[0] != "read":
                        ring_at[(n,) + it] = len(ring_at)

        @block.tensor
        def _(pe):
            def product(n, kind, k, x):
                q = ring_at[n, kind, k, x]
                if q >= 2:
                    pe.wait_ge(x_out, q - 1)
                b = ring[q % 2]
                if kind == "cross":
                    pe.matmul(b[:, 0:3 * P].rearrange("p (k b t) -> p k b t", k=3, b=BATCH), z5[:, x, k, :],
                              far5[:, x, :, :, n, :], start=True, stop=True).then_inc(x_done, 1)
                else:
                    pe.matmul(b[:, 0:3 * P // 2].rearrange("p (k b t) -> p k b t", k=3, b=BATCH), zn5[:, x, n, :],
                              near5[:, x, :, :, n, :], start=True, stop=True).then_inc(x_done, 1)

            def read_far(n, k, x):
                pe.wait_ge(x_out, ring_at[n, "cross", k, x] + 1)
                if k == 0 and n >= 2:
                    pe.wait_ge(acc_read, 2 * (n - 1))
                return pe.matmul(accv[n % 2][x], s.wt[:, k, x, :], s.cross[:, k, x, :, :, :],
                                 start=(k == 0), stop=(k == n - 1), skip_group_check=True)

            def turn_w(n, h):
                pe.wait_ge(w_ready, BLK * n + HALF * (h + 1))
                if 2 * n + h >= 1:
                    pe.wait_ge(wt_out, 2 * n + h)
                for x in range(2):
                    ins = pe.transpose(wtb[:, x * P:(x + 1) * P], w[:, x, 0, :, :].rearrange("p b t -> p (b t)"),
                                       c.ident[:, :])
                ins.then_inc(wt_ready, 1)
                pe.wait_ge(wt_out, 2 * n + h + 1)

            for x in range(2):
                product(0, "near", 0, x)
            for n in range(NB):
                work = items(n + 1)
                if 1 <= n < NB - 1:
                    zwait = n
                else:
                    zwait = 0
                for t in range(BLK):
                    T = BLK * n + t
                    pe.wait_ge(sq_ready, T + 1)
                    pe.matmul(errb[:, 0:BATCH], c.ones[:, :], sq[:, :], start=True, stop=True).then_inc(err_ready, 1)
                    if t == 0 and zwait:
                        pe.wait_ge(z_ready, zwait)
                    for kind, k, x in work[t]:
                        if kind == "read":
                            read_far(n + 1, k, x)
                        else:
                            product(n + 1, kind, k, x)
                    if t == HALF - 1:
                        turn_w(n, 0)
                        pe.wait_ge(acc_read, 2 * n + 1)
                        for x in range(2):
                            pe.wait_ge(x_out, ring_at[n, "near", n, x] + 1)
                            ins = pe.matmul(accv[n % 2][x][:, :, :, HALF:BLK], s.wt[:, n, x, :],
                                            s.near[:, n % 2, x, :, :, :], start=(n == 0), stop=True,
                                            skip_group_check=True)
                        ins.then_inc(acc_ready, 1)
                    if t == BLK - 1 and n < NB - 1:
                        turn_w(n, 1)
                        for x in range(2):
                            ins = read_far(n + 1, n, x)
                        ins.then_inc(acc_ready, 1)

        @block.scalar
        def _(act):
            for n in range(NB):
                for t in range(BLK):
                    act.wait_ge(err_ready, BLK * n + t + 1)
                    act.activation(sig5[:, :, n, t], errb[:, 0:BATCH], ACT.Sigmoid, scale=1.0 / (1.0 + 1e-6)
                                   ).then_inc(sig_ready, 1)
                    if t in (HALF - 1, BLK - 1) and (n < NB - 1 or t < BLK - 1):
                        act.wait_ge(wt_ready, 2 * n + t // HALF + 1)
                        act.activation(s.wt[:, n, :, :].rearrange("p x v -> p (x v)"), wtb[:, 0:2 * P], ACT.Copy
                                       ).then_inc(wt_out, 1)

        @block.gpsimd
        def _(pool):
            done = Tally(pool_done)
            last = done.inc(pool.memset(m.out[:, :, :], 0.0))
            pool.wait_ge(pool_done, last)
            pool.sem_inc(out_done, 1)
            for n in range(NB):
                if 1 <= n < NB - 1:
                    pool.wait_ge(x_done, max(q for key, q in ring_at.items() if key[0] == n) + 1)
                    for x in range(2):
                        zb = f.z[:, x, 0:n, :, :]
                        ins = pool.tensor_tensor(zb, zb, dec5[:, x, :, n].unsqueeze(1).unsqueeze(3)
                                                 .broadcast_to([P, n, BATCH, BLK]), ALU.mult)
                        last = done.inc(ins)
                    pool.wait_ge(pool_done, last)
                    pool.sem_inc(z_ready, 1)
                for t in range(BLK):
                    h, s0 = divmod(t, HALF)
                    i0 = PAIR_O.index((s0, s0))
                    cnt = HALF - s0
                    pool.wait_ge(w_ready, BLK * n + t + 1)
                    last = done.inc(pool.tensor_tensor(
                        tmpo[:, :, 0:cnt, :], co[:, :, i0:i0 + cnt, :, 2 * n + h],
                        w[:, :, 0, :, t].unsqueeze(2).broadcast_to([P, 2, cnt, BATCH]), ALU.mult))
                    pool.wait_ge(pool_done, last)
                    o = out5[:, :, :, n, t:HALF * (h + 1)].rearrange("p x b t -> p x t b")
                    last = done.inc(pool.tensor_tensor(o, o, tmpo[:, :, 0:cnt, :], ALU.add))
                    pool.wait_ge(pool_done, last)
                    pool.sem_inc(out_done, 1)

        @block.vector
        def _(dve):
            done = Tally(dve_done)

            def then(ins):
                dve.wait_ge(dve_done, done.inc(ins))

            def store_coefs(n, kind, k, x):
                q = ring_at[n, kind, k, x]
                dve.wait_ge(x_done, q + 1)
                width = BLK if kind == "cross" else HALF
                src = ring[q % 2][:, 0:3 * BATCH * width].rearrange("p (k b t) -> p k b t", k=3, b=BATCH)
                own = c.batch_mask[:, :].unsqueeze(1).unsqueeze(3).broadcast_to([P, 3, BATCH, width])
                dve.tensor_tensor(coef(n, kind, k, x), src, own, ALU.mult).then_inc(x_out, 1)

            then(dve.memset(w[:, :, :, :, :], 0.0))
            for x in range(2):
                store_coefs(0, "near", 0, x)
            for n in range(NB):
                work = items(n + 1)
                for t in range(BLK):
                    T = BLK * n + t
                    h, r = divmod(t, HALF)
                    lo, hi = HALF * h, HALF * (h + 1)
                    if r == 0:
                        vh = v5[:, :, n, lo:hi]
                        if T == 0:
                            done.inc(dve.tensor_copy(res[:, 0, :, :, lo:hi], vh.unsqueeze(1).broadcast_to([P, 2, BATCH, HALF])))
                            done.inc(dve.tensor_copy(res[:, 1, 0, :, lo:hi], vh))
                            done.inc(dve.memset(res[:, 1, 1, :, lo:hi], 0.0))
                        else:
                            dve.wait_ge(acc_ready, 2 * n + h)
                            a = accv[n % 2]
                            done.inc(dve.tensor_tensor(res[:, 0, :, :, lo:hi], vh.unsqueeze(1).broadcast_to([P, 2, BATCH, HALF]),
                                                       a[0][:, 0:2, :, lo:hi], ALU.subtract))
                            done.inc(dve.tensor_tensor(res[:, 1, 0, :, lo:hi], vh, a[1][:, 0, :, lo:hi], ALU.subtract))
                            done.inc(dve.tensor_scalar(res[:, 1, 1, :, lo:hi], a[1][:, 1, :, lo:hi], -1.0, None, ALU.mult))
                        dve.wait_ge(dve_done, done.n)
                    else:
                        i = PAIR_S.index((r - 1, r))
                        then(dve.tensor_tensor(tmp1[:, :, :], cp[:, :, i, :, 2 * n + h], w4[:, :, :, t - 1], ALU.mult))
                        then(dve.tensor_tensor(res4[:, :, :, t], res4[:, :, :, t], tmp1[:, :, :], ALU.subtract))
                    then(dve.tensor_tensor(pred[:, :], res[:, 0, 1, :, t], res[:, 1, 1, :, t], ALU.add))
                    if T:
                        dve.wait_ge(err_ready, T)
                    dve.tensor_tensor(sq[:, :], pred[:, :], pred[:, :], ALU.mult).then_inc(sq_ready, 1)
                    if r == 0:
                        if T:
                            dve.wait_ge(out_done, 1)
                            for x in range(2):
                                done.inc(dve.tensor_copy(out5[:, x, :, n, lo:hi], accv[n % 2][x][:, KIND_O, :, lo:hi]))
                            dve.wait_ge(dve_done, done.n)
                        dve.sem_inc(acc_read, 1)
                    elif r < HALF - 1:
                        cnt = HALF - 1 - r
                        i = PAIR_S.index((r - 1, r + 1))
                        later = res4[:, :, :, t + 1:hi].rearrange("p c b t -> p c t b")
                        then(dve.tensor_tensor(tmp2[:, :, 0:cnt, :], cp[:, :, i:i + cnt, :, 2 * n + h],
                                               w4[:, :, :, t - 1].unsqueeze(2).broadcast_to([P, 4, cnt, BATCH]), ALU.mult))
                        done.inc(dve.tensor_tensor(later, later, tmp2[:, :, 0:cnt, :], ALU.subtract))
                    for it in work[t]:
                        if it[0] != "read":
                            store_coefs(n + 1, *it)
                    dve.wait_ge(sig_ready, T + 1)
                    dve.wait_ge(dve_done, done.n)
                    if T >= BLK:
                        dve.wait_ge(out_done, T - BLK + 2)
                    ins = dve.tensor_tensor(w[:, :, :, :, t], res[:, :, 0, :, t].unsqueeze(2).broadcast_to([P, 2, 2, BATCH]),
                                            sig5[:, :, n, t].unsqueeze(1).unsqueeze(1).broadcast_to([P, 2, 2, BATCH]), ALU.mult)
                    ins.then_inc(w_ready, 1)
                    dve.wait_ge(w_ready, T + 1)


def memory_output(nc, io, c, t, m, bank):
    with ExitStack() as ctx:
        def sem(name):
            return ctx.enter_context(nc.semaphore(name))

        wo = ctx.enter_context(nc.sbuf_tensor("wo", [P, DM], F32))
        nw = ctx.enter_context(nc.sbuf_tensor("nw", [P, 1], F32))
        tmp = ctx.enter_context(nc.sbuf_tensor("mo_tmp", [P, TOK], F32))
        keep = ctx.enter_context(nc.sbuf_tensor("mo_keep", [P, TOK], F32))
        w_in, dve_done, sq_ready, summed, rooted = (sem("o_w_in"), sem("o_dve_done"), sem("o_sq_ready"), sem("o_summed"),
                                                    sem("o_rooted"))
        normed, projected, var_ready, std_ready = sem("o_normed"), sem("o_projected"), sem("o_var_ready"), sem("o_std_ready")
        y_ready, turned, moved = sem("o_y_ready"), sem("o_turned"), sem("o_moved")
        block = ctx.enter_context(nc.Block())

        @block.sync
        def _(sp):
            sp.dma_start(wo[:, :], io["Wo"]).then_inc(w_in, 16)
            sp.dma_start(nw[:, :], io["norm_w"]).then_inc(w_in, 16)
            sp.wait_ge(w_in, 32)

        @block.vector
        def _(dve):
            done = Tally(dve_done)

            def then(ins):
                dve.wait_ge(dve_done, done.inc(ins))

            then(dve.tensor_scalar(tmp[:, :], m.sig[:, :], 0.7, 0.1, ALU.is_gt, ALU.mult))
            then(dve.tensor_scalar(keep[:, :], tmp[:, :], -1.0, 1.0, ALU.mult, ALU.add))
            then(dve.memset(keep[:, :].rearrange("p (b t) -> p b t", t=STEPS)[:, :, 0], 0.0))
            then(dve.tensor_tensor(m.nu[:, :], m.nu[:, :], tmp[:, :], ALU.mult))
            then(dve.tensor_tensor_scan(tmp[:, :], keep[:, :], m.nu[:, :], 0.0, ALU.mult, ALU.add))
            then(dve.tensor_tensor(tmp[:, :], tmp[:, :], m.pw2[:, :], ALU.mult))
            then(dve.tensor_tensor(tmp[:, :], tmp[:, :], m.out[:, 0, :], ALU.add))
            then(dve.tensor_tensor(tmp[:, :], tmp[:, :], m.out[:, 1, :], ALU.add))
            dve.tensor_tensor(m.sig[:, :], tmp[:, :], tmp[:, :], ALU.mult).then_inc(sq_ready, 1)
            dve.wait_ge(w_in, 32)
            for h in range(2):
                dve.wait_ge(summed, h + 1)
                done.inc(dve.tensor_scalar(keep[:, 512 * h:512 * h + 512], bank[h][:, :], 1.0 / DS, 1e-6, ALU.mult, ALU.add))
            dve.wait_ge(dve_done, done.n)
            dve.sem_inc(sq_ready, 1)
            dve.wait_ge(rooted, 1)
            then(dve.reciprocal(keep[:, :], keep[:, :]))
            dve.scalar_tensor_tensor(out=tmp[:, :], in0=tmp[:, :], scalar=nw[:, 0:1], in1=keep[:, :],
                                     op0=ALU.mult, op1=ALU.mult).then_inc(normed, 1)
            for n in range(TILES):
                dve.wait_ge(projected, n + 1)
                last = done.inc(dve.tensor_tensor(t.x[:, n, :], bank[n][:, 0:DM], t.x[:, n, :], ALU.add))
            dve.wait_ge(dve_done, last)
            last = row_stats(dve, t, t.x, done)
            dve.wait_ge(dve_done, last)
            dve.sem_inc(var_ready, 1)
            dve.wait_ge(std_ready, 1)
            last = normalise(dve, t, t.y, t.x, done)
            dve.wait_ge(dve_done, last)
            dve.sem_inc(y_ready, 1)
            for n in range(TILES):
                dve.wait_ge(turned, n + 1)
                dve.tensor_copy(t.yT[:, :, n * P:(n + 1) * P],
                                bank[n][:, 0:DM].rearrange("p (j q) -> p j q", j=CI)).then_inc(moved, 1)

        @block.scalar
        def _(act):
            act.wait_ge(sq_ready, 2)
            act.activation(keep[:, :], keep[:, :], ACT.Sqrt).then_inc(rooted, 1)
            act.wait_ge(var_ready, 1)
            act.activation(t.std[:, :], t.var[:, :], ACT.Sqrt).then_inc(std_ready, 1)

        @block.tensor
        def _(pe):
            pe.wait_ge(sq_ready, 1)
            for h in range(2):
                pe.matmul(bank[h][:, :], c.ones[:, :], m.sig[:, 512 * h:512 * h + 512], start=True, stop=True
                          ).then_inc(summed, 1)
            pe.wait_ge(w_in, 32)
            pe.wait_ge(normed, 1)
            for n in range(TILES):
                pe.matmul(bank[n][:, 0:DM], tmp[:, n * P:(n + 1) * P], wo[:, :], start=True, stop=True).then_inc(projected, 1)
            pe.wait_ge(y_ready, 1)
            for n in range(TILES):
                for i in range(CI):
                    ins = pe.transpose(bank[n][:, i * P:(i + 1) * P], t.y[:, n, i * P:(i + 1) * P], c.ident[:, :])
                ins.then_inc(turned, 1)


EXPERTS, EW, TOPK = 64, 96, 8
SLABS = EXPERTS * EW // P
CW_GROUP = 32
CW_COPIES = EW // CW_GROUP
CW_ROWS = P // CW_GROUP
UNITS = 2


def route(nc, io, c, t, cw_rows, bank):
    with ExitStack() as ctx:
        def sb(name, shape):
            return ctx.enter_context(nc.sbuf_tensor(name, shape, F32))

        def sem(name):
            return ctx.enter_context(nc.semaphore(name))

        rw, prob, rest = sb("rw", [P, CI, EXPERTS]), sb("r_prob", [P, TILES, EXPERTS]), sb("r_rest", [P, TILES, EXPERTS])
        top, cwT = sb("r_top", [P, TILES, TOPK]), sb("cwT", [EXPERTS, TOK])
        neg, den, sum8 = sb("r_neg", [P, TILES]), sb("r_den", [P, TILES]), sb("r_sum8", [P, TILES])
        w_in, routed, neg_ready, exped, dve_done = sem("r_w_in"), sem("r_routed"), sem("r_neg_ready"), sem("r_exped"), sem("r_dve_done")
        chosen, turned, moved, stored = sem("r_chosen"), sem("r_turned"), sem("r_moved"), sem("r_stored")
        block = ctx.enter_context(nc.Block())

        @block.sync
        def _(sp):
            sp.dma_start(rw[:, :, :], io["routerT"].rearrange("(i p) e -> p i e", p=P)).then_inc(w_in, 16)
            sp.wait_ge(moved, 2)
            for k in range(CW_COPIES):
                sp.dma_start(cw_rows.rearrange("(e k) t -> k e t", k=CW_COPIES)[k], cwT[:, :]).then_inc(stored, 16)
            sp.wait_ge(stored, 16 * CW_COPIES)

        @block.tensor
        def _(pe):
            pe.wait_ge(w_in, 16)
            for n in range(TILES):
                for i in range(CI):
                    ins = pe.matmul(bank[n][:, 0:EXPERTS], t.yT[:, i, n * P:(n + 1) * P], rw[:, i, :],
                                    start=(i == 0), stop=(i == CI - 1))
                ins.then_inc(routed, 1)
            pe.wait_ge(chosen, 1)
            for n in range(TILES):
                ins = pe.transpose(bank[n // 4][0:EXPERTS, (n % 4) * P:(n % 4 + 1) * P], prob[:, n, :], c.ident[:, :])
                if n % 4 == 3:
                    ins.then_inc(turned, 1)

        @block.scalar
        def _(act):
            for n in range(TILES):
                act.wait_ge(neg_ready, n + 1)
                act.activation(prob[:, n, :], bank[n][:, 0:EXPERTS], ACT.Exp, bias=neg[:, n:n + 1],
                               accum_out=den[:, n:n + 1]).then_inc(exped, 1)

        @block.vector
        def _(dve):
            done = Tally(dve_done)

            def then(ins):
                dve.wait_ge(dve_done, done.inc(ins))

            for n in range(TILES):
                dve.wait_ge(routed, n + 1)
                dve.tensor_reduce(neg[:, n:n + 1], bank[n][:, 0:EXPERTS], AX.X, ALU.max, negate=True).then_inc(neg_ready, 1)
            dve.wait_ge(exped, TILES)
            then(dve.reciprocal(den[:, :], den[:, :]))
            for n in range(TILES):
                done.inc(dve.tensor_scalar(prob[:, n, :], prob[:, n, :], den[:, n:n + 1], None, ALU.mult))
            dve.wait_ge(dve_done, done.n)
            for n in range(TILES):
                done.inc(dve.max(top[:, n, :], prob[:, n, :]))
            dve.wait_ge(dve_done, done.n)
            for n in range(TILES):
                done.inc(dve.match_replace(rest[:, n, :], top[:, n, :], prob[:, n, :], 0.0))
            dve.wait_ge(dve_done, done.n)
            done.inc(dve.tensor_tensor(prob[:, :, :], prob[:, :, :], rest[:, :, :], ALU.subtract))
            then(dve.tensor_reduce(sum8[:, :], top[:, :, :], AX.X, ALU.add))
            then(dve.reciprocal(sum8[:, :], sum8[:, :]))
            for n in range(TILES):
                done.inc(dve.tensor_scalar(prob[:, n, :], prob[:, n, :], sum8[:, n:n + 1], None, ALU.mult))
            dve.wait_ge(dve_done, done.n)
            dve.sem_inc(chosen, 1)
            for k in range(2):
                dve.wait_ge(turned, k + 1)
                dve.tensor_copy(cwT[:, 512 * k:512 * k + 512], bank[k][0:EXPERTS, :]).then_inc(moved, 1)


def experts(nc, io, c, t, cw_rows, bank):
    acc = bank[0:4]
    gate, up = bank[4:6], bank[6:8]
    WS, XS, HS = 64.0, 64.0, 16.0
    with ExitStack() as ctx:
        def sb(name, shape, dt=F32):
            return ctx.enter_context(nc.sbuf_tensor(name, shape, dt))

        def sem(name):
            return ctx.enter_context(nc.semaphore(name))

        wgu = [sb(f"wgu{u}", [P, CI, 2, P]) for u in range(2)]
        wd = [sb(f"wd{u}", [P, DM]) for u in range(2)]
        wgu_hl = [[sb(f"wgu{part}{u}", [P, CI, 2, P], F16) for part in "hl"] for u in range(2)]
        wd_hl = [[sb(f"wd{part}{u}", [P, DM], F16) for part in "hl"] for u in range(2)]
        x_hl = [sb(f"xT{part}", [P, CI, TOK], F16) for part in "hl"]
        cw = [sb(f"cw{u}", [P, TOK]) for u in range(2)]
        silu = [sb(f"silu{h}", [P, 512]) for h in range(2)]
        upw = [sb(f"upw{h}", [P, 512]) for h in range(2)]
        hid = [sb(f"hid{h}", [P, 512]) for h in range(2)]
        hid_hl = [[sb(f"hid{part}{h}", [P, 512], F16) for part in "hl"] for h in range(2)]
        zeros = sb("zeros", [P, P], F16)
        w_in, cw_in = [sem(f"e_w_in{u}") for u in range(2)], [sem(f"e_cw_in{u}") for u in range(2)]
        zeroed, gated, upped, silued, weighted, hid_ready = (sem("e_zeroed"), sem("e_gated"), sem("e_upped"), sem("e_silued"),
                                                             sem("e_weighted"), sem("e_hid_ready"))
        x_high, x_low, w_high, w_low, hid_high, hid_low = (sem("e_x_high"), sem("e_x_low"), sem("e_w_high"), sem("e_w_low"),
                                                           sem("e_hid_high"), sem("e_hid_low"))
        down_done, out_ready, out_sent = sem("e_down_done"), sem("e_out_ready"), sem("e_out_sent")
        block = ctx.enter_context(nc.Block())

        def load(sp, e, u):
            one = bass.ds(e, 1)
            sp.dma_start(wgu[u][:, :, :, :], io["guT"][one].rearrange("o p i g w -> p (o i) g w")).then_inc(w_in[u], 16)
            sp.dma_start(wd[u][:, :], io["downT"][one].rearrange("o w d -> (o w) d")).then_inc(w_in[u], 16)
            for k in range(CW_ROWS):
                sp.dma_start(cw[u][k * CW_GROUP:(k + 1) * CW_GROUP, :],
                             cw_rows[bass.ds(e * CW_ROWS + k, 1), :].broadcast_to([CW_GROUP, TOK])).then_inc(cw_in[u], 16)

        @block.sync
        def _(sp):
            load(sp, 0, 0)
            load(sp, 1, 1)
            with sp.Fori(0, SLABS // 2 - 1) as i:
                for u in range(2):
                    sp.wait_ge(w_low, 4 * i + 2 * u + 2)
                    sp.wait_ge(weighted, 4 * i + 2 * u + 2)
                    load(sp, 2 * i + u + 2, u)
            for n in range(TILES // 2):
                sp.wait_ge(out_ready, 2 * n + 2)
                sp.dma_start(io["out"].rearrange("b t d -> (b t) d").rearrange("(n p) d -> p n d", p=P)[:, 2 * n:2 * n + 2, :],
                             t.x[:, 2 * n:2 * n + 2, :]).then_inc(out_sent, 16)
            sp.wait_ge(out_sent, 16 * TILES // 2)

        @block.gpsimd
        def _(pool):
            pool.memset(zeros[:, :], 0.0).then_inc(zeroed, 1)

        @block.tensor
        def _(pe):
            def gate_up(q, r, first=False):
                u, h = (r // 2) % 2, r % 2
                if h == 0:
                    pe.wait_ge(w_low, q + 2)
                if not first:
                    pe.wait_ge(hid_ready, q - 1)
                cols = slice(512 * h, 512 * h + 512)
                for g, (dst, done) in enumerate(((gate[h], gated), (up[h], upped))):
                    terms = [(a, b, i) for a, b in ((0, 0), (0, 1), (1, 0)) for i in range(CI)]
                    for k, (a, b, i) in enumerate(terms):
                        ins = pe.matmul(dst[:, :], wgu_hl[u][a][:, i, g, :], x_hl[b][:, i, cols],
                                        start=(k == 0), stop=(k == len(terms) - 1))
                    ins.then_inc(done, 1)

            def down(q, r):
                u, h = (r // 2) % 2, r % 2
                pe.wait_ge(hid_low, q + 1)
                for k in range(4):
                    n = 4 * h + k
                    for a, b in ((0, 0), (0, 1), (1, 0)):
                        ins = pe.matmul(acc[n // 2][:, (n % 2) * DM:(n % 2 + 1) * DM], hid_hl[h][a][:, k * P:(k + 1) * P],
                                        wd_hl[u][b][:, :], start=False, stop=True, skip_group_check=True)
                ins.then_inc(down_done, 1)

            pe.wait_ge(zeroed, 1)
            pe.wait_ge(x_low, 1)
            for a in acc:
                pe.matmul(a[:, :], zeros[:, :], x_hl[0][:, 0, 0:512], start=True, stop=True)
            gate_up(0, 0, True)
            gate_up(1, 1, True)
            down(0, 0)
            with pe.Fori(0, SLABS // 2 - 1) as i:
                for r in range(4):
                    gate_up(4 * i + r + 2, r + 2)
                    down(4 * i + r + 1, r + 1)
            last = 2 * SLABS - 4
            for r in range(2):
                gate_up(last + r + 2, r + 2)
                down(last + r + 1, r + 1)
            down(last + 3, 3)

        @block.scalar
        def _(act):
            def split_weights(e, u, loads, first):
                act.wait_ge(w_in[u], 32 * loads)
                if not first:
                    act.wait_ge(down_done, 2 * e - 2)
                act.activation(wgu_hl[u][0][:, :, :, :], wgu[u][:, :, :, :], ACT.Copy, scale=WS).then_inc(w_high, 1)
                act.activation(wd_hl[u][0][:, :], wd[u][:, :], ACT.Copy, scale=WS).then_inc(w_high, 1)

            def unit(q, r, first=False):
                h = r % 2
                act.wait_ge(gated, q + 1)
                if not first:
                    act.wait_ge(hid_ready, q - 1)
                act.activation(silu[h][:, :], gate[h][:, :], ACT.Silu, scale=1.0 / (WS * XS)).then_inc(silued, 1)
                act.wait_ge(hid_ready, q + 1)
                if not first:
                    act.wait_ge(down_done, q - 1)
                act.activation(hid_hl[h][0][:, :], hid[h][:, :], ACT.Copy).then_inc(hid_high, 1)

            act.activation(x_hl[0][:, :, :], t.yT[:, :, :], ACT.Copy, scale=XS).then_inc(x_high, 1)
            split_weights(0, 0, 1, True)
            split_weights(1, 1, 1, True)
            for r in range(2):
                unit(r, r, True)
            with act.Fori(0, SLABS // 2 - 1) as i:
                for u in range(2):
                    unit(4 * i + 2 * u + 2, 2)
                    split_weights(2 * i + 2 + u, u, i + 2, False)
                    unit(4 * i + 2 * u + 3, 3)
            for r in range(2, 4):
                unit(2 * SLABS - 4 + r, r)

        @block.vector
        def _(dve):
            def split_weights(e, u):
                for k, (w, hl) in enumerate(((wgu, wgu_hl), (wd, wd_hl))):
                    dve.wait_ge(w_high, 2 * e + k + 1)
                    if k == 0:
                        src, high, low = w[u][:, :, :, :], hl[u][0][:, :, :, :], hl[u][1][:, :, :, :]
                        src, high, low = (a.rearrange("p i g w -> p (i g w)") for a in (src, high, low))
                    else:
                        src, high, low = w[u][:, :], hl[u][0][:, :], hl[u][1][:, :]
                    dve.scalar_tensor_tensor(out=low, in0=src, scalar=WS, in1=high, op0=ALU.mult,
                                             op1=ALU.subtract).then_inc(w_low, 1)

            def unit(q, r, loads, first=False):
                u, h = (r // 2) % 2, r % 2
                if h == 0:
                    dve.wait_ge(cw_in[u], 16 * CW_ROWS * loads)
                dve.wait_ge(upped, q + 1)
                if not first:
                    dve.wait_ge(hid_ready, q - 1)
                dve.scalar_tensor_tensor(out=upw[h][:, :], in0=up[h][:, :], scalar=HS / (WS * XS),
                                         in1=cw[u][:, 512 * h:512 * h + 512], op0=ALU.mult, op1=ALU.mult
                                         ).then_inc(weighted, 1)
                dve.wait_ge(weighted, q + 1)
                dve.wait_ge(silued, q + 1)
                if not first:
                    dve.wait_ge(hid_low, q - 1)
                dve.tensor_tensor(hid[h][:, :], upw[h][:, :], silu[h][:, :], ALU.mult).then_inc(hid_ready, 1)

            def low(q, r):
                h = r % 2
                dve.wait_ge(hid_high, q + 1)
                dve.tensor_tensor(hid_hl[h][1][:, :], hid[h][:, :], hid_hl[h][0][:, :], ALU.subtract).then_inc(hid_low, 1)

            dve.wait_ge(x_high, 1)
            dve.scalar_tensor_tensor(out=x_hl[1][:, :, :].rearrange("p i n -> p (i n)"),
                                     in0=t.yT[:, :, :].rearrange("p i n -> p (i n)"), scalar=XS,
                                     in1=x_hl[0][:, :, :].rearrange("p i n -> p (i n)"), op0=ALU.mult, op1=ALU.subtract
                                     ).then_inc(x_low, 1)
            split_weights(0, 0)
            split_weights(1, 1)
            for r in range(2):
                unit(r, r, 1, True)
                low(r, r)
            with dve.Fori(0, SLABS // 2 - 1) as i:
                for u in range(2):
                    q = 4 * i + 2 * u + 2
                    unit(q, 2 + 2 * u, i + 1 + u)
                    low(q, 0)
                    split_weights(2 * i + 2 + u, u)
                    unit(q + 1, 3 + 2 * u, i + 1 + u)
                    low(q + 1, 1)
            for r in range(2, 4):
                unit(2 * SLABS - 4 + r, r, SLABS // 2)
                low(2 * SLABS - 4 + r, r)
            dve.wait_ge(down_done, 2 * SLABS)
            for n in range(TILES):
                dve.scalar_tensor_tensor(out=t.x[:, n, :], in0=acc[n // 2][:, (n % 2) * DM:(n % 2 + 1) * DM],
                                         scalar=1.0 / (WS * HS), in1=t.x[:, n, :], op0=ALU.mult, op1=ALU.add
                                         ).then_inc(out_ready, 1)


def store_rows(nc, src, dst):
    with nc.semaphore("st_out") as st_out, nc.Block() as block:
        @block.sync
        def _(sp):
            sp.dma_start(dst.rearrange("b t d -> (b t) d").rearrange("(n p) d -> p n d", p=P), src[:, :, :]
                         ).then_inc(st_out, 16)
            sp.wait_ge(st_out, 16)


def perceiver_layer(nc, io, upto=9):
    with ExitStack() as ctx:
        def sb(name, shape):
            return ctx.enter_context(nc.sbuf_tensor(name, shape, F32))

        bank = [ctx.enter_context(nc.psum_tensor(f"bank{n}", [P, 512], F32)) for n in range(8)]
        t = Named()
        t.x = sb("x", [P, TILES, DM])
        t.y = sb("y", [P, TILES, DM])
        t.yT = sb("yT", [P, CI, TOK])
        t.stat = sb("stat", [P, TILES, 6])
        t.mv = sb("mv", [P, TILES, 2])
        t.var = sb("var", [P, TILES])
        t.std = sb("std", [P, TILES])
        t.rstd = sb("rstd", [P, TILES])
        t.amax = sb("amax", [P, TILES])
        t.qs = sb("qs", [P, TILES])
        t.qr = sb("qr", [P, TILES])
        c = Named()
        c.ident = sb("ident", [P, P])
        c.ones = sb("ones", [P, P])
        c.batch_mask = sb("batch_mask", [P, BATCH])
        with ExitStack() as xa:
            def xb(name, shape, dt=F32):
                return xa.enter_context(nc.sbuf_tensor(name, shape, dt))
            c.head_mask = xb("head_mask", [P, HG])
            c.pair_mask = xb("pair_mask", [P, 2, 2, DH])
            c.gather = xb("gather", [P, 3 * STEPS])
            c.w_hl = [xb(f"wkv{part}", [P, CI, 2 * DM], F16) for part in "hl"]
            c.q_hl = [xb(f"qT{part}", [P, CI, TOK], F16) for part in "hl"]
            c.wqT = xb("wqT", [P, CI, DM])
            c.wpT = xb("wpT", [P, CI, DM])
            c.bq, c.bk = xb("bq", [P, CI]), xb("bk", [P, CI])
            c.bv, c.bp = xb("bv", [P, DM]), xb("bp", [P, DM])
            t.o = xb("o", [P, BATCH, PAIRS, 2 * DH])
            with ExitStack() as wa:
                t.wq = wa.enter_context(nc.sbuf_tensor("wq", [P, CI, DM], F32))
                t.wp = wa.enter_context(nc.sbuf_tensor("wp", [P, CI, DM], F32))
                t.wkvT = wa.enter_context(nc.sbuf_tensor("wkvT", [P, CI, 2 * DM], F32))
                t.qT = wa.enter_context(nc.sbuf_tensor("qT", [P, CI, TOK], F32))
                queries(nc, io, c, t, bank)
            attention(nc, io, c, t, bank)
            project_attention(nc, io, c, t, bank)
        if upto == 3:
            store_rows(nc, t.x, io["out"])
            return
        with ExitStack() as me:
            def mb(name, shape):
                return me.enter_context(nc.sbuf_tensor(name, shape, F32))
            m = Named()
            m.v = mb("v", [P, TOK])
            m.nu = mb("nu", [P, TOK])
            m.sig = mb("sig", [P, TOK])
            m.pw2 = mb("pw2", [P, TOK])
            m.out = mb("out", [P, 2, TOK])
            with ExitStack() as sc:
                room = sc.enter_context(nc.sbuf_tensor("room", [P, 10 * TOK], F32))
                place = 0

                def carve(pattern, size, **dims):
                    nonlocal place
                    place += size
                    return room[:, place - size:place].rearrange(pattern, **dims)

                m.k, m.qh = carve("p (a t) -> p (a t)", TOK, a=1), carve("p (a t) -> p (a t)", TOK, a=1)
                m.oq, m.lb, m.lx, m.u = [carve("p (x t) -> p x t", 2 * TOK, x=2) for _ in range(4)]
                features(nc, io, c, t, m, bank)

                def fb(name, shape):
                    return sc.enter_context(nc.sbuf_tensor(name, shape, F32))
                f = Named()
                f.cp = fb("cp", [P, 2, 2, len(PAIR_S), GROUPS])
                f.co = fb("co", [P, 2, len(PAIR_O), GROUPS])
                f.far = fb("far", [P, 2, 3, TOK])
                f.near = fb("near", [P, 2, 3, TOK // BLK, HALF])
                f.z = fb("z", [P, 2, NB, BATCH, BLK])
                f.zn = fb("zn", [P, 2, NB, BATCH, BLK])
                f.dec = fb("dec", [P, 2, TOK // BLK])
                factors(nc, c, m, f, bank)
                place = 0
                s = Named()
                s.cross = carve("p (k x i b t) -> p k x i b t", (NB - 1) * 2 * 3 * P, k=NB - 1, x=2, i=3, b=BATCH)
                s.wt = carve("p (k x v) -> p k x v", NB * 2 * P, k=NB, x=2)
                s.near = carve("p (u x i b t) -> p u x i b t", 2 * 2 * 3 * P // 2, u=2, x=2, i=3, b=BATCH)
                scan(nc, c, m, f, s, bank)
            memory_output(nc, io, c, t, m, bank)
        if upto == 7:
            store_rows(nc, t.x, io["out"])
            return
        cw_rows = nc.dram_tensor("cw_rows", [CW_COPIES * EXPERTS, TOK], F32, kind="Internal").ap()
        route(nc, io, c, t, cw_rows, bank)
        experts(nc, io, c, t, cw_rows, bank)


def layout(inputs):
    import numpy as np
    a = {k: np.asarray(v) for k, v in inputs.items()}
    X, A, F = "L0_xattn_", "L0_attn_", "L0_ffn_"
    return {
        "x": a["x"],
        "ctxT": a["ctx_2048"].transpose(0, 2, 1),
        "wq": a[X + "wq"], "wp": a[X + "wp"],
        "wkvT": a[X + "wkv"].T,
        "bqT": a[X + "bq"].reshape(CI, P).T,
        "bkvT": a[X + "bkv"][:DM].reshape(CI, P).T,
        "bv": a[X + "bkv"][DM:], "bp": a[X + "bp"],
        "Wk": a[A + "Wk"], "Wv": a[A + "Wv"], "Wq": a[A + "Wq"], "Waf": a[A + "Waf"], "Was": a[A + "Was"],
        "Wir": a[A + "ir_w1"], "ir_w2": a[A + "ir_w2"], "ir_b2": a[A + "ir_b2"],
        "pw_w": a[A + "pw_w"], "pw_b": a[A + "pw_b"], "nm_w1": a[A + "nm_w1"], "nm_w2": a[A + "nm_w2"],
        "cols6": np.stack([a[A + "baf"], a[A + "bas"], a[A + "ir_b1"], *a[A + "nm_b1"].reshape(2, P), a[A + "nm_b2"]], 1),
        "lam": np.stack([a[A + "fast_lambda"], a[A + "slow_lambda"]], 1),
        "Wo": a[A + "Wo"], "norm_w": a[A + "norm_w"].reshape(P, 1),
        "routerT": a[F + "router_w"].T,
        "guT": np.stack([a[F + n].reshape(SLABS, P, CI, P).transpose(0, 3, 2, 1) for n in ("gate_w", "up_w")], 3),
        "downT": a[F + "down_w"].transpose(0, 2, 1).reshape(SLABS, P, DM),
    }


def kernel(**inputs):
    import numpy as np
    import concourse.bacc as bacc
    from concourse.bass_utils import run_bass_kernel_spmd

    nc = bacc.Bacc("TRN2", target_bir_lowering=False, num_devices=1)
    arrays, io = {}, {}
    for name, a in layout(inputs).items():
        a = np.ascontiguousarray(a)
        arrays[f"in_{name}_dram"] = a
        io[name] = nc.dram_tensor(f"in_{name}_dram", a.shape, mybir.dt.from_np(a.dtype), kind="ExternalInput").ap()
    io["out"] = nc.dram_tensor("out_0_dram", (BATCH, STEPS, DM), F32, kind="ExternalOutput").ap()
    perceiver_layer(nc, io)
    r = run_bass_kernel_spmd(nc, [arrays], core_ids=[0])
    return r.results[0]["out_0_dram"]
```

```python
from contextlib import ExitStack

import concourse.bass as bass
from concourse import mybir

F32 = mybir.dt.float32
F16 = mybir.dt.float16
ACT = mybir.ActivationFunctionType
ALU = mybir.AluOpType
AX = mybir.AxisListType

P = 128
BATCH, STEPS, DM = 16, 64, 256
CTX = 1601
HEADS, DH = 16, 16
TOK = BATCH * STEPS
TILES = TOK // P
CI = DM // P
PAIRS = HEADS // 2
PAIR_ROWS = 2 * DH
THIRDS = ((0, 0), (0, 1), (1, 0))
V_COLS = 2 * PAIR_ROWS + 1
NCH = 4
COLS = [(n * 3 * P, 3 * P if n < NCH - 1 else CTX - n * 3 * P) for n in range(NCH)]
ROWS = [(m, min(P, CTX - m)) for m in range(0, CTX, P)]
KROW = len(ROWS)
KGROUPS = CI * NCH
VTILES = [(m, 2 if m + 1 < KROW and ROWS[m + 1][1] == P else 1) for m in range(0, KROW, 2)]
PROJ = KGROUPS + len(VTILES)
TURNS = [[(m, rows) for m, rows in ROWS if c0 <= m < c0 + w] for c0, w in COLS]
TBLOCKS = max(len(turns) for turns in TURNS)
ROUND = 12582912.0
EPS_LN = 1e-5
SPLIT, Q_SPLIT = 64.0, 4.0
P_SPLIT = 1024.0
assert PROJ == 2 * PAIRS - 1


class Named:
    pass


class Tally:

    def __init__(self, sem):
        self.sem, self.n = sem, 0

    def inc(self, ins, by=1):
        ins.then_inc(self.sem, by)
        self.n += by
        return self.n


def row_stats(dve, t, src, done):
    for n in range(TILES):
        last = done.inc(dve.bn_stats(t.stat[:, n, :], src[:, n, :]))
    dve.wait_ge(done.sem, last)
    for n in range(TILES):
        last = done.inc(dve.bn_aggr(t.mv[:, n, :], t.stat[:, n, :]))
    dve.wait_ge(done.sem, last)
    return done.inc(dve.tensor_scalar(t.var[:, :], t.mv[:, :, 1], EPS_LN, None, ALU.add))


def normalise(dve, t, dst, src, done):
    last = done.inc(dve.reciprocal(t.rstd[:, :], t.std[:, :]))
    dve.wait_ge(done.sem, last)
    for n in range(TILES):
        last = done.inc(dve.tensor_scalar(dst[:, n, :], src[:, n, :], t.mv[:, n, 0:1], t.rstd[:, n:n + 1],
                                          ALU.subtract, ALU.mult))
    return last


def fake_quantise(dve, t, dst, src, n, done):
    last = done.inc(dve.tensor_reduce(t.amax[:, 0:n], src[:, :, :], AX.X, ALU.max, apply_absolute_value=True))
    dve.wait_ge(done.sem, last)
    last = done.inc(dve.tensor_scalar(t.qs[:, 0:n], t.amax[:, 0:n], 1.0 / 127.0, 1e-8, ALU.mult, ALU.max))
    dve.wait_ge(done.sem, last)
    last = done.inc(dve.reciprocal(t.qr[:, 0:n], t.qs[:, 0:n]))
    dve.wait_ge(done.sem, last)
    for k in range(n):
        last = done.inc(dve.tensor_scalar(src[:, k, :], src[:, k, :], t.qr[:, k:k + 1], ROUND, ALU.mult, ALU.add))
    dve.wait_ge(done.sem, last)
    last = done.inc(dve.tensor_scalar(src[:, :, :], src[:, :, :], ROUND, -127.0, ALU.subtract, ALU.max))
    dve.wait_ge(done.sem, last)
    for k in range(n):
        last = done.inc(dve.tensor_scalar(dst[:, k, :], src[:, k, :], 127.0, t.qs[:, k:k + 1], ALU.min, ALU.mult))
    return last


def queries(nc, io, c, t, bank):
    with ExitStack() as ctx:
        def sem(name):
            return ctx.enter_context(nc.semaphore(name))

        x_in, w_in, b_in = sem("q_x_in"), sem("q_w_in"), sem("q_b_in")
        pool_done, dve_done = sem("q_pool_done"), sem("q_dve_done")
        std_ready, turned, moved, wq_moved = (sem("q_std_ready"), sem("q_turned"), sem("q_moved"),
                                              sem("q_weights_moved"))
        w_turned, q_ready = sem("q_w_turned"), sem("q_ready")
        consts_ready = sem("q_consts_ready")
        var_ready, wquant, xquant = sem("q_var_ready"), sem("q_wquant"), sem("q_xquant")
        q_moved, rows_moved = sem("q_moved_out"), sem("q_rows_moved")
        block = ctx.enter_context(nc.Block())

        @block.sync
        def _(sp):
            sp.dma_start(t.x[:, :, :], io["x"].rearrange("b t d -> (b t) d")
                         .rearrange("(n p) d -> p n d", p=P)).then_inc(x_in, 16)
            for w, dst in ((io["wq"], t.wq), (io["wp"], t.wp)):
                sp.dma_start(dst[:, :, :], w.rearrange("(j p) i -> p j i", p=P)).then_inc(w_in, 16)
            sp.dma_start(t.wkvT[:, :, :], io["wkvT"].rearrange("(j p) o -> p j o", p=P)).then_inc(b_in, 16)
            sp.dma_start(c.bk[:, :], io["bkvT"]).then_inc(b_in, 16)
            sp.dma_start(c.bq[:, :], io["bqT"]).then_inc(b_in, 16)
            sp.dma_start(c.bv[:, :], io["bv"].partition_broadcast(P)).then_inc(b_in, 16)
            sp.dma_start(c.bp[:, :], io["bp"].partition_broadcast(P)).then_inc(b_in, 16)
            sp.wait_ge(b_in, 80)
            sp.wait_ge(consts_ready, 1)
            for third in range(1, len(THIRDS)):
                sp.dma_start(c.head_mask[third * PAIR_ROWS:(third + 1) * PAIR_ROWS, :], c.head_mask[0:PAIR_ROWS, :]
                             ).then_inc(rows_moved, 16)
            sp.wait_ge(rows_moved, 16 * (len(THIRDS) - 1))

        @block.gpsimd
        def _(pool):
            done = Tally(pool_done)
            done.inc(pool.memset(c.ident[:, :], 0.0))
            done.inc(pool.memset(c.head_mask[:, :], 1.0))
            done.inc(pool.memset(c.pair_mask[:, :, :, :], 1.0 / SPLIT))
            done.inc(pool.memset(c.gather[:, :], 0.0))
            done.inc(pool.memset(c.ones[:, :], 1.0))
            done.inc(pool.memset(c.split_scale[:, :], SPLIT))
            last = done.inc(pool.memset(c.batch_mask[:, :], 1.0))
            pool.wait_ge(pool_done, last)
            done.inc(pool.affine_select(out=c.ident[:, :], in_=c.ident[:, :], compare_op=ALU.not_equal,
                                        fill=1.0, base=0, pattern=[[-1, P]], channel_multiplier=1))
            last = done.inc(pool.affine_select(out=c.head_mask[:, :], in_=c.head_mask[:, :],
                                               compare_op=ALU.is_ge, fill=0.0, base=0,
                                               pattern=[[-DH, 2]], channel_multiplier=1))
            pool.wait_ge(pool_done, last)
            done.inc(pool.affine_select(out=c.head_mask[:, :], in_=c.head_mask[:, :], compare_op=ALU.is_ge,
                                        fill=0.0, base=DH - 1, pattern=[[DH, 2]], channel_multiplier=-1))
            for half, sign in enumerate((-1, 1)):
                own = c.pair_mask[:, :, half, :]
                done.inc(pool.affine_select(out=own, in_=own, compare_op=ALU.is_ge, fill=0.0,
                                            base=(STEPS - 1, -STEPS)[half], pattern=[[0, 2], [0, DH]],
                                            channel_multiplier=sign))
            mid = c.gather[:, STEPS:2 * STEPS]
            last = done.inc(pool.affine_select(out=mid, in_=mid, compare_op=ALU.not_equal, fill=1.0, base=0,
                                               pattern=[[-1, STEPS]], channel_multiplier=1))
            done.inc(pool.affine_select(out=c.batch_mask[:, :], in_=c.batch_mask[:, :], compare_op=ALU.is_ge,
                                        fill=0.0, base=0, pattern=[[-8, BATCH]], channel_multiplier=1))
            last = done.n
            pool.wait_ge(pool_done, last)
            done.inc(pool.affine_select(out=mid, in_=mid, compare_op=ALU.not_equal, fill=1.0, base=-STEPS,
                                        pattern=[[-1, STEPS]], channel_multiplier=1))
            last = done.inc(pool.affine_select(out=c.batch_mask[:, :], in_=c.batch_mask[:, :],
                                               compare_op=ALU.is_ge, fill=0.0, base=7,
                                               pattern=[[8, BATCH]], channel_multiplier=-1))
            pool.wait_ge(pool_done, last)
            pool.sem_inc(consts_ready, 1)

        @block.vector
        def _(dve):
            done = Tally(dve_done)
            dve.wait_ge(w_in, 32)
            fake_quantise(dve, t, t.wq, t.wq, CI, done)
            dve.wait_ge(dve_done, done.n)
            last = fake_quantise(dve, t, t.wp, t.wp, CI, done)
            dve.wait_ge(dve_done, last)
            dve.sem_inc(wquant, 1)
            dve.wait_ge(x_in, 16)
            last = row_stats(dve, t, t.x, done)
            dve.wait_ge(dve_done, last)
            dve.sem_inc(var_ready, 1)
            dve.wait_ge(std_ready, 1)
            last = normalise(dve, t, t.y, t.x, done)
            dve.wait_ge(dve_done, last)
            last = fake_quantise(dve, t, t.y, t.y, TILES, done)
            dve.wait_ge(dve_done, last)
            dve.sem_inc(xquant, 1)
            for n in range(TILES):
                dve.wait_ge(turned, n + 1)
                dve.tensor_copy(t.yT[:, :, n * P:(n + 1) * P],
                                bank[n][:, 0:DM].rearrange("p (j q) -> p j q", j=CI)).then_inc(moved, 1)
            dve.wait_ge(b_in, 80)
            for k in range(CI):
                high = done.inc(dve.tensor_scalar(c.w_hl[0][:, k, :], t.wkvT[:, k, :], SPLIT, None, ALU.mult))
            dve.wait_ge(dve_done, high)
            for k in range(CI):
                done.inc(dve.scalar_tensor_tensor(out=c.w_hl[1][:, k, :], in0=t.wkvT[:, k, :], scalar=SPLIT,
                                                  in1=c.w_hl[0][:, k, :], op0=ALU.mult, op1=ALU.subtract))
            for k in range(2 * CI):
                j, cols = k // 2, slice(k % 2 * 512, k % 2 * 512 + 512)
                dve.wait_ge(q_moved, k + 1)
                high = done.inc(dve.tensor_scalar(c.q_hl[0][:, j, cols], t.qT[:, j, cols], Q_SPLIT, None, ALU.mult))
                dve.wait_ge(dve_done, high)
                done.inc(dve.scalar_tensor_tensor(out=c.q_hl[1][:, j, cols], in0=t.qT[:, j, cols], scalar=Q_SPLIT,
                                                  in1=c.q_hl[0][:, j, cols], op0=ALU.mult, op1=ALU.subtract))

        @block.scalar
        def _(act):
            act.wait_ge(w_turned, 2)
            for k, dst in enumerate((c.wqT, c.wpT)):
                act.activation(dst[:, :, :], bank[k][:, :].rearrange("p (j o) -> p j o", j=CI),
                               ACT.Copy).then_inc(wq_moved, 1)
            act.wait_ge(var_ready, 1)
            act.activation(t.std[:, :], t.var[:, :], ACT.Sqrt).then_inc(std_ready, 1)
            act.wait_ge(b_in, 80)
            for k in range(2 * CI):
                j, half = k // 2, k % 2
                act.wait_ge(q_ready, k + 1)
                act.activation(t.qT[:, j, half * 512:half * 512 + 512], bank[k][:, :], ACT.Identity,
                               bias=c.bq[:, j:j + 1]).then_inc(q_moved, 1)

        @block.tensor
        def _(pe):
            pe.wait_ge(consts_ready, 1)
            pe.wait_ge(wquant, 1)
            for k, w in enumerate((t.wq, t.wp)):
                for i in range(CI):
                    for o in range(CI):
                        ins = pe.transpose(bank[k][:, i * DM + o * P:i * DM + o * P + P],
                                           w[:, o, i * P:(i + 1) * P], c.ident[:, :])
                ins.then_inc(w_turned, 1)
            pe.wait_ge(xquant, 1)
            pe.wait_ge(wq_moved, 2)
            for n in range(TILES):
                for i in range(CI):
                    ins = pe.transpose(bank[n][:, i * P:(i + 1) * P], t.y[:, n, i * P:(i + 1) * P],
                                       c.ident[:, :])
                ins.then_inc(turned, 1)
            for k in range(2 * CI):
                j, half = k // 2, k % 2
                if k == 0:
                    pe.wait_ge(moved, TILES)
                for i in range(CI):
                    ins = pe.matmul(bank[k][:, :], c.wqT[:, i, j * P:(j + 1) * P],
                                    t.yT[:, i, half * 512:half * 512 + 512], start=(i == 0), stop=(i == CI - 1))
                ins.then_inc(q_ready, 1)


def attention(nc, io, c, t, rows_room, weights_room, bank):
    score = bank[0:4]
    turn = bank[4:6]
    pvb = bank[6]
    TERMS = THIRDS
    K_MOVES = 16 * len(THIRDS) * (PAIRS // CI)
    with ExitStack() as ctx:
        def sb(name, shape, dt=F32):
            return ctx.enter_context(nc.sbuf_tensor(name, shape, dt))

        def sem(name):
            return ctx.enter_context(nc.semaphore(name))

        raw = rows_room[:, 0:CI * CTX].rearrange("p (i m) -> p i m", i=CI)
        fresh = [rows_room[:, CI * CTX + k * 2 * DM:CI * CTX + (k + 1) * 2 * DM] for k in range(2)]
        ctx_hl = [[sb(f"ctx{part}{u}", [P, CI, CTX], F16) for part in "hl"] for u in range(2)]
        k_hl = [[sb(f"k{part}{j}", [P, CTX], F16) for part in "hl"] for j in range(CI)]
        kT = [sb(f"kT{u}", [len(THIRDS) * PAIR_ROWS, PAIRS, CTX], F16) for u in range(2)]
        v = [sb("v0", [P, KROW, PAIRS, V_COLS + 1], F16),
             c.v_room[:, :].rearrange("p (m g d) -> p m g d", m=KROW, g=PAIRS)]
        q_rows = sb("q_rows", [len(THIRDS) * PAIR_ROWS, PAIRS, TOK], F16)
        qblk = [sb(f"qblk{u}", [len(THIRDS) * PAIR_ROWS, PAIRS, 2, STEPS], F16) for u in range(2)]
        after = CI * CTX + 4 * DM
        prob = [rows_room[:, after:after + CTX], weights_room[:, 0:CTX]]
        probT = [[sb(f"probT{part}{u}", [P, TBLOCKS * P], F16) for part in "hl"] for u in range(2)]
        bk = sb("bk_scaled", [P, CI])
        mx, top, minus_scale = sb("mx", [P, NCH]), sb("row_max", [P, 1]), sb("minus_scale", [P, 1])
        shift = [sb(f"shift{u}", [P, 1]) for u in range(2)]
        rden = sb("rden", [P, 1])
        parts_out = [sb(f"parts_out{u}", [P, 2, 2 * DH]) for u in range(2)]

        ctx_in = [sem(f"ctx_in{j}") for j in range(CI)]
        ctx_scaled, ctx_high, ctx_low = sem("ctx_scaled"), sem("ctx_high"), sem("ctx_low")
        rows_moved = sem("rows_moved")
        k_moved = [sem(f"k_moved{j}") for j in range(CI)]
        bk_scaled, kv_high, kv_low = sem("bk_scaled_up"), sem("kv_high"), sem("kv_low")
        q_masked, proj_done, proj_out = sem("q_masked"), sem("proj_done"), sem("proj_out")
        scored, max_ready, exp_done = sem("scored"), sem("max_ready"), sem("exp_done")
        turned, p_high, p_low = sem("a_turned"), sem("p_high"), sem("p_low")
        pv_done, o_out, o_summed = sem("pv_done"), sem("o_out"), sem("o_summed")
        scale_set, cleared, mx_done, den_done = sem("scale_set"), sem("cleared"), sem("mx_done"), sem("den_done")
        block = ctx.enter_context(nc.Block())

        def prj_bank(k, alone):
            return bank[7 - k % 2] if alone else bank[7]

        def kv_parts(k, u):
            now = fresh[(u * PROJ + k) % 2]
            if k < KGROUPS:
                j, (c0, w) = k // NCH, COLS[k % NCH]
                return (*(k_hl[j][part][:, c0:c0 + w] for part in range(2)), now[:, 0:w])
            m, n = VTILES[k - KGROUPS]
            rows = ROWS[m][1]
            return (*(v[u][0:rows, m:m + n, :, part * PAIR_ROWS:(part + 1) * PAIR_ROWS].rearrange("p m g d -> p (m g) d") for part in range(2)),
                    now[0:rows, 0:n * DM].rearrange("p (g d) -> p g d", g=n * PAIRS))

        def before(b, g, u):
            return (b, g - 1, u) if g > 0 else (b - 1, PAIRS - 1, 1 - u)

        def in_batches(eng, batch):
            batch(0, 0, True, True, True, 3)
            with eng.Fori(0, BATCH // 2 - 2) as i:
                batch(2 * i + 1, 1, True, True, False, 2 * i + 4)
                batch(2 * i + 2, 0, True, True, False, 2 * i + 5)
            batch(BATCH - 3, 1, True, True, False, BATCH)
            batch(BATCH - 2, 0, True, False, False, 0)
            batch(BATCH - 1, 1, False, False, False, 0)

        @block.sync
        def _(sp):
            def load(b, j):
                sp.dma_start(raw[:, j, :], io["ctxT"][bass.ds(b, 1), j * P:(j + 1) * P, :]
                             .rearrange("o p m -> p (o m)")).then_inc(ctx_in[j], 16)

            def move_k(b, j, u):
                sp.wait_ge(kv_low, b * PROJ + (j + 1) * NCH)
                for i in range(PAIRS // CI):
                    for third, (_, part) in enumerate(THIRDS):
                        sp.dma_start(kT[u][third * PAIR_ROWS:(third + 1) * PAIR_ROWS, j * (PAIRS // CI) + i, :],
                                     k_hl[j][part][i * PAIR_ROWS:(i + 1) * PAIR_ROWS, :]).then_inc(k_moved[j], 16)

            def reload(b, j):
                sp.wait_ge(ctx_low, (b - 1) * KGROUPS + (j + 1) * NCH)
                load(b, j)

            for j in range(CI):
                load(0, j)
            for g in range(PAIRS):
                j, i = divmod(g, PAIRS // CI)
                for third, (part, _) in enumerate(THIRDS):
                    sp.dma_start(q_rows[third * PAIR_ROWS:(third + 1) * PAIR_ROWS, g, :],
                                 c.q_hl[part][i * PAIR_ROWS:(i + 1) * PAIR_ROWS, j, :]).then_inc(rows_moved, 16)
            for j in range(CI):
                reload(1, j)
            with sp.Fori(0, BATCH // 2 - 1) as i:
                for u in range(2):
                    for j in range(CI):
                        move_k(2 * i + u, j, u)
                        reload(2 * i + u + 2, j)
            for b in range(BATCH - 2, BATCH):
                for j in range(CI):
                    move_k(b, j, b % 2)

        @block.gpsimd
        def _(pool):
            def mask(b, u, k, first):
                if not first:
                    pool.wait_ge(scored, (b - 1) * (PAIRS * NCH))
                rows, two = len(THIRDS) * PAIR_ROWS, slice(2 * k, 2 * k + 2)
                q = q_rows[:, two, bass.ds(b * STEPS, STEPS)].unsqueeze(2).broadcast_to([rows, 2, 2, STEPS])
                own = c.head_mask[0:rows, :].unsqueeze(1).unsqueeze(3).broadcast_to([rows, 2, 2, STEPS])
                pool.tensor_tensor(qblk[u][:, two, :, :], q, own, ALU.mult).then_inc(q_masked, 1)

            def scale_ctx(b, n, loads):
                j, (c0, w) = n // NCH, COLS[n % NCH]
                if n % NCH == 0:
                    pool.wait_ge(ctx_in[j], 16 * loads)
                pool.tensor_tensor(raw[:, j, c0:c0 + w], raw[:, j, c0:c0 + w], c.split_scale[:, :].broadcast_to([P, w]),
                                   ALU.mult).then_inc(ctx_scaled, 1)

            def ctx_lows(b, u, n):
                j, (c0, w) = n // NCH, COLS[n % NCH]
                pool.wait_ge(ctx_high, b * KGROUPS + n + 1)
                pool.tensor_tensor(ctx_hl[u][1][:, j, c0:c0 + w], raw[:, j, c0:c0 + w], ctx_hl[u][0][:, j, c0:c0 + w],
                                   ALU.subtract).then_inc(ctx_low, 1)

            def kv_lows(b, k, u):
                pool.wait_ge(kv_high, b * PROJ + k + 1)
                high, low, src = kv_parts(k, u)
                pool.tensor_tensor(low, src, high, ALU.subtract).then_inc(kv_low, 1)

            def sum_parts(b, g):
                pool.wait_ge(o_out, b * PAIRS + g + 1)
                pool.tensor_tensor(t.o[:, bass.ds(b, 1), g, :].rearrange("p o d -> p (o d)"), parts_out[g % 2][:, 0, :],
                                   parts_out[g % 2][:, 1, :], ALU.add).then_inc(o_summed, 1)

            def batch(b, u, more, split, first, loads):
                for g in range(PAIRS):
                    if more and g > 0:
                        kv_lows(b + 1, 2 * g - 1, 1 - u)
                    if more and g < 2 * CI:
                        mask(b + 1, 1 - u, g, first)
                    if split:
                        scale_ctx(b + 2, g, loads)
                    if more:
                        kv_lows(b + 1, 2 * g, 1 - u)
                    if split:
                        ctx_lows(b + 2, u, g)
                    if not (first and g == 0):
                        sum_parts(*before(b, g, u)[0:2])

            for n in range(KGROUPS):
                ctx_lows(0, 0, n)
            for k in range(PROJ + 1):
                if k < PROJ:
                    kv_lows(0, k, 0)
                if k >= KGROUPS:
                    ctx_lows(1, 1, k - KGROUPS)
                if k == KGROUPS - 1:
                    pool.wait_ge(rows_moved, 16 * len(THIRDS) * PAIRS)
                    pool.memset(v[1][:, :, :, V_COLS - 1:V_COLS], 1.0).then_inc(cleared, 1)
                    for q in range(2 * CI):
                        mask(0, 0, q, True)
            in_batches(pool, batch)
            sum_parts(BATCH - 1, PAIRS - 1)

        @block.scalar
        def _(act):
            def project_out(b, k, u, first=False, alone=False):
                act.wait_ge(proj_done, b * PROJ + k + 1)
                if not first:
                    act.wait_ge(kv_low, b * PROJ + k - 1)
                now = fresh[(u * PROJ + k) % 2]
                prj = prj_bank(k, alone)
                if k < KGROUPS:
                    j, w = k // NCH, COLS[k % NCH][1]
                    ins = act.activation(now[:, 0:w], prj[:, 0:w], ACT.Identity, bias=bk[:, j:j + 1], scale=1.0 / SPLIT)
                else:
                    m, n = VTILES[k - KGROUPS]
                    rows = ROWS[m][1]
                    ins = act.activation(now[0:rows, 0:n * DM], prj[0:rows, 0:n * DM], ACT.Copy, scale=1.0 / SPLIT)
                ins.then_inc(proj_out, 1)

            def exp(b, g, n, first):
                if n == 0:
                    act.wait_ge(max_ready, b * PAIRS + g + 1)
                    if not first:
                        act.wait_ge(turned, (b * PAIRS + g - 1) * NCH)
                c0, w = COLS[n]
                act.activation(prob[g % 2][:, c0:c0 + w], score[n][:, 0:w], ACT.Exp,
                               bias=shift[g % 2][:, 0:1], scale=1.0 / (4 * SPLIT * Q_SPLIT)).then_inc(exp_done, 1)

            def highs(b, g, r, first):
                k = (b * PAIRS + g) * NCH + r
                act.wait_ge(turned, k + 1)
                if not first:
                    act.wait_ge(pv_done, k - 1)
                rows, n = group(r)
                act.activation(probT[k2(g, r)][0][0:rows, 0:n * P], turn[k2(g, r)][0:rows, 0:n * P], ACT.Copy,
                               scale=P_SPLIT).then_inc(p_high, 1)

            def batch(b, u, more, split, first, loads):
                for g in range(PAIRS):
                    for n in range(NCH):
                        exp(b, g, n, first and g < 2)
                        if n == 1 and more and g > 0:
                            project_out(b + 1, 2 * g - 1, 1 - u)
                        if n > 0:
                            highs(b, g, n - 1, first and g == 0 and n <= 2)
                        if n == 3 and more:
                            project_out(b + 1, 2 * g, 1 - u)
                    highs(b, g, NCH - 1, False)

            act.activation(bk[:, :], c.bk[:, :], ACT.Copy, scale=SPLIT).then_inc(bk_scaled, 1)
            act.wait_ge(bk_scaled, 1)
            for k in range(PROJ):
                project_out(0, k, 0, k < 2, True)
            in_batches(act, batch)

        @block.vector
        def _(dve):
            def scale_ctx(b, n, loads):
                j, (c0, w) = n // NCH, COLS[n % NCH]
                if n % NCH == 0:
                    dve.wait_ge(ctx_in[j], 16 * loads)
                dve.tensor_scalar(raw[:, j, c0:c0 + w], raw[:, j, c0:c0 + w], SPLIT, None, ALU.mult
                                  ).then_inc(ctx_scaled, 1)

            def ctx_highs(b, u, n):
                j, (c0, w) = n // NCH, COLS[n % NCH]
                dve.wait_ge(ctx_scaled, b * KGROUPS + n + 1)
                dve.tensor_copy(ctx_hl[u][0][:, j, c0:c0 + w], raw[:, j, c0:c0 + w]).then_inc(ctx_high, 1)

            def kv_highs(b, k, u, first=False):
                dve.wait_ge(proj_out, b * PROJ + k + 1)
                if k % NCH == 0 and k < KGROUPS and not first:
                    dve.wait_ge(k_moved[k // NCH], b * K_MOVES)
                high, _, src = kv_parts(k, u)
                dve.tensor_copy(high, src).then_inc(kv_high, 1)

            def maximum(b, g, n):
                dve.wait_ge(scored, (b * PAIRS + g) * NCH + n + 1)
                dve.tensor_reduce(mx[:, n:n + 1], score[n][:, 0:COLS[n][1]], AX.X, ALU.max).then_inc(mx_done, 1)

            def maximum_so_far(b, g):
                dve.wait_ge(mx_done, (b * PAIRS + g) * (NCH + 1) + NCH - 1)
                dve.tensor_reduce(top[:, :], mx[:, 0:NCH - 1], AX.X, ALU.max).then_inc(mx_done, 1)

            def overall(b, g):
                dve.wait_ge(mx_done, (b * PAIRS + g + 1) * (NCH + 1))
                dve.scalar_tensor_tensor(out=shift[g % 2][:, :], in0=mx[:, NCH - 1:NCH], scalar=top[:, 0:1],
                                         in1=minus_scale[:, :], op0=ALU.max, op1=ALU.mult).then_inc(max_ready, 1)

            def lows(b, g, r):
                dve.wait_ge(p_high, (b * PAIRS + g) * NCH + r + 1)
                rows, n = group(r)
                high, low = (probT[k2(g, r)][part][0:rows, 0:n * P] for part in range(2))
                dve.scalar_tensor_tensor(out=low, in0=turn[k2(g, r)][0:rows, 0:n * P], scalar=P_SPLIT, in1=high,
                                         op0=ALU.mult, op1=ALU.subtract).then_inc(p_low, 1)

            def output(b, g, first):
                G = b * PAIRS + g
                dve.wait_ge(pv_done, (G + 1) * NCH)
                dve.reciprocal(rden[:, :], pvb[:, V_COLS - 1:V_COLS]).then_inc(den_done, 1)
                dve.wait_ge(den_done, G + 1)
                if not first:
                    dve.wait_ge(o_summed, G - 1)
                dve.scalar_tensor_tensor(out=parts_out[g % 2][:, :, :].rearrange("p a d -> p (a d)"),
                                         in0=pvb[:, 0:4 * DH], scalar=rden[:, 0:1],
                                         in1=c.pair_mask[:, :, :, :].rearrange("p a h d -> p (a h d)"),
                                         op0=ALU.mult, op1=ALU.mult).then_inc(o_out, 1)

            def batch(b, u, more, split, first, loads):
                for g in range(PAIRS):
                    ahead = more or g < PAIRS - 1
                    nxt = (b, g + 1) if g < PAIRS - 1 else (b + 1, 0)
                    for n in range(NCH):
                        if n == NCH - 1 and ahead:
                            maximum_so_far(*nxt)
                        if ahead:
                            maximum(*nxt, n)
                        if n == NCH - 1 and ahead:
                            overall(*nxt)
                        if n == NCH - 1:
                            lows(b, g, n - 1)
                        if n != NCH - 2:
                            lows(b, g, n)
                        if n == 0 and not (first and g == 0):
                            output(*before(b, g, u)[0:2], first and g < 3)
                        if n == 0 and more and g > 0:
                            kv_highs(b + 1, 2 * g - 1, 1 - u)
                    if more:
                        kv_highs(b + 1, 2 * g, 1 - u)
                    if split:
                        ctx_highs(b + 2, u, g)

            dve.memset(minus_scale[:, :], -1.0 / (4 * SPLIT * Q_SPLIT)).then_inc(scale_set, 1)
            dve.wait_ge(scale_set, 1)
            dve.memset(v[0][:, :, :, V_COLS - 1:V_COLS], 1.0).then_inc(cleared, 1)
            dve.memset(turn[k2(0, NCH - 1)][:, (TBLOCKS - 1) * P:TBLOCKS * P], 0.0).then_inc(cleared, 1)
            for n in range(KGROUPS):
                scale_ctx(0, n, 1)
                ctx_highs(0, 0, n)
            for k in range(PROJ + 1):
                if k < PROJ:
                    kv_highs(0, k, 0, True)
                if k >= KGROUPS:
                    scale_ctx(1, k - KGROUPS, 2)
                    ctx_highs(1, 1, k - KGROUPS)
            for n in range(NCH):
                if n == NCH - 1:
                    maximum_so_far(0, 0)
                maximum(0, 0, n)
            overall(0, 0)
            in_batches(dve, batch)
            output(BATCH - 1, PAIRS - 1, False)

        @block.tensor
        def _(pe):
            def project(b, k, u, alone=False):
                prj = prj_bank(k, alone)
                if not alone:
                    pe.wait_ge(proj_out, b * PROJ + k)
                elif k >= 2:
                    pe.wait_ge(proj_out, k - 1)
                terms = [(a, x, i) for a, x in TERMS for i in range(CI)]
                for q, (a, x, i) in enumerate(terms if k < KGROUPS else ()):
                    j, (c0, w) = k // NCH, COLS[k % NCH]
                    ins = pe.matmul(prj[:, 0:w], c.w_hl[a][:, i, j * P:(j + 1) * P], ctx_hl[u][x][:, i, c0:c0 + w],
                                    start=(q == 0), stop=(q == len(terms) - 1))
                m, n = VTILES[k - KGROUPS] if k >= KGROUPS else (0, 0)
                for s in range(n):
                    m0, rows = ROWS[m + s]
                    for q, (a, x, i) in enumerate(terms):
                        ins = pe.matmul(prj[0:rows, s * DM:(s + 1) * DM], ctx_hl[u][a][:, i, m0:m0 + rows],
                                        c.w_hl[x][:, i, DM:2 * DM], start=(q == 0), stop=(q == len(terms) - 1))
                ins.then_inc(proj_done, 1)

            def scores(b, g, n, u, first):
                if g == 0 and n == 0:
                    pe.wait_ge(q_masked, (b + 1) * 2 * CI)
                if g % (PAIRS // CI) == 0 and n == 0:
                    pe.wait_ge(k_moved[g // (PAIRS // CI)], (b + 1) * K_MOVES)
                c0, w = COLS[n]
                if not first:
                    pe.wait_ge(exp_done, (b * PAIRS + g - 1) * NCH + n + 1)
                ins = pe.matmul(score[n][:, 0:w], qblk[u][:, g, :, :].rearrange("p h q -> p (h q)"),
                                kT[u][:, g, c0:c0 + w], start=True, stop=True)
                ins.then_inc(scored, 1)

            def turn_probs(b, g, r, first):
                k = (b * PAIRS + g) * NCH + r
                pe.wait_ge(exp_done, k + 1)
                if not first:
                    pe.wait_ge(p_low, k - 1)
                for s, (m0, rows) in enumerate(TURNS[r]):
                    ins = pe.transpose(turn[k2(g, r)][0:rows, s * P:(s + 1) * P], prob[g % 2][:, m0:m0 + rows],
                                       c.ident[:, :])
                ins.then_inc(turned, 1)

            def times_v(b, g, u, r, first):
                k = (b * PAIRS + g) * NCH + r
                pe.wait_ge(p_low, k + 1)
                if g == 0 and r == 0:
                    pe.wait_ge(kv_low, (b + 1) * PROJ)
                if r == 0 and not first:
                    pe.wait_ge(o_out, b * PAIRS + g)
                for s, (m0, rows) in enumerate(TURNS[r]):
                    m = m0 // P
                    for part in range(2):
                        ins = pe.matmul(pvb[:, 0:V_COLS], probT[k2(g, r)][part][0:rows, s * P:(s + 1) * P],
                                        v[u][0:rows, m, g, 0:V_COLS],
                                        start=(m == 0 and part == 0), stop=(m == KROW - 1 and part == 1))
                ins.then_inc(pv_done, 1)

            def batch(b, u, more, split, first, loads):
                for g in range(PAIRS):
                    start = first and g == 0
                    for n in range(NCH):
                        if g < PAIRS - 1:
                            scores(b, g + 1, n, u, False)
                        elif more:
                            scores(b + 1, 0, n, 1 - u, False)
                        turn_probs(b, g, n, start and n < 2)
                        if n == 0 and not start:
                            times_v(*before(b, g, u), NCH - 1, False)
                        if n == 0 and more and g == 0:
                            pe.wait_ge(ctx_low, (b + 2) * KGROUPS)
                        if n == 0 and more:
                            project(b + 1, 2 * g, 1 - u)
                        if n == NCH - 1 and more and g < PAIRS - 1:
                            project(b + 1, 2 * g + 1, 1 - u)
                        if n > 0:
                            times_v(b, g, u, n - 1, start)

            pe.wait_ge(ctx_low, KGROUPS)
            for k in range(PROJ):
                project(0, k, 0, True)
            for n in range(NCH):
                scores(0, 0, n, 0, True)
            pe.wait_ge(cleared, 3)
            in_batches(pe, batch)
            times_v(BATCH - 1, PAIRS - 1, 1, NCH - 1, False)


def group(r):
    return P, len(TURNS[r])


def k2(g, r):
    return (g * NCH + r) % 2


def project_attention(nc, io, c, t, w, bank):
    with ExitStack() as ctx:
        def sem(name):
            return ctx.enter_context(nc.semaphore(name))

        gathered, dve_done, oquant = sem("p_gathered"), sem("p_dve_done"), sem("p_oquant")
        turned, moved, projected, var_ready, std_ready = (sem("p_turned"), sem("p_moved"), sem("p_projected"),
                                                          sem("p_var_ready"), sem("p_std_ready"))
        y_ready, w_in, x_in = sem("p_y_ready"), sem("p_w_in"), sem("p_x_in")
        block = ctx.enter_context(nc.Block())

        @block.sync
        def _(sp):
            sp.dma_start(t.x[:, :, :], io["x"].rearrange("b t d -> (b t) d")
                         .rearrange("(n p) d -> p n d", p=P)).then_inc(x_in, 16)
            for n in w.wide:
                sp.dma_start(w.wide[n][:, :, :], io["W" + n].rearrange("(i p) o -> p i o", p=P)).then_inc(w_in, 16)
            sp.dma_start(w.pw[:, :, :], io["pw_w"].rearrange("(i p) o -> p i o", p=P)).then_inc(w_in, 16)
            sp.dma_start(w.ir2[:, :], io["ir_w2"]).then_inc(w_in, 16)
            sp.dma_start(w.nm1[:, :], io["nm_w1"]).then_inc(w_in, 16)
            sp.dma_start(w.nm2[:, :, :], io["nm_w2"].rearrange("(i p) o -> p i o", p=P)).then_inc(w_in, 16)
            sp.dma_start(w.cols[:, 0:6], io["cols6"]).then_inc(w_in, 16)
            sp.dma_start(w.cols[:, 6:7], io["ir_b2"].partition_broadcast(P)).then_inc(w_in, 16)
            sp.dma_start(w.cols[:, 7:10], io["pw_b"].partition_broadcast(P)).then_inc(w_in, 16)
            sp.dma_start(w.cols[:, 10:12], io["lam"]).then_inc(w_in, 16)
            sp.dma_start(w.o[:, :], io["Wo"]).then_inc(w_in, 16)
            sp.dma_start(w.norm[:, :], io["norm_w"]).then_inc(w_in, 16)
            sp.dma_start(w.router[:, :, :], io["routerT"].rearrange("(i p) e -> p i e", p=P)).then_inc(w_in, 16)
            sp.wait_ge(w_in, 17 * 16)
            sp.wait_ge(x_in, 16)

        @block.tensor
        def _(pe):
            for n in range(TILES):
                for half in range(2):
                    sel = c.gather[:, (1 - half) * STEPS:(1 - half) * STEPS + P]
                    ins = pe.matmul(bank[n][:, 0:DM], sel, t.o[:, 2 * n + half, :, :].rearrange("p g d -> p (g d)"),
                                    start=(half == 0), stop=(half == 1))
                ins.then_inc(gathered, 1)
            pe.wait_ge(oquant, 1)
            for n in range(TILES):
                for i in range(CI):
                    ins = pe.transpose(bank[n][:, i * P:(i + 1) * P], t.y[:, n, i * P:(i + 1) * P], c.ident[:, :])
                ins.then_inc(turned, 1)
            for n in range(TILES):
                pe.wait_ge(moved, n + 1)
                for i in range(CI):
                    ins = pe.matmul(bank[n][:, 0:DM], t.yT[:, i, n * P:(n + 1) * P], c.wpT[:, i, :],
                                    start=(i == 0), stop=(i == CI - 1))
                ins.then_inc(projected, 1)
            pe.wait_ge(y_ready, 1)
            for n in range(TILES):
                for i in range(CI):
                    ins = pe.transpose(bank[n][:, i * P:(i + 1) * P], t.y[:, n, i * P:(i + 1) * P], c.ident[:, :])
                ins.then_inc(turned, 1)

        @block.scalar
        def _(act):
            act.wait_ge(var_ready, 1)
            act.activation(t.std[:, :], t.var[:, :], ACT.Sqrt).then_inc(std_ready, 1)

        @block.vector
        def _(dve):
            done = Tally(dve_done)
            for n in range(TILES):
                dve.wait_ge(gathered, n + 1)
                last = done.inc(dve.tensor_tensor(t.y[:, n, :], bank[n][:, 0:DM], c.bv[:, :], ALU.add))
            dve.wait_ge(dve_done, last)
            last = fake_quantise(dve, t, t.y, t.y, TILES, done)
            dve.wait_ge(dve_done, last)
            dve.sem_inc(oquant, 1)
            for n in range(TILES):
                dve.wait_ge(turned, n + 1)
                dve.tensor_copy(t.yT[:, :, n * P:(n + 1) * P],
                                bank[n][:, 0:DM].rearrange("p (j q) -> p j q", j=CI)).then_inc(moved, 1)
            dve.wait_ge(x_in, 16)
            for n in range(TILES):
                last = done.inc(dve.tensor_tensor(t.x[:, n, :], t.x[:, n, :], c.bp[:, :], ALU.add))
            dve.wait_ge(dve_done, last)
            for n in range(TILES):
                dve.wait_ge(projected, n + 1)
                last = done.inc(dve.tensor_tensor(t.x[:, n, :], bank[n][:, 0:DM], t.x[:, n, :], ALU.add))
            dve.wait_ge(dve_done, last)
            last = row_stats(dve, t, t.x, done)
            dve.wait_ge(dve_done, last)
            dve.sem_inc(var_ready, 1)
            dve.wait_ge(std_ready, 1)
            last = normalise(dve, t, t.y, t.x, done)
            dve.wait_ge(dve_done, last)
            dve.sem_inc(y_ready, 1)
            for n in range(TILES):
                dve.wait_ge(turned, TILES + n + 1)
                dve.tensor_copy(t.yT[:, :, n * P:(n + 1) * P],
                                bank[n][:, 0:DM].rearrange("p (j q) -> p j q", j=CI)).then_inc(moved, 1)


DS = 128
BLK = 8
NB = STEPS // BLK
HALF = BLK // 2
GROUPS = TOK // HALF
PAIR_S = [(s, r) for s in range(HALF) for r in range(s + 1, HALF)]
PAIR_O = [(s, r) for s in range(HALF) for r in range(s, HALF)]
DECAY = 8.0
KIND_K, KIND_Q, KIND_O = range(3)


def features(nc, io, c, t, m, w, bank):
    with ExitStack() as ctx:
        def sb(name, shape):
            return ctx.enter_context(nc.sbuf_tensor(name, shape, F32))

        def sem(name):
            return ctx.enter_context(nc.semaphore(name))

        w_pwb, w_irb = sb("w_pwb", [P, CI, 3, P]), sb("w_irb", [P, P])
        lam8 = sb("lam8", [P, 2])
        la, irg, h1 = sb("la", [P, 2, TOK]), sb("irg", [P, TOK]), sb("h1", [P, 2, TOK])
        lg, sq, nrm = sb("lg", [P, 3, TOK]), sb("sq", [P, 2, TOK]), sb("nrm", [P, 2, TOK])
        upd, keep, top, al = sb("upd", [P, TOK]), sb("keep", [P, TOK]), sb("top", [P, TOK]), sb("al", [P, 2, TOK])

        took = {"dve": sem("f_dve_took"), "act": sem("f_act_took")}
        repeated, dve_done, pe_done, kept = sem("f_repeated"), sem("f_dve_done"), sem("f_pe_done"), sem("f_kept")
        squared, lam_sig, lam_eps, logs, lam_scaled = (sem("f_squared"), sem("f_lam_sig"), sem("f_lam_eps"), sem("f_logs"),
                                                       sem("f_lam_scaled"))
        nrm_inverse, lg_shifted, lg_exped, al_exped = sem("f_nrm_inverse"), sem("f_lg_shifted"), sem("f_lg_exped"), sem("f_al_exped")
        lg_summed, sum_log, sum_inverse, units = sem("f_lg_summed"), sem("f_sum_log"), sem("f_sum_inverse"), sem("f_units")
        pool_weighted, pool_done = sem("f_pool_weighted"), sem("f_pool_done")
        block = ctx.enter_context(nc.Block())

        jobs = ([(n, h, "dve") for n in ("k", "q") for h in range(2)]
                + [(("pw", n), h, "act") for n in range(3) for h in range(2)]
                + [("v", h, "dve") for h in range(2)]
                + [(("norm", n), h, "dve") for n in range(2) for h in range(2)]
                + [(n, h, "act") for n in ("af", "as", "ir") for h in range(2)]
                + [(("nm1", j), h, "act") for j in range(2) for h in range(2)]
                + [("imp", h, "dve") for h in range(2)] + [("nu", h, "act") for h in range(2)])
        counts, taken = {"dve": 0, "act": 0}, []
        for name, h, e in jobs:
            counts[e] += 1
            taken.append((e, counts[e]))
        at = {(name, h): taken[k] for k, (name, h, _) in enumerate(jobs)}

        @block.gpsimd
        def _(pool):
            pool.memset(keep[:, :], 1.0).then_inc(kept, 1)
            pool.wait_ge(kept, 1)
            pool.memset(keep[:, :].rearrange("p (g t) -> p g t", t=BLK)[:, :, 0], 0.0).then_inc(kept, 1)
            pool.memset(m.lx[:, :, :], 0.0).then_inc(kept, 1)
            for n, src in enumerate((m.k, m.qh)):
                for h in range(2):
                    pool.wait_ge(took["dve"], 2 * n + h + 1)
                    half = slice(512 * h, 512 * h + 512)
                    pool.tensor_tensor(sq[:, n, half], src[:, half], src[:, half], ALU.mult).then_inc(squared, 1)
            pool.wait_ge(lg_exped, 1)
            pool.tensor_tensor(top[:, :], lg[:, 0, :], lg[:, 1, :], ALU.add).then_inc(pool_done, 1)
            pool.wait_ge(pool_done, 1)
            pool.tensor_tensor(top[:, :], top[:, :], lg[:, 2, :], ALU.add).then_inc(lg_summed, 1)
            pool.wait_ge(sum_inverse, 1)
            pool.tensor_tensor(lg[:, 0, :], lg[:, 0, :], top[:, :], ALU.mult).then_inc(pool_done, 1)
            pool.wait_ge(pool_done, 2)
            pool.wait_ge(units, 2)
            pool.tensor_tensor(m.oq[:, 0, :], lg[:, 0, :], m.qh[:, :], ALU.mult).then_inc(pool_weighted, 1)

        @block.tensor
        def _(pe):
            def wait_for(e, n):
                pe.wait_ge(took[e], n)

            for k, (name, h, _) in enumerate(jobs):
                if k >= 8:
                    wait_for(*taken[k - 8])
                b = bank[k % 8]
                half = slice(512 * h, 512 * h + 512)
                if name in w.wide:
                    parts = [(w.wide[name][:, i, :], t.yT[:, i, half]) for i in range(CI)]
                elif name[0] == "pw":
                    pe.wait_ge(repeated, 1)
                    parts = [(w_pwb[:, i, name[1], :], t.yT[:, i, half]) for i in range(CI)]
                elif name[0] == "nm1":
                    wait_for(*at["v", h])
                    parts = [(w.nm1[:, name[1] * DS:(name[1] + 1) * DS], m.v[:, half])]
                elif name == "imp":
                    wait_for(*at["ir", h])
                    parts = [(w_irb[:, :], irg[:, half])]
                elif name == "nu":
                    wait_for(*at[("nm1", 1), h])
                    parts = [(w.nm2[:, j, :], h1[:, j, half]) for j in range(2)]
                else:
                    pe.wait_ge(squared, 2 * name[1] + h + 1)
                    parts = [(c.ones[:, :], sq[:, name[1], half])]
                for i, (lhs, rhs) in enumerate(parts):
                    ins = pe.matmul(b[:, :], lhs, rhs, start=(i == 0), stop=(i == len(parts) - 1))
                ins.then_inc(pe_done, 1)

        @block.scalar
        def _(act):
            def take(name, h):
                k = next(k for k, job in enumerate(jobs) if job[0:2] == (name, h))
                act.wait_ge(pe_done, k + 1)
                half = slice(512 * h, 512 * h + 512)
                b = bank[k % 8][:, :]
                if name == "af":
                    ins = act.activation(la[:, 0, half], b, ACT.Sigmoid, bias=w.cols[:, 0:1])
                elif name == "as":
                    ins = act.activation(la[:, 1, half], b, ACT.Sigmoid, bias=w.cols[:, 1:2])
                elif name == "ir":
                    ins = act.activation(irg[:, half], b, ACT.Gelu, bias=w.cols[:, 2:3])
                elif name[0] == "nm1":
                    ins = act.activation(h1[:, name[1], half], b, ACT.Gelu, bias=w.cols[:, 3 + name[1]:4 + name[1]])
                elif name[0] == "pw":
                    ins = act.activation(lg[:, name[1], half], b, ACT.Identity, bias=w.cols[:, 7 + name[1]:8 + name[1]])
                else:
                    ins = act.activation(m.nu[:, half], b, ACT.Identity, bias=w.cols[:, 5:6])
                ins.then_inc(took["act"], 1)

            act.activation(lam8[:, :], w.cols[:, 10:12], ACT.Sigmoid).then_inc(lam_sig, 1)
            for name, h, e in jobs:
                if e == "act" and name != "nu":
                    take(name, h)
            act.wait_ge(lam_eps, 1)
            act.activation(lam8[:, :], lam8[:, :], ACT.Ln).then_inc(logs, 1)
            act.wait_ge(took["dve"], at[("norm", 1), 1][1])
            act.activation(nrm[:, :, :], nrm[:, :, :], ACT.Ln).then_inc(logs, 1)
            act.wait_ge(logs, 2)
            act.activation(nrm[:, :, :], nrm[:, :, :], ACT.Exp, scale=-0.5).then_inc(nrm_inverse, 1)
            act.wait_ge(lg_shifted, 1)
            act.activation(lg[:, :, :], lg[:, :, :], ACT.Exp).then_inc(lg_exped, 1)
            act.wait_ge(lam_scaled, 1)
            act.activation(al[:, :, :], la[:, :, :], ACT.Exp).then_inc(al_exped, 1)
            for h in range(2):
                take("nu", h)
            act.wait_ge(lg_summed, 1)
            act.activation(top[:, :], top[:, :], ACT.Ln).then_inc(sum_log, 1)
            act.wait_ge(sum_log, 1)
            act.activation(top[:, :], top[:, :], ACT.Exp, scale=-1.0).then_inc(sum_inverse, 1)

        @block.vector
        def _(dve):
            done = Tally(dve_done)

            def then(ins):
                dve.wait_ge(dve_done, done.inc(ins))

            def take(name, h):
                k = next(k for k, job in enumerate(jobs) if job[0:2] == (name, h))
                dve.wait_ge(pe_done, k + 1)
                half = slice(512 * h, 512 * h + 512)
                b = bank[k % 8][:, :]
                if name == "imp":
                    ins = dve.tensor_scalar(upd[:, half], b, w.cols[:, 6:7], 0.0, ALU.add, ALU.is_gt)
                elif name[0] == "norm":
                    ins = dve.tensor_scalar(nrm[:, name[1], half], b, 1e-24, None, ALU.max)
                else:
                    ins = dve.tensor_copy({"v": m.v, "k": m.k, "q": m.qh}[name][:, half], b)
                ins.then_inc(took["dve"], 1)

            for name in ("k", "q"):
                for h in range(2):
                    take(name, h)
                if name == "k":
                    for i in range(CI):
                        for n in range(3):
                            done.inc(dve.tensor_scalar(w_pwb[:, i, n, :], c.ones[:, :], w.pw[:, i, n:n + 1], None, ALU.mult))
                    dve.wait_ge(dve_done, done.n)
                    dve.tensor_scalar(w_irb[:, :], c.ones[:, :], w.ir2[:, 0:1], None, ALU.mult).then_inc(repeated, 1)
            dve.wait_ge(lam_sig, 1)
            dve.tensor_scalar(lam8[:, :], lam8[:, :], 1e-8, None, ALU.add).then_inc(lam_eps, 1)
            for h in range(2):
                take("v", h)
            for n in range(2):
                for h in range(2):
                    take(("norm", n), h)
            dve.wait_ge(took["act"], at[("pw", 2), 1][1])
            then(dve.tensor_tensor(top[:, :], lg[:, 0, :], lg[:, 1, :], ALU.max))
            then(dve.tensor_tensor(top[:, :], top[:, :], lg[:, 2, :], ALU.max))
            dve.tensor_tensor(lg[:, :, :], lg[:, :, :], top[:, :].unsqueeze(1).broadcast_to([P, 3, TOK]),
                              ALU.subtract).then_inc(lg_shifted, 1)
            for h in range(2):
                take("imp", h)
            dve.wait_ge(logs, 1)
            then(dve.tensor_scalar(lam8[:, :], lam8[:, :], DECAY, None, ALU.mult))
            done.inc(dve.tensor_scalar(la[:, 0, :], la[:, 0, :], lam8[:, 0:1], None, ALU.mult))
            then(dve.tensor_scalar(la[:, 1, :], la[:, 1, :], lam8[:, 1:2], None, ALU.mult))
            dve.sem_inc(lam_scaled, 1)
            dve.wait_ge(kept, 3)
            for x in range(2):
                done.inc(dve.tensor_tensor_scan(m.lb[:, x, :], keep[:, :], la[:, x, :], 0.0, ALU.mult, ALU.add))
            dve.wait_ge(nrm_inverse, 1)
            for n, own in enumerate((m.k, m.qh)):
                dve.tensor_tensor(own[:, :], own[:, :], nrm[:, n, :], ALU.mult).then_inc(units, 1)
            dve.wait_ge(dve_done, done.n)
            lb8 = m.lb[:, :, :].rearrange("p x (g t) -> p (x g) t", t=BLK)
            lx8 = m.lx[:, :, :].rearrange("p x (g t) -> p (x g) t", t=BLK)
            done.inc(dve.tensor_copy(lx8[:, :, 1:BLK], lb8[:, :, 0:BLK - 1]))
            dve.wait_ge(al_exped, 1)
            then(dve.tensor_scalar(al[:, :, :], al[:, :, :], -1.0, 1.0, ALU.mult, ALU.add))
            dve.wait_ge(units, 2)
            then(dve.tensor_tensor(m.u[:, :, :], al[:, :, :], m.k[:, :].unsqueeze(1).broadcast_to([P, 2, TOK]), ALU.mult))
            done.inc(dve.tensor_tensor(m.u[:, 1, :], m.u[:, 1, :], upd[:, :], ALU.mult))
            dve.wait_ge(sum_inverse, 1)
            then(dve.tensor_tensor(lg[:, 1, :], lg[:, 1, :], top[:, :], ALU.mult))
            done.inc(dve.tensor_tensor(m.oq[:, 1, :], lg[:, 1, :], m.qh[:, :], ALU.mult))
            done.inc(dve.tensor_tensor(m.pw2[:, :], lg[:, 2, :], top[:, :], ALU.mult))
            dve.wait_ge(pool_weighted, 1)
            dve.wait_ge(dve_done, done.n)
            then(dve.tensor_scalar(m.qh[:, :], m.qh[:, :], 0.5, None, ALU.mult))


def factors(nc, c, m, f, bank):
    with ExitStack() as ctx:
        def sem(name):
            return ctx.enter_context(nc.semaphore(name))

        diff, exped, mult, summed, stored, pool_done = (sem("g_diff"), sem("g_exped"), sem("g_mult"), sem("g_summed"),
                                                        sem("g_stored"), sem("g_pool_done"))
        block = ctx.enter_context(nc.Block())

        def by(tensor, n):
            return tensor.rearrange("p x (g t) -> p x g t", t=n)

        lb8, lx8 = by(m.lb[:, :, :], BLK), by(m.lx[:, :, :], BLK)
        lb4, lx4, u4 = by(m.lb[:, :, :], HALF), by(m.lx[:, :, :], HALF), by(m.u[:, :, :], HALF)
        k4 = m.k[:, :].rearrange("p (g t) -> p g t", t=HALF)
        q4 = m.qh[:, :].rearrange("p (g t) -> p g t", t=HALF)
        k8 = m.k[:, :].rearrange("p (g t) -> p g t", t=BLK)
        q8 = m.qh[:, :].rearrange("p (g t) -> p g t", t=BLK)
        oq4, oq8 = by(m.oq[:, :, :], HALF), by(m.oq[:, :, :], BLK)
        z = [f.z[:, x, :, :, :].rearrange("p n b t -> p b n t") for x in range(2)]
        zn = [f.zn[:, x, :, :, :].rearrange("p n b t -> p b n t") for x in range(2)]
        lbn = [m.lb[:, x, :].rearrange("p (b n t) -> p b n t", b=BATCH, n=NB) for x in range(2)]
        un = [m.u[:, x, :].rearrange("p (b n t) -> p b n t", b=BATCH, n=NB) for x in range(2)]
        G8 = TOK // BLK
        CHUNK = 512
        cp_cols = f.cp[:, :, :, :, :].rearrange("p x k i g -> p (x k i g)")
        co_cols = f.co[:, :, :, :].rearrange("p x i g -> p (x i g)")
        chunks = ([cp_cols[:, a:a + CHUNK] for a in range(0, 4 * len(PAIR_S) * GROUPS, CHUNK)]
                  + [co_cols[:, a:a + CHUNK] for a in range(0, 2 * len(PAIR_O) * GROUPS, CHUNK)])
        n_cp = 4 * len(PAIR_S) * GROUPS // CHUNK
        near = [f.near[:, x, :, :, :] for x in range(2)]

        def end(x, i):
            return lb8[:, x, :, i].unsqueeze(2).broadcast_to([P, G8, HALF])

        @block.vector
        def _(dve):
            done = Tally(diff)
            for i, (s, r) in enumerate(PAIR_S):
                ins = dve.tensor_tensor(f.cp[:, :, 0, i, :], lx4[:, :, :, r], lb4[:, :, :, s], ALU.subtract)
            done.inc(ins)
            for i, (s, r) in enumerate(PAIR_O):
                if s < r:
                    ins = dve.tensor_tensor(f.co[:, :, i, :], lb4[:, :, :, r], lb4[:, :, :, s], ALU.subtract)
                else:
                    ins = dve.memset(f.co[:, :, i, :], 0.0)
            done.inc(ins)
            for x in range(2):
                ins = dve.tensor_tensor(z[x], lbn[x][:, :, :, BLK - 1:BLK].broadcast_to([P, BATCH, NB, BLK]), lbn[x],
                                        ALU.subtract)
            done.inc(ins)
            for x in range(2):
                dve.tensor_tensor(near[x][:, KIND_K], lx8[:, x, :, HALF:BLK], end(x, HALF - 1), ALU.subtract)
                dve.tensor_tensor(near[x][:, KIND_O], lb8[:, x, :, HALF:BLK], end(x, HALF - 1), ALU.subtract)
                dve.memset(zn[x][:, :, :, HALF:BLK], 0.0)
                ins = dve.tensor_tensor(zn[x][:, :, :, 0:HALF],
                                        lbn[x][:, :, :, HALF - 1:HALF].broadcast_to([P, BATCH, NB, HALF]),
                                        lbn[x][:, :, :, 0:HALF], ALU.subtract)
            done.inc(ins)

            md = Tally(mult)
            dve.wait_ge(exped, 1)
            for i, (s, r) in enumerate(PAIR_S):
                last = md.inc(dve.tensor_tensor(f.cp[:, :, 0, i, :], f.cp[:, :, 0, i, :], u4[:, :, :, s], ALU.mult))
            dve.wait_ge(mult, last)
            for i, (s, r) in enumerate(PAIR_S):
                last = md.inc(dve.tensor_tensor(f.cp[:, :, 1, i, :], f.cp[:, :, 0, i, :],
                                                q4[:, :, r].unsqueeze(1).broadcast_to([P, 2, GROUPS]), ALU.mult))
            dve.wait_ge(mult, last)
            for i, (s, r) in enumerate(PAIR_S):
                last = md.inc(dve.tensor_tensor(f.cp[:, :, 0, i, :], f.cp[:, :, 0, i, :],
                                                k4[:, :, r].unsqueeze(1).broadcast_to([P, 2, GROUPS]), ALU.mult))
            assert last == 3 * len(PAIR_S)
            dve.wait_ge(exped, 4)
            kb = m.k[:, :].unsqueeze(1).broadcast_to([P, 2, TOK])
            qb = m.qh[:, :].unsqueeze(1).broadcast_to([P, 2, TOK])
            for x in range(2):
                last = md.inc(dve.tensor_tensor(z[x], z[x], un[x], ALU.mult))
            last = md.inc(dve.tensor_tensor(f.far[:, :, KIND_Q, :], f.far[:, :, KIND_K, :], qb, ALU.mult))
            last = md.inc(dve.tensor_tensor(f.far[:, :, KIND_O, :], f.far[:, :, KIND_O, :], m.oq[:, :, :], ALU.mult))
            dve.wait_ge(mult, last)
            last = md.inc(dve.tensor_tensor(f.far[:, :, KIND_K, :], f.far[:, :, KIND_K, :], kb, ALU.mult))
            dve.wait_ge(exped, 5)
            for x in range(2):
                last = md.inc(dve.tensor_tensor(near[x][:, KIND_Q], near[x][:, KIND_K], q8[:, :, HALF:BLK], ALU.mult))
                last = md.inc(dve.tensor_tensor(near[x][:, KIND_O], near[x][:, KIND_O], oq8[:, x, :, HALF:BLK], ALU.mult))
                last = md.inc(dve.tensor_tensor(zn[x][:, :, :, 0:HALF], zn[x][:, :, :, 0:HALF], un[x][:, :, :, 0:HALF],
                                                ALU.mult))
                dve.wait_ge(mult, last)
                last = md.inc(dve.tensor_tensor(near[x][:, KIND_K], near[x][:, KIND_K], k8[:, :, HALF:BLK], ALU.mult))
            dve.wait_ge(mult, last)

        @block.scalar
        def _(act):
            act.wait_ge(diff, 1)
            act.activation(f.cp[:, :, 0, :, :], f.cp[:, :, 0, :, :], ACT.Exp).then_inc(exped, 1)
            act.wait_ge(diff, 2)
            act.activation(f.co[:, :, :, :], f.co[:, :, :, :], ACT.Exp).then_inc(exped, 1)
            act.activation(f.far[:, :, KIND_K, :], m.lx[:, :, :], ACT.Exp)
            act.activation(f.far[:, :, KIND_O, :], m.lb[:, :, :], ACT.Exp).then_inc(exped, 1)
            act.wait_ge(diff, 3)
            act.activation(f.z[:, :, :, :, :], f.z[:, :, :, :, :], ACT.Exp).then_inc(exped, 1)
            act.activation(f.dec[:, :, :], lb8[:, :, :, BLK - 1], ACT.Exp)
            act.wait_ge(diff, 4)
            for x in range(2):
                act.activation(near[x][:, KIND_K], near[x][:, KIND_K], ACT.Exp)
                act.activation(near[x][:, KIND_O], near[x][:, KIND_O], ACT.Exp)
                ins = act.activation(zn[x][:, :, :, 0:HALF], zn[x][:, :, :, 0:HALF], ACT.Exp)
            ins.then_inc(exped, 1)
            for k, cols in enumerate(chunks):
                act.wait_ge(summed, k + 1)
                act.activation(cols, bank[k % 8][:, :], ACT.Copy).then_inc(stored, 1)

        @block.gpsimd
        def _(pool):
            done = Tally(pool_done)
            pool.wait_ge(exped, 2)
            for i, (s, r) in enumerate(PAIR_O):
                last = done.inc(pool.tensor_tensor(f.co[:, :, i, :], f.co[:, :, i, :], u4[:, :, :, s], ALU.mult))
            pool.wait_ge(pool_done, last)
            for i, (s, r) in enumerate(PAIR_O):
                last = done.inc(pool.tensor_tensor(f.co[:, :, i, :], f.co[:, :, i, :], oq4[:, :, :, r], ALU.mult))

        @block.tensor
        def _(pe):
            pe.wait_ge(mult, 3 * len(PAIR_S))
            for k, cols in enumerate(chunks):
                if k == n_cp:
                    pe.wait_ge(pool_done, 2 * len(PAIR_O))
                if k >= 8:
                    pe.wait_ge(stored, k - 7)
                pe.matmul(bank[k % 8][:, :], c.ones[:, :], cols, start=True, stop=True).then_inc(summed, 1)


def scan(nc, c, m, f, s, bank):
    acc = [bank[0:2], bank[2:4]]
    ring, errb, wtb = bank[4:6], bank[6], bank[7]
    with ExitStack() as ctx:
        def sb(name, shape):
            return ctx.enter_context(nc.sbuf_tensor(name, shape, F32))

        def sem(name):
            return ctx.enter_context(nc.semaphore(name))

        res = sb("res", [P, 2, 2, BATCH, BLK])
        w = sb("w", [P, 2, 2, BATCH, BLK])
        pred, sq = sb("pred", [P, BATCH]), sb("sqe", [P, BATCH])
        tmp1, tmp2 = sb("tmp1", [P, 4, BATCH]), sb("tmp2", [P, 4, 2, BATCH])
        tmpo = sb("tmpo", [P, 2, HALF, BATCH])
        raw = [sb(f"raw_coef{k}", [P, 3, BATCH, BLK]) for k in range(2)]

        dve_done, sq_ready, err_ready, sig_ready, w_ready = (sem("s_dve_done"), sem("s_sq_ready"), sem("s_err_ready"),
                                                             sem("s_sig_ready"), sem("s_w_ready"))
        x_done, x_out, acc_ready, acc_read = sem("s_x_done"), sem("s_x_out"), sem("s_acc_ready"), sem("s_acc_read")
        wt_ready, wt_out, z_ready, out_done, pool_done = (sem("s_wt_ready"), sem("s_wt_out"), sem("s_z_ready"),
                                                          sem("s_out_done"), sem("s_pool_done"))
        x_copied, x_masked = sem("s_x_copied"), sem("s_x_masked")
        block = ctx.enter_context(nc.Block())

        v5 = m.v[:, :].rearrange("p (b n t) -> p b n t", b=BATCH, n=NB)
        sig5 = m.sig[:, :].rearrange("p (b n t) -> p b n t", b=BATCH, n=NB)
        out5 = m.out[:, :, :].rearrange("p x (b n t) -> p x b n t", b=BATCH, n=NB)
        z5 = f.z[:, :, :, :, :].rearrange("p x n b t -> p x n (b t)")
        zn5 = f.zn[:, :, :, :, :].rearrange("p x n b t -> p x n (b t)")
        far5 = f.far[:, :, :, :].rearrange("p x k (b n t) -> p x k b n t", b=BATCH, n=NB)
        near5 = f.near[:, :, :, :, :].rearrange("p x k (b n) t -> p x k b n t", b=BATCH)
        dec5 = f.dec[:, :, :].rearrange("p x (b n) -> p x b n", b=BATCH)
        cp = f.cp[:, :, :, :, :].rearrange("p x k i (b g) -> p (x k) i b g", b=BATCH)
        co = f.co[:, :, :, :].rearrange("p x i (b g) -> p x i b g", b=BATCH)
        accv = [[a[:, 0:3 * P].rearrange("p (k b t) -> p k b t", k=3, b=BATCH) for a in pair] for pair in acc]
        res4 = res[:, :, :, :, :].rearrange("p x k b t -> p (x k) b t")
        w4 = w[:, :, :, :, :].rearrange("p x k b t -> p (x k) b t")

        SPAN = BLK - 1

        def items(n):
            steps = [[] for _ in range(BLK)]
            if n == NB:
                return steps
            cross = [(k, x) for k in range(n) for x in range(2)]
            for i, (k, x) in enumerate(cross):
                steps[i * SPAN // len(cross)].append(("cross", k, x))
            for i, (k, x) in enumerate(cross[:-2]):
                steps[i * SPAN // len(cross) + 2].append(("read", k, x))
            steps[-1] += [("near", n, x) for x in range(2)]
            return steps

        def by_pool(step, it):
            return it[0] == "cross" and [j for j in step if j[0] == "cross"].index(it) == 1

        def coef(n, kind, k, x):
            if kind == "cross":
                return s.cross[:, k, x, :, :, :]
            return s.near[:, n % 2, x, :, :, :]

        ring_at = {}
        freed, stored = [], {}
        counts = {"dve": 0, "pool": 0}
        for n in range(NB):
            for step in items(n) if n else [[("near", 0, x) for x in range(2)]]:
                for it in step:
                    if it[0] != "read":
                        ring_at[(n,) + it] = len(ring_at)
                        e = "pool" if by_pool(step, it) else "dve"
                        counts[e] += 1
                        freed.append((x_copied if e == "pool" else x_out, counts[e]))
                        stored[(n,) + it] = (x_masked if e == "pool" else x_out, counts[e])

        @block.tensor
        def _(pe):
            def product(n, kind, k, x):
                q = ring_at[n, kind, k, x]
                if q >= 2:
                    pe.wait_ge(*freed[q - 2])
                b = ring[q % 2]
                if kind == "cross":
                    pe.matmul(b[:, 0:3 * P].rearrange("p (k b t) -> p k b t", k=3, b=BATCH), z5[:, x, k, :],
                              far5[:, x, :, :, n, :], start=True, stop=True).then_inc(x_done, 1)
                else:
                    pe.matmul(b[:, 0:3 * P // 2].rearrange("p (k b t) -> p k b t", k=3, b=BATCH), zn5[:, x, n, :],
                              near5[:, x, :, :, n, :], start=True, stop=True).then_inc(x_done, 1)

            def read_far(n, k, x):
                pe.wait_ge(*stored[n, "cross", k, x])
                if k == 0 and n >= 2:
                    pe.wait_ge(acc_read, 2 * (n - 1))
                return pe.matmul(accv[n % 2][x], s.wt[:, k, x, :], s.cross[:, k, x, :, :, :],
                                 start=(k == 0), stop=(k == n - 1), skip_group_check=True)

            def turn_w(n, h):
                pe.wait_ge(w_ready, BLK * n + HALF * (h + 1))
                if 2 * n + h >= 1:
                    pe.wait_ge(wt_out, 2 * n + h)
                for x in range(2):
                    ins = pe.transpose(wtb[:, x * P:(x + 1) * P], w[:, x, 0, :, :].rearrange("p b t -> p (b t)"),
                                       c.ident[:, :])
                ins.then_inc(wt_ready, 1)
                pe.wait_ge(wt_out, 2 * n + h + 1)

            def prepare(n, t, kinds):
                for kind, k, x in items(n + 1)[t]:
                    if kind in kinds:
                        if kind == "read":
                            read_far(n + 1, k, x)
                        else:
                            product(n + 1, kind, k, x)

            for x in range(2):
                product(0, "near", 0, x)
            for n in range(NB):
                if 1 <= n < NB - 1:
                    zwait = n
                else:
                    zwait = 0
                for t in range(BLK):
                    T = BLK * n + t
                    pe.wait_ge(sq_ready, T + 1)
                    pe.matmul(errb[:, 0:BATCH], c.ones[:, :], sq[:, :], start=True, stop=True).then_inc(err_ready, 1)
                    if t == 0 and zwait:
                        pe.wait_ge(z_ready, zwait)
                    if t != HALF - 1:
                        prepare(n, t, ("read", "cross"))
                    if t == HALF - 1:
                        turn_w(n, 0)
                        pe.wait_ge(acc_read, 2 * n + 1)
                        for x in range(2):
                            pe.wait_ge(*stored[n, "near", n, x])
                            ins = pe.matmul(accv[n % 2][x][:, :, :, HALF:BLK], s.wt[:, n, x, :],
                                            s.near[:, n % 2, x, :, :, :], start=(n == 0), stop=True,
                                            skip_group_check=True)
                        ins.then_inc(acc_ready, 1)
                        prepare(n, t, ("read", "cross"))
                    if t == BLK - 1 and n < NB - 1:
                        turn_w(n, 1)
                        for x in range(2):
                            ins = read_far(n + 1, n, x)
                        ins.then_inc(acc_ready, 1)
                        prepare(n, t, ("near",))

        @block.scalar
        def _(act):
            def copy_coefs(n, k, x):
                act.wait_ge(x_done, ring_at[n, "cross", k, x] + 1)
                i = stored[n, "cross", k, x][1]
                if i > 2:
                    act.wait_ge(x_masked, i - 2)
                act.activation(raw[i % 2][:, :, :, :].rearrange("p k b t -> p (k b t)"),
                               ring[ring_at[n, "cross", k, x] % 2][:, 0:3 * P], ACT.Copy).then_inc(x_copied, 1)

            for n in range(NB):
                work = items(n + 1)
                for t in range(BLK):
                    act.wait_ge(err_ready, BLK * n + t + 1)
                    act.activation(sig5[:, :, n, t], errb[:, 0:BATCH], ACT.Sigmoid, scale=1.0 / (1.0 + 1e-6)
                                   ).then_inc(sig_ready, 1)
                    if t in (HALF - 1, BLK - 1) and (n < NB - 1 or t < BLK - 1):
                        act.wait_ge(wt_ready, 2 * n + t // HALF + 1)
                        act.activation(s.wt[:, n, :, :].rearrange("p x v -> p (x v)"), wtb[:, 0:2 * P], ACT.Copy
                                       ).then_inc(wt_out, 1)
                    for it in work[t]:
                        if by_pool(work[t], it):
                            copy_coefs(n + 1, *it[1:])

        @block.gpsimd
        def _(pool):
            done = Tally(pool_done)
            last = done.inc(pool.memset(m.out[:, :, :], 0.0))
            pool.wait_ge(pool_done, last)
            pool.sem_inc(out_done, 1)
            for n in range(NB):
                work = items(n + 1)
                for t in range(BLK):
                    h, s0 = divmod(t, HALF)
                    i0 = PAIR_O.index((s0, s0))
                    cnt = HALF - s0
                    pool.wait_ge(w_ready, BLK * n + t + 1)
                    last = done.inc(pool.tensor_tensor(
                        tmpo[:, :, 0:cnt, :], co[:, :, i0:i0 + cnt, :, 2 * n + h],
                        w[:, :, 0, :, t].unsqueeze(2).broadcast_to([P, 2, cnt, BATCH]), ALU.mult))
                    pool.wait_ge(pool_done, last)
                    o = out5[:, :, :, n, t:HALF * (h + 1)].rearrange("p x b t -> p x t b")
                    last = done.inc(pool.tensor_tensor(o, o, tmpo[:, :, 0:cnt, :], ALU.add))
                    pool.wait_ge(pool_done, last)
                    pool.sem_inc(out_done, 1)
                    for it in work[t]:
                        if by_pool(work[t], it):
                            i = stored[(n + 1,) + it][1]
                            pool.wait_ge(x_copied, i)
                            own = c.batch_mask[:, :].unsqueeze(1).unsqueeze(3).broadcast_to([P, 3, BATCH, BLK])
                            pool.tensor_tensor(coef(n + 1, *it), raw[i % 2][:, :, :, :], own, ALU.mult).then_inc(x_masked, 1)
                    if t == SPAN - 1 and 1 <= n + 1 < NB - 1:
                        pool.wait_ge(x_done, max(q for key, q in ring_at.items() if key[0:2] == (n + 1, "cross")) + 1)
                        for x in range(2):
                            zb = f.z[:, x, 0:n + 1, :, :]
                            last = done.inc(pool.tensor_tensor(zb, zb, dec5[:, x, :, n + 1].unsqueeze(1).unsqueeze(3)
                                                               .broadcast_to([P, n + 1, BATCH, BLK]), ALU.mult))
                        pool.wait_ge(pool_done, last)
                        pool.sem_inc(z_ready, 1)

        @block.vector
        def _(dve):
            done = Tally(dve_done)

            def then(ins):
                dve.wait_ge(dve_done, done.inc(ins))

            def store_coefs(n, kind, k, x):
                q = ring_at[n, kind, k, x]
                dve.wait_ge(x_done, q + 1)
                width = BLK if kind == "cross" else HALF
                src = ring[q % 2][:, 0:3 * BATCH * width].rearrange("p (k b t) -> p k b t", k=3, b=BATCH)
                own = c.batch_mask[:, :].unsqueeze(1).unsqueeze(3).broadcast_to([P, 3, BATCH, width])
                dve.tensor_tensor(coef(n, kind, k, x), src, own, ALU.mult).then_inc(x_out, 1)

            then(dve.memset(w[:, :, :, :, :], 0.0))
            for x in range(2):
                store_coefs(0, "near", 0, x)
            for n in range(NB):
                work = items(n + 1)
                for t in range(BLK):
                    T = BLK * n + t
                    h, r = divmod(t, HALF)
                    lo, hi = HALF * h, HALF * (h + 1)
                    if r == 0:
                        vh = v5[:, :, n, lo:hi]
                        if T == 0:
                            done.inc(dve.tensor_copy(res[:, 0, :, :, lo:hi], vh.unsqueeze(1).broadcast_to([P, 2, BATCH, HALF])))
                            done.inc(dve.tensor_copy(res[:, 1, 0, :, lo:hi], vh))
                            done.inc(dve.memset(res[:, 1, 1, :, lo:hi], 0.0))
                        else:
                            dve.wait_ge(acc_ready, 2 * n + h)
                            a = accv[n % 2]
                            done.inc(dve.tensor_tensor(res[:, 0, :, :, lo:hi], vh.unsqueeze(1).broadcast_to([P, 2, BATCH, HALF]),
                                                       a[0][:, 0:2, :, lo:hi], ALU.subtract))
                            done.inc(dve.tensor_tensor(res[:, 1, 0, :, lo:hi], vh, a[1][:, 0, :, lo:hi], ALU.subtract))
                            done.inc(dve.tensor_scalar(res[:, 1, 1, :, lo:hi], a[1][:, 1, :, lo:hi], -1.0, None, ALU.mult))
                        dve.wait_ge(dve_done, done.n)
                    else:
                        i = PAIR_S.index((r - 1, r))
                        then(dve.tensor_tensor(tmp1[:, :, :], cp[:, :, i, :, 2 * n + h], w4[:, :, :, t - 1], ALU.mult))
                        then(dve.tensor_tensor(res4[:, :, :, t], res4[:, :, :, t], tmp1[:, :, :], ALU.subtract))
                    then(dve.tensor_tensor(pred[:, :], res[:, 0, 1, :, t], res[:, 1, 1, :, t], ALU.add))
                    if T:
                        dve.wait_ge(err_ready, T)
                    dve.tensor_tensor(sq[:, :], pred[:, :], pred[:, :], ALU.mult).then_inc(sq_ready, 1)
                    if r == 0:
                        if T:
                            dve.wait_ge(out_done, 1)
                            for x in range(2):
                                done.inc(dve.tensor_copy(out5[:, x, :, n, lo:hi], accv[n % 2][x][:, KIND_O, :, lo:hi]))
                            dve.wait_ge(dve_done, done.n)
                        dve.sem_inc(acc_read, 1)
                    elif r < HALF - 1:
                        cnt = HALF - 1 - r
                        i = PAIR_S.index((r - 1, r + 1))
                        later = res4[:, :, :, t + 1:hi].rearrange("p c b t -> p c t b")
                        then(dve.tensor_tensor(tmp2[:, :, 0:cnt, :], cp[:, :, i:i + cnt, :, 2 * n + h],
                                               w4[:, :, :, t - 1].unsqueeze(2).broadcast_to([P, 4, cnt, BATCH]), ALU.mult))
                        done.inc(dve.tensor_tensor(later, later, tmp2[:, :, 0:cnt, :], ALU.subtract))
                    for it in work[t - 1] if t else items(n)[-1] if n else []:
                        if it[0] != "read" and not by_pool(work[t - 1] if t else [], it):
                            store_coefs(n + 1 if t else n, *it)
                    dve.wait_ge(sig_ready, T + 1)
                    dve.wait_ge(dve_done, done.n)
                    if T >= BLK:
                        dve.wait_ge(out_done, T - BLK + 2)
                    ins = dve.tensor_tensor(w[:, :, :, :, t], res[:, :, 0, :, t].unsqueeze(2).broadcast_to([P, 2, 2, BATCH]),
                                            sig5[:, :, n, t].unsqueeze(1).unsqueeze(1).broadcast_to([P, 2, 2, BATCH]), ALU.mult)
                    ins.then_inc(w_ready, 1)
                    dve.wait_ge(w_ready, T + 1)


def memory_output(nc, io, c, t, m, w, bank):
    with ExitStack() as ctx:
        def sem(name):
            return ctx.enter_context(nc.semaphore(name))

        tmp = ctx.enter_context(nc.sbuf_tensor("mo_tmp", [P, TOK], F32))
        keep = ctx.enter_context(nc.sbuf_tensor("mo_keep", [P, TOK], F32))
        dve_done, sq_ready, summed, rooted = (sem("o_dve_done"), sem("o_sq_ready"), sem("o_summed"),
                                                    sem("o_rooted"))
        normed, projected, var_ready, std_ready = sem("o_normed"), sem("o_projected"), sem("o_var_ready"), sem("o_std_ready")
        y_ready, turned, moved = sem("o_y_ready"), sem("o_turned"), sem("o_moved")
        block = ctx.enter_context(nc.Block())

        @block.vector
        def _(dve):
            done = Tally(dve_done)

            def then(ins):
                dve.wait_ge(dve_done, done.inc(ins))

            then(dve.tensor_scalar(tmp[:, :], m.sig[:, :], 0.7, 0.1, ALU.is_gt, ALU.mult))
            then(dve.tensor_scalar(keep[:, :], tmp[:, :], -1.0, 1.0, ALU.mult, ALU.add))
            then(dve.memset(keep[:, :].rearrange("p (b t) -> p b t", t=STEPS)[:, :, 0], 0.0))
            then(dve.tensor_tensor(m.nu[:, :], m.nu[:, :], tmp[:, :], ALU.mult))
            then(dve.tensor_tensor_scan(tmp[:, :], keep[:, :], m.nu[:, :], 0.0, ALU.mult, ALU.add))
            then(dve.tensor_tensor(tmp[:, :], tmp[:, :], m.pw2[:, :], ALU.mult))
            then(dve.tensor_tensor(tmp[:, :], tmp[:, :], m.out[:, 0, :], ALU.add))
            then(dve.tensor_tensor(tmp[:, :], tmp[:, :], m.out[:, 1, :], ALU.add))
            dve.tensor_tensor(m.sig[:, :], tmp[:, :], tmp[:, :], ALU.mult).then_inc(sq_ready, 1)
            for h in range(2):
                dve.wait_ge(summed, h + 1)
                done.inc(dve.tensor_scalar(keep[:, 512 * h:512 * h + 512], bank[h][:, :], 1.0 / DS, 1e-6, ALU.mult, ALU.add))
            dve.wait_ge(dve_done, done.n)
            dve.sem_inc(sq_ready, 1)
            dve.wait_ge(rooted, 2)
            dve.scalar_tensor_tensor(out=tmp[:, :], in0=tmp[:, :], scalar=w.norm[:, 0:1], in1=keep[:, :],
                                     op0=ALU.mult, op1=ALU.mult).then_inc(normed, 1)
            for n in range(TILES):
                dve.wait_ge(projected, n + 1)
                last = done.inc(dve.tensor_tensor(t.x[:, n, :], bank[n][:, 0:DM], t.x[:, n, :], ALU.add))
            dve.wait_ge(dve_done, last)
            last = row_stats(dve, t, t.x, done)
            dve.wait_ge(dve_done, last)
            dve.sem_inc(var_ready, 1)
            dve.wait_ge(std_ready, 1)
            last = normalise(dve, t, t.y, t.x, done)
            dve.wait_ge(dve_done, last)
            dve.sem_inc(y_ready, 1)
            for n in range(TILES):
                dve.wait_ge(turned, n + 1)
                dve.tensor_copy(t.yT[:, :, n * P:(n + 1) * P],
                                bank[n][:, 0:DM].rearrange("p (j q) -> p j q", j=CI)).then_inc(moved, 1)

        @block.scalar
        def _(act):
            act.wait_ge(sq_ready, 2)
            act.activation(keep[:, :], keep[:, :], ACT.Ln).then_inc(rooted, 1)
            act.wait_ge(rooted, 1)
            act.activation(keep[:, :], keep[:, :], ACT.Exp, scale=-0.5).then_inc(rooted, 1)
            act.wait_ge(var_ready, 1)
            act.activation(t.std[:, :], t.var[:, :], ACT.Sqrt).then_inc(std_ready, 1)

        @block.tensor
        def _(pe):
            pe.wait_ge(sq_ready, 1)
            for h in range(2):
                pe.matmul(bank[h][:, :], c.ones[:, :], m.sig[:, 512 * h:512 * h + 512], start=True, stop=True
                          ).then_inc(summed, 1)
            pe.wait_ge(normed, 1)
            for n in range(TILES):
                pe.matmul(bank[n][:, 0:DM], tmp[:, n * P:(n + 1) * P], w.o[:, :], start=True, stop=True).then_inc(projected, 1)
            pe.wait_ge(y_ready, 1)
            for n in range(TILES):
                for i in range(CI):
                    ins = pe.transpose(bank[n][:, i * P:(i + 1) * P], t.y[:, n, i * P:(i + 1) * P], c.ident[:, :])
                ins.then_inc(turned, 1)


EXPERTS, EW, TOPK = 64, 96, 8
SLABS = EXPERTS * EW // P
CW_GROUP = 32
CW_COPIES = EW // CW_GROUP
CW_ROWS = P // CW_GROUP
WS, XS, HS = 64.0, 64.0, 16.0


def route(nc, io, c, t, w, f, cw_rows, bank):
    with ExitStack() as ctx:
        def sb(name, shape):
            return ctx.enter_context(nc.sbuf_tensor(name, shape, F32))

        def sem(name):
            return ctx.enter_context(nc.semaphore(name))

        prob, rest = sb("r_prob", [P, TILES, EXPERTS]), sb("r_rest", [P, TILES, EXPERTS])
        top, cwT = sb("r_top", [P, TILES, TOPK]), sb("cwT", [EXPERTS, TOK])
        neg, den, sum8 = sb("r_neg", [P, TILES]), sb("r_den", [P, TILES]), sb("r_sum8", [P, TILES])
        routed, neg_ready, exped, dve_done = sem("r_routed"), sem("r_neg_ready"), sem("r_exped"), sem("r_dve_done")
        first_in, x_high = sem("r_first_in"), sem("r_x_high")
        chosen, turned, moved, stored = sem("r_chosen"), sem("r_turned"), sem("r_moved"), sem("r_stored")
        block = ctx.enter_context(nc.Block())

        @block.sync
        def _(sp):
            for u in range(2):
                load_weights(sp, io, f, u, u, first_in)
            sp.wait_ge(first_in, 64)
            sp.wait_ge(moved, 2)
            for k in range(CW_COPIES):
                sp.dma_start(cw_rows.rearrange("(e k) t -> k e t", k=CW_COPIES)[k], cwT[:, :]).then_inc(stored, 16)
            sp.wait_ge(stored, 16 * CW_COPIES)

        @block.tensor
        def _(pe):
            for n in range(TILES):
                for i in range(CI):
                    ins = pe.matmul(bank[n][:, 0:EXPERTS], t.yT[:, i, n * P:(n + 1) * P], w.router[:, i, :],
                                    start=(i == 0), stop=(i == CI - 1))
                ins.then_inc(routed, 1)
            pe.wait_ge(chosen, 1)
            for n in range(TILES):
                ins = pe.transpose(bank[n // 4][0:EXPERTS, (n % 4) * P:(n % 4 + 1) * P], prob[:, n, :], c.ident[:, :])
                if n % 4 == 3:
                    ins.then_inc(turned, 1)

        @block.scalar
        def _(act):
            act.activation(f.x_hl[0][:, :, :], t.yT[:, :, :], ACT.Copy, scale=XS).then_inc(x_high, 1)
            for n in range(TILES):
                act.wait_ge(neg_ready, n + 1)
                act.activation(prob[:, n, :], bank[n][:, 0:EXPERTS], ACT.Exp, bias=neg[:, n:n + 1],
                               accum_out=den[:, n:n + 1]).then_inc(exped, 1)

        @block.vector
        def _(dve):
            done = Tally(dve_done)

            def then(ins):
                dve.wait_ge(dve_done, done.inc(ins))

            for n in range(TILES):
                dve.wait_ge(routed, n + 1)
                dve.tensor_reduce(neg[:, n:n + 1], bank[n][:, 0:EXPERTS], AX.X, ALU.max, negate=True).then_inc(neg_ready, 1)
            dve.wait_ge(x_high, 1)
            dve.scalar_tensor_tensor(out=f.x_hl[1][:, :, :].rearrange("p i n -> p (i n)"),
                                     in0=t.yT[:, :, :].rearrange("p i n -> p (i n)"), scalar=XS,
                                     in1=f.x_hl[0][:, :, :].rearrange("p i n -> p (i n)"), op0=ALU.mult, op1=ALU.subtract)
            dve.wait_ge(exped, TILES)
            then(dve.reciprocal(den[:, :], den[:, :]))
            for n in range(TILES):
                done.inc(dve.tensor_scalar(prob[:, n, :], prob[:, n, :], den[:, n:n + 1], None, ALU.mult))
            dve.wait_ge(dve_done, done.n)
            for n in range(TILES):
                done.inc(dve.max(top[:, n, :], prob[:, n, :]))
            dve.wait_ge(dve_done, done.n)
            for n in range(TILES):
                done.inc(dve.match_replace(rest[:, n, :], top[:, n, :], prob[:, n, :], 0.0))
            dve.wait_ge(dve_done, done.n)
            done.inc(dve.tensor_tensor(prob[:, :, :], prob[:, :, :], rest[:, :, :], ALU.subtract))
            then(dve.tensor_reduce(sum8[:, :], top[:, :, :], AX.X, ALU.add))
            then(dve.reciprocal(sum8[:, :], sum8[:, :]))
            for n in range(TILES):
                done.inc(dve.tensor_scalar(prob[:, n, :], prob[:, n, :], sum8[:, n:n + 1], None, ALU.mult))
            dve.wait_ge(dve_done, done.n)
            dve.sem_inc(chosen, 1)
            for k in range(2):
                dve.wait_ge(turned, k + 1)
                dve.tensor_copy(cwT[:, 512 * k:512 * k + 512], bank[k][0:EXPERTS, :]).then_inc(moved, 1)


def load_weights(sp, io, f, e, u, done):
    one = bass.ds(e, 1)
    sp.dma_start(f.wgu[u][:, :, :, :], io["guT"][one].rearrange("o p i g w -> p (o i) g w")).then_inc(done, 16)
    sp.dma_start(f.wd[u][:, :], io["downT"][one].rearrange("o w d -> (o w) d")).then_inc(done, 16)


def experts(nc, io, t, f, cw_rows, bank):
    acc = bank[0:4]
    gate, up = bank[4:6], bank[6:8]
    wgu, wd, x_hl = f.wgu, f.wd, f.x_hl
    with ExitStack() as ctx:
        def sb(name, shape, dt=F32):
            return ctx.enter_context(nc.sbuf_tensor(name, shape, dt))

        def sem(name):
            return ctx.enter_context(nc.semaphore(name))

        wgu_hl = [[sb(f"wgu{part}{u}", [P, CI, 2, P], F16) for part in "hl"] for u in range(2)]
        wd_hl = [[sb(f"wd{part}{u}", [P, DM], F16) for part in "hl"] for u in range(2)]
        cw = [sb(f"cw{u}", [P, TOK]) for u in range(2)]
        silu = [sb(f"silu{h}", [P, 512]) for h in range(2)]
        upw = [sb(f"upw{h}", [P, 512]) for h in range(2)]
        hid = [sb(f"hid{h}", [P, 512]) for h in range(2)]
        hid_hl = [[sb(f"hid{part}{h}", [P, 512], F16) for part in "hl"] for h in range(2)]
        zeros = sb("zeros", [P, P], F16)
        w_in, cw_in = [sem(f"e_w_in{u}") for u in range(2)], [sem(f"e_cw_in{u}") for u in range(2)]
        zeroed, gated, upped, silued, weighted, hid_ready = (sem("e_zeroed"), sem("e_gated"), sem("e_upped"), sem("e_silued"),
                                                             sem("e_weighted"), sem("e_hid_ready"))
        w_high, w_low, hid_high, hid_low = sem("e_w_high"), sem("e_w_low"), sem("e_hid_high"), sem("e_hid_low")
        down_done, out_ready, out_sent = sem("e_down_done"), sem("e_out_ready"), sem("e_out_sent")
        block = ctx.enter_context(nc.Block())

        def load_cw(sp, e, u):
            for k in range(CW_ROWS):
                sp.dma_start(cw[u][k * CW_GROUP:(k + 1) * CW_GROUP, :],
                             cw_rows[bass.ds(e * CW_ROWS + k, 1), :].broadcast_to([CW_GROUP, TOK])).then_inc(cw_in[u], 16)

        @block.sync
        def _(sp):
            load_cw(sp, 0, 0)
            load_cw(sp, 1, 1)
            with sp.Fori(0, SLABS // 2 - 1) as i:
                for u in range(2):
                    sp.wait_ge(w_low, 4 * i + 2 * u + 2)
                    load_weights(sp, io, f, 2 * i + u + 2, u, w_in[u])
                    sp.wait_ge(weighted, 4 * i + 2 * u + 2)
                    load_cw(sp, 2 * i + u + 2, u)
            for n in range(TILES // 2):
                sp.wait_ge(out_ready, 2 * n + 2)
                sp.dma_start(io["out"].rearrange("b t d -> (b t) d").rearrange("(n p) d -> p n d", p=P)[:, 2 * n:2 * n + 2, :],
                             t.x[:, 2 * n:2 * n + 2, :]).then_inc(out_sent, 16)
            sp.wait_ge(out_sent, 16 * TILES // 2)

        @block.gpsimd
        def _(pool):
            pool.memset(zeros[:, :], 0.0).then_inc(zeroed, 1)

        @block.tensor
        def _(pe):
            def gate_up(q, r, first=False):
                u, h = (r // 2) % 2, r % 2
                if h == 0:
                    pe.wait_ge(w_low, q + 2)
                if not first:
                    pe.wait_ge(hid_ready, q - 1)
                cols = slice(512 * h, 512 * h + 512)
                for g, (dst, done) in enumerate(((gate[h], gated), (up[h], upped))):
                    terms = [(a, b, i) for a, b in ((0, 0), (0, 1), (1, 0)) for i in range(CI)]
                    for k, (a, b, i) in enumerate(terms):
                        ins = pe.matmul(dst[:, :], wgu_hl[u][a][:, i, g, :], x_hl[b][:, i, cols],
                                        start=(k == 0), stop=(k == len(terms) - 1))
                    ins.then_inc(done, 1)

            def down(q, r):
                u, h = (r // 2) % 2, r % 2
                pe.wait_ge(hid_low, q + 1)
                for k in range(4):
                    n = 4 * h + k
                    for a, b in ((0, 0), (0, 1), (1, 0)):
                        ins = pe.matmul(acc[n // 2][:, (n % 2) * DM:(n % 2 + 1) * DM], hid_hl[h][a][:, k * P:(k + 1) * P],
                                        wd_hl[u][b][:, :], start=False, stop=True, skip_group_check=True)
                ins.then_inc(down_done, 1)

            pe.wait_ge(zeroed, 1)
            for a in acc:
                pe.matmul(a[:, :], zeros[:, :], x_hl[0][:, 0, 0:512], start=True, stop=True)
            gate_up(0, 0, True)
            gate_up(1, 1, True)
            down(0, 0)
            with pe.Fori(0, SLABS // 2 - 1) as i:
                for r in range(4):
                    gate_up(4 * i + r + 2, r + 2)
                    down(4 * i + r + 1, r + 1)
            last = 2 * SLABS - 4
            for r in range(2):
                gate_up(last + r + 2, r + 2)
                down(last + r + 1, r + 1)
            down(last + 3, 3)

        @block.scalar
        def _(act):
            def split_weights(e, u, loads, first):
                if not first:
                    act.wait_ge(w_in[u], 32 * loads)
                    act.wait_ge(down_done, 2 * e - 2)
                act.activation(wgu_hl[u][0][:, :, :, :], wgu[u][:, :, :, :], ACT.Copy, scale=WS).then_inc(w_high, 1)
                act.activation(wd_hl[u][0][:, :], wd[u][:, :], ACT.Copy, scale=WS).then_inc(w_high, 1)

            def unit(q, r, first=False):
                h = r % 2
                act.wait_ge(gated, q + 1)
                if not first:
                    act.wait_ge(hid_ready, q - 1)
                act.activation(silu[h][:, :], gate[h][:, :], ACT.Silu, scale=1.0 / (WS * XS)).then_inc(silued, 1)
                act.wait_ge(hid_ready, q + 1)
                if not first:
                    act.wait_ge(down_done, q - 1)
                act.activation(hid_hl[h][0][:, :], hid[h][:, :], ACT.Copy).then_inc(hid_high, 1)

            split_weights(0, 0, 0, True)
            split_weights(1, 1, 0, True)
            for r in range(2):
                unit(r, r, True)
            with act.Fori(0, SLABS // 2 - 1) as i:
                for u in range(2):
                    unit(4 * i + 2 * u + 2, 2)
                    split_weights(2 * i + 2 + u, u, i + 1, False)
                    unit(4 * i + 2 * u + 3, 3)
            for r in range(2, 4):
                unit(2 * SLABS - 4 + r, r)

        @block.vector
        def _(dve):
            def split_weights(e, u):
                for k, (w, hl) in enumerate(((wgu, wgu_hl), (wd, wd_hl))):
                    dve.wait_ge(w_high, 2 * e + k + 1)
                    if k == 0:
                        src, high, low = w[u][:, :, :, :], hl[u][0][:, :, :, :], hl[u][1][:, :, :, :]
                        src, high, low = (a.rearrange("p i g w -> p (i g w)") for a in (src, high, low))
                    else:
                        src, high, low = w[u][:, :], hl[u][0][:, :], hl[u][1][:, :]
                    dve.scalar_tensor_tensor(out=low, in0=src, scalar=WS, in1=high, op0=ALU.mult,
                                             op1=ALU.subtract).then_inc(w_low, 1)

            def unit(q, r, loads, first=False):
                u, h = (r // 2) % 2, r % 2
                if h == 0:
                    dve.wait_ge(cw_in[u], 16 * CW_ROWS * loads)
                dve.wait_ge(upped, q + 1)
                if not first:
                    dve.wait_ge(hid_ready, q - 1)
                dve.scalar_tensor_tensor(out=upw[h][:, :], in0=up[h][:, :], scalar=HS / (WS * XS),
                                         in1=cw[u][:, 512 * h:512 * h + 512], op0=ALU.mult, op1=ALU.mult
                                         ).then_inc(weighted, 1)
                dve.wait_ge(weighted, q + 1)
                dve.wait_ge(silued, q + 1)
                if not first:
                    dve.wait_ge(hid_low, q - 1)
                dve.tensor_tensor(hid[h][:, :], upw[h][:, :], silu[h][:, :], ALU.mult).then_inc(hid_ready, 1)

            def low(q, r):
                h = r % 2
                dve.wait_ge(hid_high, q + 1)
                dve.tensor_tensor(hid_hl[h][1][:, :], hid[h][:, :], hid_hl[h][0][:, :], ALU.subtract).then_inc(hid_low, 1)

            split_weights(0, 0)
            split_weights(1, 1)
            for r in range(2):
                unit(r, r, 1, True)
                low(r, r)
            with dve.Fori(0, SLABS // 2 - 1) as i:
                for u in range(2):
                    q = 4 * i + 2 * u + 2
                    unit(q, 2 + 2 * u, i + 1 + u)
                    low(q, 0)
                    split_weights(2 * i + 2 + u, u)
                    unit(q + 1, 3 + 2 * u, i + 1 + u)
                    low(q + 1, 1)
            for r in range(2, 4):
                unit(2 * SLABS - 4 + r, r, SLABS // 2)
                low(2 * SLABS - 4 + r, r)
            dve.wait_ge(down_done, 2 * SLABS)
            for n in range(TILES):
                dve.scalar_tensor_tensor(out=t.x[:, n, :], in0=acc[n // 2][:, (n % 2) * DM:(n % 2 + 1) * DM],
                                         scalar=1.0 / (WS * HS), in1=t.x[:, n, :], op0=ALU.mult, op1=ALU.add
                                         ).then_inc(out_ready, 1)


def store_rows(nc, src, dst):
    with nc.semaphore("st_out") as st_out, nc.Block() as block:
        @block.sync
        def _(sp):
            sp.dma_start(dst.rearrange("b t d -> (b t) d").rearrange("(n p) d -> p n d", p=P), src[:, :, :]
                         ).then_inc(st_out, 16)
            sp.wait_ge(st_out, 16)


def perceiver_layer(nc, io, upto=9):
    with ExitStack() as ctx:
        def sb(name, shape):
            return ctx.enter_context(nc.sbuf_tensor(name, shape, F32))

        bank = [ctx.enter_context(nc.psum_tensor(f"bank{n}", [P, 512], F32)) for n in range(8)]
        t = Named()
        rows_room = sb("rows_room", [P, 3 * TILES * DM])
        t.x, t.y = (rows_room[:, k * TILES * DM:(k + 1) * TILES * DM].rearrange("p (n d) -> p n d", n=TILES)
                    for k in range(2))
        t.yT = rows_room[:, 2 * TILES * DM:3 * TILES * DM].rearrange("p (i t) -> p i t", i=CI)
        t.stat = sb("stat", [P, TILES, 6])
        t.mv = sb("mv", [P, TILES, 2])
        t.var = sb("var", [P, TILES])
        t.std = sb("std", [P, TILES])
        t.rstd = sb("rstd", [P, TILES])
        t.amax = sb("amax", [P, TILES])
        t.qs = sb("qs", [P, TILES])
        t.qr = sb("qr", [P, TILES])
        weights_room = sb("weights_room", [P, 9 * CI * DS + CI * EXPERTS + CI * 3 + 14])
        mw = Named()
        place = 0

        def weights(*shape):
            nonlocal place
            size = 1
            for n in shape:
                size *= n
            place += size
            flat = weights_room[:, place - size:place]
            if len(shape) == 1:
                return flat
            return flat.rearrange("p (i o) -> p i o", i=shape[0])

        mw.wide = {n: weights(CI, DS) for n in ("k", "v", "q", "af", "as", "ir")}
        mw.nm1, mw.nm2, mw.o, mw.router, mw.pw = (weights(2 * DS), weights(2, DS), weights(DM), weights(CI, EXPERTS),
                                                  weights(CI, 3))
        mw.cols = weights(12)
        mw.ir2, mw.norm = weights(1), weights(1)
        c = Named()
        c.ident = sb("ident", [P, P])
        c.ones = sb("ones", [P, P])
        c.batch_mask = sb("batch_mask", [P, BATCH])
        with ExitStack() as xa:
            def xb(name, shape, dt=F32):
                return xa.enter_context(nc.sbuf_tensor(name, shape, dt))
            c.head_mask = xb("head_mask", [P, 2])
            c.pair_mask = xb("pair_mask", [P, 2, 2, DH])
            c.split_scale = xb("split_scale", [P, 1])
            c.gather = xb("gather", [P, 3 * STEPS])
            c.w_hl = [xb(f"wkv{part}", [P, CI, 2 * DM], F16) for part in "hl"]
            c.v_room = xb("v1", [P, KROW * PAIRS * (V_COLS + 1)], F16)
            c.q_hl = [c.v_room[:, k * CI * TOK:(k + 1) * CI * TOK].rearrange("p (j t) -> p j t", j=CI) for k in range(2)]
            c.wqT = xb("wqT", [P, CI, DM])
            c.wpT = xb("wpT", [P, CI, DM])
            c.bq, c.bk = xb("bq", [P, CI]), xb("bk", [P, CI])
            c.bv, c.bp = xb("bv", [P, DM]), xb("bp", [P, DM])
            t.o = xb("o", [P, BATCH, PAIRS, 2 * DH])
            with ExitStack() as wa:
                t.wq = wa.enter_context(nc.sbuf_tensor("wq", [P, CI, DM], F32))
                t.wp = wa.enter_context(nc.sbuf_tensor("wp", [P, CI, DM], F32))
                t.wkvT = wa.enter_context(nc.sbuf_tensor("wkvT", [P, CI, 2 * DM], F32))
                t.qT = wa.enter_context(nc.sbuf_tensor("qT", [P, CI, TOK], F32))
                queries(nc, io, c, t, bank)
            attention(nc, io, c, t, rows_room, weights_room, bank)
            project_attention(nc, io, c, t, mw, bank)
        if upto == 3:
            store_rows(nc, t.x, io["out"])
            return
        with ExitStack() as me:
            def mb(name, shape):
                return me.enter_context(nc.sbuf_tensor(name, shape, F32))
            m = Named()
            m.v = mb("v", [P, TOK])
            m.nu = mb("nu", [P, TOK])
            m.sig = mb("sig", [P, TOK])
            m.pw2 = mb("pw2", [P, TOK])
            m.out = mb("out", [P, 2, TOK])
            with ExitStack() as sc:
                room = sc.enter_context(nc.sbuf_tensor("room", [P, 10 * TOK], F32))
                place = 0

                def carve(pattern, size, **dims):
                    nonlocal place
                    place += size
                    return room[:, place - size:place].rearrange(pattern, **dims)

                m.k, m.qh = carve("p (a t) -> p (a t)", TOK, a=1), carve("p (a t) -> p (a t)", TOK, a=1)
                m.oq, m.lb, m.lx, m.u = [carve("p (x t) -> p x t", 2 * TOK, x=2) for _ in range(4)]
                features(nc, io, c, t, m, mw, bank)

                def fb(name, shape):
                    return sc.enter_context(nc.sbuf_tensor(name, shape, F32))
                f = Named()
                f.cp = fb("cp", [P, 2, 2, len(PAIR_S), GROUPS])
                f.co = fb("co", [P, 2, len(PAIR_O), GROUPS])
                f.far = fb("far", [P, 2, 3, TOK])
                f.near = fb("near", [P, 2, 3, TOK // BLK, HALF])
                f.z = fb("z", [P, 2, NB, BATCH, BLK])
                f.zn = fb("zn", [P, 2, NB, BATCH, BLK])
                f.dec = fb("dec", [P, 2, TOK // BLK])
                factors(nc, c, m, f, bank)
                place = 0
                s = Named()
                s.cross = carve("p (k x i b t) -> p k x i b t", (NB - 1) * 2 * 3 * P, k=NB - 1, x=2, i=3, b=BATCH)
                s.wt = carve("p (k x v) -> p k x v", NB * 2 * P, k=NB, x=2)
                s.near = carve("p (u x i b t) -> p u x i b t", 2 * 2 * 3 * P // 2, u=2, x=2, i=3, b=BATCH)
                scan(nc, c, m, f, s, bank)
            memory_output(nc, io, c, t, m, mw, bank)
        if upto == 7:
            store_rows(nc, t.x, io["out"])
            return
        cw_rows = nc.dram_tensor("cw_rows", [CW_COPIES * EXPERTS, TOK], F32, kind="Internal").ap()
        f = Named()
        f.wgu = [sb(f"wgu{u}", [P, CI, 2, P]) for u in range(2)]
        f.wd = [sb(f"wd{u}", [P, DM]) for u in range(2)]
        f.x_hl = [ctx.enter_context(nc.sbuf_tensor(f"xT{part}", [P, CI, TOK], F16)) for part in "hl"]
        route(nc, io, c, t, mw, f, cw_rows, bank)
        experts(nc, io, t, f, cw_rows, bank)


def layout(inputs):
    import numpy as np
    a = {k: np.asarray(v) for k, v in inputs.items()}
    X, A, F = "L0_xattn_", "L0_attn_", "L0_ffn_"
    return {
        "x": a["x"],
        "ctxT": a["ctx_2048"].transpose(0, 2, 1),
        "wq": a[X + "wq"], "wp": a[X + "wp"],
        "wkvT": a[X + "wkv"].T,
        "bqT": a[X + "bq"].reshape(CI, P).T,
        "bkvT": a[X + "bkv"][:DM].reshape(CI, P).T,
        "bv": a[X + "bkv"][DM:], "bp": a[X + "bp"],
        "Wk": a[A + "Wk"], "Wv": a[A + "Wv"], "Wq": a[A + "Wq"], "Waf": a[A + "Waf"], "Was": a[A + "Was"],
        "Wir": a[A + "ir_w1"], "ir_w2": a[A + "ir_w2"], "ir_b2": a[A + "ir_b2"],
        "pw_w": a[A + "pw_w"], "pw_b": a[A + "pw_b"], "nm_w1": a[A + "nm_w1"], "nm_w2": a[A + "nm_w2"],
        "cols6": np.stack([a[A + "baf"], a[A + "bas"], a[A + "ir_b1"], *a[A + "nm_b1"].reshape(2, P), a[A + "nm_b2"]], 1),
        "lam": np.stack([a[A + "fast_lambda"], a[A + "slow_lambda"]], 1),
        "Wo": a[A + "Wo"], "norm_w": a[A + "norm_w"].reshape(P, 1),
        "routerT": a[F + "router_w"].T,
        "guT": np.stack([a[F + n].reshape(SLABS, P, CI, P).transpose(0, 3, 2, 1) for n in ("gate_w", "up_w")], 3),
        "downT": a[F + "down_w"].transpose(0, 2, 1).reshape(SLABS, P, DM),
    }


def kernel(**inputs):
    import numpy as np
    import concourse.bacc as bacc
    from concourse.bass_utils import run_bass_kernel_spmd

    nc = bacc.Bacc("TRN2", target_bir_lowering=False, num_devices=1)
    arrays, io = {}, {}
    for name, a in layout(inputs).items():
        a = np.ascontiguousarray(a)
        arrays[f"in_{name}_dram"] = a
        io[name] = nc.dram_tensor(f"in_{name}_dram", a.shape, mybir.dt.from_np(a.dtype), kind="ExternalInput").ap()
    io["out"] = nc.dram_tensor("out_0_dram", (BATCH, STEPS, DM), F32, kind="ExternalOutput").ap()
    perceiver_layer(nc, io)
    r = run_bass_kernel_spmd(nc, [arrays], core_ids=[0])
    return r.results[0]["out_0_dram"]
```
